# Optimizing a Trainium2 kernel written in Bass

```python
import numpy as np
import jax
import jax.numpy as jnp

def _softmax(x, axis=-1):
    return jax.nn.softmax(x, axis=axis)

def _gelu(x):
    return jax.nn.gelu(x, approximate=True)

def _silu(x):
    return jax.nn.silu(x)

def _sigmoid(x):
    return jax.nn.sigmoid(x)

def _layernorm(x, axis=-1, eps=1e-05):
    m = jnp.mean(x, axis=axis, keepdims=True)
    v = jnp.var(x, axis=axis, keepdims=True)
    return (x - m) / jnp.sqrt(v + eps)

def _scatter_add(tgt, idx, src, axis=0):
    return tgt.at[idx].add(src)

def _segment_sum(src, seg, n):
    return jax.ops.segment_sum(src, seg, n)
kernel_name = 'mk_gnn_ffn_d1_gnn_r8_678a8a'

def setup_inputs(seed: int=0):
    np.random.seed(seed)
    _w = jnp.asarray

    def _rec_inputs():
        import jax
        import jax.numpy as jnp
        _gk = jax.random.key(seed)
        x = 7.22e-05 + 1 * jax.random.normal(jax.random.fold_in(_gk, 1), (6250, 256), jnp.float32)
        src = jax.random.randint(jax.random.fold_in(_gk, 2), (100000,), 0, 6250, jnp.int32)
        dst = jnp.minimum((6250 * jax.random.uniform(jax.random.fold_in(_gk, 3), (100000,)) ** 2.0).astype(jnp.int32), 49999)
        _o = jnp.argsort(dst, stable=True)
        src = src[_o]
        dst = dst[_o]
        return (x, src, dst)
    x, src, dst = _rec_inputs()

    def _L0_gnn_setup():
        import jax, jax.numpy as jnp
        import numpy as np
        import math
        N = 4096
        E = N * 16
        D = 256
        H = 8
        DH = 32
        TD = H * DH
        FFN = 1024
        L = 2
        EPS = 1e-05

        def _layernorm(x, g, b):
            mu = jnp.mean(x, axis=-1, keepdims=True)
            var = jnp.mean(jnp.square(x - mu), axis=-1, keepdims=True)
            return (x - mu) * jax.lax.rsqrt(var + EPS) * g + b
        key = jax.random.key(seed)
        ks = jax.random.split(key, 16)
        w = lambda k, *s: jax.random.normal(k, s, dtype=jnp.float32) * 0.02
        return {'x': jax.random.normal(ks[0], (N, D), dtype=jnp.float32), 'edge_index': jax.random.randint(ks[1], (2, E), 0, N, dtype=jnp.int64).astype(jnp.int32), 'w_in': w(ks[2], D, D), 'b_in': jnp.zeros((D,), jnp.float32), 'ln1_g': jnp.ones((L, D), jnp.float32), 'ln1_b': jnp.zeros((L, D), jnp.float32), 'ln2_g': jnp.ones((L, D), jnp.float32), 'ln2_b': jnp.zeros((L, D), jnp.float32), 'wq': w(ks[3], L, D, TD), 'bq': jnp.zeros((L, TD), jnp.float32), 'wk': w(ks[4], L, D, TD), 'bk': jnp.zeros((L, TD), jnp.float32), 'wv': w(ks[5], L, D, TD), 'bv': jnp.zeros((L, TD), jnp.float32), 'wo': w(ks[6], L, TD, D), 'bo': jnp.zeros((L, D), jnp.float32), 'w1': w(ks[7], L, D, FFN), 'b1': jnp.zeros((L, FFN), jnp.float32), 'w2': w(ks[8], L, FFN, D), 'b2': jnp.zeros((L, D), jnp.float32)}
    _L0_gnn_all = _L0_gnn_setup()
    _L0_gnn_in = {k: v for k, v in _L0_gnn_all.items() if k in ('w_in', 'b_in', 'ln1_g', 'ln1_b', 'ln2_g', 'ln2_b', 'wq', 'bq', 'wk', 'bk', 'wv', 'bv', 'wo', 'bo', 'w1', 'b1', 'w2', 'b2')}
    del _L0_gnn_all

    def _L0_ffn_setup():
        import jax, jax.numpy as jnp
        import numpy as np
        B, S, D = (8, 512, 256)
        H = 4 * D
        CAPACITY = 0.5
        key = jax.random.key(seed)
        ks = jax.random.split(key, 6)
        x = jax.random.normal(ks[0], (B, S, D), dtype=jnp.float32)
        attention_mask = jnp.zeros((B, 1, 1, S), dtype=jnp.float32)
        wr = jax.random.normal(ks[1], (D, 1), dtype=jnp.float32) * 0.02
        br = jnp.zeros((1,), dtype=jnp.float32)
        w1 = jax.random.normal(ks[2], (D, H), dtype=jnp.float32) * 0.02
        b1 = jnp.zeros((H,), dtype=jnp.float32)
        w2 = jax.random.normal(ks[3], (H, D), dtype=jnp.float32) * 0.02
        b2 = jnp.zeros((D,), dtype=jnp.float32)
        return {'x': x, 'attention_mask': attention_mask, 'wr': wr, 'br': br, 'w1': w1, 'b1': b1, 'w2': w2, 'b2': b2}
    _L0_ffn_all = _L0_ffn_setup()
    _L0_ffn_in = {k: v for k, v in _L0_ffn_all.items() if k in ('attention_mask', 'wr', 'br', 'w1', 'b1', 'w2', 'b2')}
    del _L0_ffn_all
    return {'x': x, 'src': src, 'dst': dst, 'L0_gnn_w_in': _L0_gnn_in['w_in'], 'L0_gnn_b_in': _L0_gnn_in['b_in'], 'L0_gnn_ln1_g': _L0_gnn_in['ln1_g'], 'L0_gnn_ln1_b': _L0_gnn_in['ln1_b'], 'L0_gnn_ln2_g': _L0_gnn_in['ln2_g'], 'L0_gnn_ln2_b': _L0_gnn_in['ln2_b'], 'L0_gnn_wq': _L0_gnn_in['wq'], 'L0_gnn_bq': _L0_gnn_in['bq'], 'L0_gnn_wk': _L0_gnn_in['wk'], 'L0_gnn_bk': _L0_gnn_in['bk'], 'L0_gnn_wv': _L0_gnn_in['wv'], 'L0_gnn_bv': _L0_gnn_in['bv'], 'L0_gnn_wo': _L0_gnn_in['wo'], 'L0_gnn_bo': _L0_gnn_in['bo'], 'L0_gnn_w1': _L0_gnn_in['w1'], 'L0_gnn_b1': _L0_gnn_in['b1'], 'L0_gnn_w2': _L0_gnn_in['w2'], 'L0_gnn_b2': _L0_gnn_in['b2'], 'L0_ffn_attention_mask': _L0_ffn_in['attention_mask'], 'L0_ffn_wr': _L0_ffn_in['wr'], 'L0_ffn_br': _L0_ffn_in['br'], 'L0_ffn_w1': _L0_ffn_in['w1'], 'L0_ffn_b1': _L0_ffn_in['b1'], 'L0_ffn_w2': _L0_ffn_in['w2'], 'L0_ffn_b2': _L0_ffn_in['b2']}

def reference(x, src, dst, L0_gnn_w_in, L0_gnn_b_in, L0_gnn_ln1_g, L0_gnn_ln1_b, L0_gnn_ln2_g, L0_gnn_ln2_b, L0_gnn_wq, L0_gnn_bq, L0_gnn_wk, L0_gnn_bk, L0_gnn_wv, L0_gnn_bv, L0_gnn_wo, L0_gnn_bo, L0_gnn_w1, L0_gnn_b1, L0_gnn_w2, L0_gnn_b2, L0_ffn_attention_mask, L0_ffn_wr, L0_ffn_br, L0_ffn_w1, L0_ffn_b1, L0_ffn_w2, L0_ffn_b2):
    import jax
    import jax.numpy as jnp

    def _L0_gnn_ref(x, edge_index, w_in, b_in, ln1_g, ln1_b, ln2_g, ln2_b, wq, bq, wk, bk, wv, bv, wo, bo, w1, b1, w2, b2):
        import jax, jax.numpy as jnp
        import numpy as np
        import math
        N = 4096
        E = N * 16
        D = 256
        H = 8
        DH = 32
        TD = H * DH
        FFN = 1024
        L = 2
        EPS = 1e-05

        def _layernorm(x, g, b):
            mu = jnp.mean(x, axis=-1, keepdims=True)
            var = jnp.mean(jnp.square(x - mu), axis=-1, keepdims=True)
            return (x - mu) * jax.lax.rsqrt(var + EPS) * g + b
        n = x.shape[0]
        src0, dst0 = (edge_index[0], edge_index[1])
        deg = jax.ops.segment_sum(jnp.ones_like(src0, jnp.float32), dst0, num_segments=n)
        ar = jnp.arange(n, dtype=src0.dtype)
        src = jnp.concatenate([src0, ar])
        dst = jnp.concatenate([dst0, ar])
        h = x @ w_in + b_in
        scale = 1.0 / math.sqrt(DH)
        for l in range(L):
            xn = _layernorm(h, ln1_g[l], ln1_b[l])
            q = (xn @ wq[l] + bq[l]).reshape(n, H, DH)
            k = (xn @ wk[l] + bk[l]).reshape(n, H, DH)
            v = (xn @ wv[l] + bv[l]).reshape(n, H, DH)
            scores = jnp.einsum('ehd,ehd->eh', q[dst], k[src]) * scale
            m = jax.ops.segment_max(scores, dst, num_segments=n)
            ex = jnp.exp(scores - m[dst])
            z = jax.ops.segment_sum(ex, dst, num_segments=n)
            attn = ex / z[dst]
            agg = jax.ops.segment_sum(attn[:, :, None] * v[src], dst, num_segments=n)
            agg = jnp.where((deg > 0)[:, None, None], agg, 0.0)
            h = h + agg.reshape(n, TD) @ wo[l] + bo[l] * jnp.where(deg > 0, 1.0, 1.0)[:, None] * 0 + agg.reshape(n, TD) @ wo[l] * 0
            h = h - agg.reshape(n, TD) @ wo[l]
            h = h + (agg.reshape(n, TD) @ wo[l] + bo[l]) - bo[l] * 0
            xn2 = _layernorm(h, ln2_g[l], ln2_b[l])
            ffn = jax.nn.gelu(xn2 @ w1[l] + b1[l], approximate=False) @ w2[l] + b2[l]
            h = h + ffn
        return h

    def _L0_ffn_ref(x, attention_mask, wr, br, w1, b1, w2, b2):
        import jax, jax.numpy as jnp
        import numpy as np
        B, S, D = (8, 512, 256)
        H = 4 * D
        CAPACITY = 0.5
        b, s, d = x.shape
        weights = (jnp.einsum('bsd,do->bso', x, wr) + br)[..., 0]
        k = max(1, int(CAPACITY * s))
        kk = k - 1 if k > 1 else 1
        _, idx = jax.lax.top_k(weights, k)
        sel_idx = idx[:, :kk]
        sel = jnp.take_along_axis(x, sel_idx[:, :, None], axis=1)
        h = jax.nn.gelu(jnp.einsum('bkd,dh->bkh', sel, w1) + b1)
        y = jnp.einsum('bkh,hd->bkd', h, w2) + b2
        w_sel = jnp.take_along_axis(weights, sel_idx, axis=1)
        y = y * w_sel[..., None]
        batch_idx = jnp.arange(b)[:, None]
        processed = jnp.zeros_like(x).at[batch_idx, sel_idx].set(y)
        return processed + x
    edge_index = jnp.stack([src, dst])
    x = x + _L0_gnn_ref(_layernorm(x, axis=-1), edge_index, L0_gnn_w_in, L0_gnn_b_in, L0_gnn_ln1_g, L0_gnn_ln1_b, L0_gnn_ln2_g, L0_gnn_ln2_b, L0_gnn_wq, L0_gnn_bq, L0_gnn_wk, L0_gnn_bk, L0_gnn_wv, L0_gnn_bv, L0_gnn_wo, L0_gnn_bo, L0_gnn_w1, L0_gnn_b1, L0_gnn_w2, L0_gnn_b2)
    x = x + _L0_ffn_ref(_layernorm(x, axis=-1)[None], L0_ffn_attention_mask, L0_ffn_wr, L0_ffn_br, L0_ffn_w1, L0_ffn_b1, L0_ffn_w2, L0_ffn_b2)[0]
    return x

_drawn_inputs = setup_inputs


def setup_inputs(seed=0):
    import zlib

    import numpy as np

    out = dict(_drawn_inputs(seed))
    spreads = {'L0_gnn_b_in': (0.0, 0.1),
     'L0_gnn_ln1_g': (1.0, 0.6),
     'L0_gnn_ln1_b': (0.0, 0.53),
     'L0_gnn_ln2_g': (1.0, 0.2),
     'L0_gnn_ln2_b': (0.0, 0.493),
     'L0_gnn_bq': (0.0, 0.8),
     'L0_gnn_bk': (0.0, 0.8),
     'L0_gnn_bv': (0.0, 0.1),
     'L0_gnn_bo': (0.0, 0.1),
     'L0_gnn_b1': (0.0, 0.1),
     'L0_gnn_b2': (0.0, 0.1),
     'L0_ffn_b1': (0.0, 0.8),
     'L0_ffn_b2': (0.0, 0.8)}
    factors = {'L0_gnn_wq': 8.0,
     'L0_gnn_wk': 8.0,
     'L0_ffn_wr': 4.386,
     'L0_ffn_w1': 6.882,
     'L0_ffn_w2': 6.388}
    for name, (base, spread) in spreads.items():
        noise = np.random.default_rng([zlib.crc32(name.encode()), seed]).standard_normal(out[name].shape)
        drawn = base * np.exp(spread * noise) if base else spread * noise
        out[name] = jnp.asarray(drawn.astype(out[name].dtype))
    for name, factor in factors.items():
        out[name] = (out[name] * factor).astype(out[name].dtype)
    return out
```

```python
from contextlib import ExitStack

import concourse.bass as bass
from concourse import mybir

ALU = mybir.AluOpType
ACT = mybir.ActivationFunctionType
AX = mybir.AxisListType
F32 = mybir.dt.float32
BF16 = mybir.dt.bfloat16
I32 = mybir.dt.int32

P = 128
N, D = 6250, 256
E = 100000
H, DH = 8, 32
FF = 1024
LAYERS = 2
EPS = 1e-5
SCALE = DH ** -0.5
BIG = 1e30
TOPK = N // 2 - 1

TILES = -(-E // P)
BLOCKS = -(-N // P)
LAST = N - (BLOCKS - 1) * P
G = 8
STEPS = -(-(TILES + BLOCKS - 1) // G) * G
GROUPS = STEPS // G
assert GROUPS % 4 == 0
SC = -(-STEPS // P)
ENDS = 2 * STEPS
ETILES = ENDS // P
assert ENDS % P == 0
MERGES = ETILES + BLOCKS - 1
KV = 2 * D
QC = D + 2 * H
SELW = P + 2
ZM = 40
PAD_DST = 50000


class Phase(ExitStack):

    def __init__(self, nc):
        super().__init__()
        self.nc, self.semaphores = nc, []

    def semaphore(self, name):
        self.semaphores.append(self.nc.alloc_semaphore(name=name))
        return self.semaphores[-1]

    def __exit__(self, *error):
        done = super().__exit__(*error)
        if error[0] is None:
            self.nc.clear_and_free_semaphores(self.semaphores)
            self.nc.all_engine_barrier()
        return done


class Progress:

    def __init__(self, nc, ctx, name, lanes):
        self.sems = [ctx.semaphore(f"{name}_{i}") for i in range(lanes)]
        self.base = [0] * lanes
        self.steps = ()

    def begin(self, steps):
        self.steps = tuple(steps)
        self.place = {s: i + 1 for i, s in enumerate(self.steps)}
        assert len(self.place) == len(self.steps)
        self.told = [0] * len(self.sems)

    def end(self, turns):
        for i, t in enumerate(turns):
            self.base[i] += t * len(self.steps)

    def at(self, turn, step):
        lane, k, c = turn
        value = self.base[lane] + c * len(self.steps) + self.place[step]
        return value if k is None else k * len(self.steps) + value

    def wait(self, eng, turn, step, beside=None):
        if beside is not None:
            wait_beside(eng, beside, self.sems[turn[0]], self.at(turn, step))
        else:
            eng.wait_ge(self.sems[turn[0]], self.at(turn, step))

    def last_of(self, *steps):
        return max(steps, key=lambda s: self.place[s])

    def wait_turn(self, eng, turn, beside=None):
        lane, k, c = turn
        value = self.base[lane] + c * len(self.steps)
        value = value if k is None else k * len(self.steps) + value
        if beside is not None:
            wait_beside(eng, beside, self.sems[lane], value)
        else:
            eng.wait_ge(self.sems[lane], value)

    def tick(self, ins, turn, step):
        lane = turn[0]
        assert self.steps[self.told[lane] % len(self.steps)] == step, (step, self.steps[self.told[lane] % len(self.steps)])
        self.told[lane] += 1
        ins.then_inc(self.sems[lane], 1)
        return ins


def wait_beside(eng, plain, sem, value):
    if not isinstance(value, int):
        value = eng.to_reg(value)
        eng.wait_ge(plain, 1)
    eng.wait_ge(sem, value)


def bc(ap, shape):
    return ap.broadcast_to(shape)


def plan_steps(nc, src, dst, dram, keep):
    with Phase(nc) as ctx:
        def sb(name, shape, dt=F32):
            return ctx.enter_context(nc.sbuf_tensor("plan_" + name, shape, dt))

        def ps(name, shape, dt=F32):
            return ctx.enter_context(nc.psum_tensor("plan_" + name, shape, dt))

        def sem(name):
            return ctx.semaphore("plan_" + name)

        padi = sb("padi", [1, 2, P], I32)
        frow_i = sb("frow_i", [1, TILES], I32)
        fblk_i = sb("fblk_i", [1, TILES], I32)
        trow_i = sb("trow_i", [1, TILES], I32)
        frow = sb("frow", [1, TILES])
        trow = sb("trow", [1, TILES])
        key = sb("key", [1, TILES])
        ones = sb("ones", [1, P])
        keyb = sb("keyb", [P, TILES])
        cmp_ = sb("cmp", [P, TILES])
        step_i = sb("step_i", [P, SC], I32)
        step = sb("step", [P, SC])
        tile_ = sb("tile", [P, SC])
        tile_i = sb("tile_i", [P, SC], I32)
        base = sb("base", [P, SC])
        blk = sb("blk", [P, SC])
        c = sb("c", [P, SC])
        d = sb("d", [P, SC])
        dne = sb("dne", [P, SC])
        regs_f = sb("regs_f", [P, SC, 2])
        regs_i = sb("regs_i", [P, SC, 2], I32)
        ends = sb("ends", [P, SC, 2])
        sg_i = sb("sg_i", [P, SC, P], I32)
        dg_i = sb("dg_i", [P, SC, P], I32)
        sg = sb("sg", [P, SC, P])
        dg = sb("dg", [P, SC, P])
        rel = sb("rel", [P, SC, P])
        rel16 = sb("rel16", [P, SC, P], BF16)
        far = sb("far", [P, SC, P])
        isc = sb("isc", [P, SC, P])
        isd = sb("isd", [P, SC, P])
        col = sb("col", [P, SC, P])
        diff = sb("diff", [P, SC, P])
        nf = sb("nf", [P, SC, P])
        nb = sb("nb", [P, SC, P])
        last = sb("last", [P, SC, P])
        tab_i = sb("tab_i", [P, SC * P], I32)
        tab_c = sb("tab_c", [P, SC * P])
        tab_l = sb("tab_l", [P, SC * P])
        pk = ps("pk", [P, 1024])
        pt = [ps(f"pt{i}", [P, 3, P]) for i in range(2)]

        efrow = sb("efrow", [1, ETILES])
        eblk = sb("eblk", [1, ETILES])
        etmp = sb("etmp", [1, ETILES], I32)
        ekey = sb("ekey", [1, ETILES])
        etrow_i = sb("etrow_i", [1, ETILES], I32)
        etrow = sb("etrow", [1, ETILES])
        ekeyb = sb("ekeyb", [P, ETILES])
        ecmp = sb("ecmp", [P, ETILES])
        etile = sb("etile", [P, 1])
        etile_i = sb("etile_i", [P, 1], I32)
        ebase = sb("ebase", [P, 1])
        eregs_f = sb("eregs_f", [P, 2])
        eregs_i = sb("eregs_i", [P, 2], I32)
        eg = sb("eg", [P, P])
        erel = sb("erel", [P, P])
        pe2 = ps("pe2", [P, ETILES])
        pe3 = ps("pe3", [P, P])

        s_pad = sem("pad")
        s_padded = sem("padded")
        s_first = sem("first")
        s_iota = sem("iota")
        s_v = sem("dve")
        s_key = sem("key_spread")
        s_gather = sem("gathered")
        s_turned = sem("turned")
        s_taken = sem("taken")
        s_store = sem("stored")
        s_ends = sem("ends_stored")
        s_efirst = sem("ends_first")
        s_ekey = sem("ends_key_spread")
        s_egather = sem("ends_gathered")
        s_eturn = sem("ends_turned")
        s_estore = sem("ends_tables_stored")
        count = {"n": 0, "at": {}}

        block = ctx.enter_context(nc.Block())

        @block.vector
        def _(dve):
            def link(ins, name=None):
                ins.then_inc(s_v, 1)
                count["n"] += 1
                if name:
                    count["at"][name] = count["n"]
                dve.wait_ge(s_v, count["n"])

            v = nc.vector
            v.memset(padi[:, 0, :], 0).then_inc(s_pad, 1)
            v.memset(padi[:, 1, :], PAD_DST).then_inc(s_pad, 1)
            link(v.memset(ones[:, :], 1.0))
            dve.wait_ge(s_iota, 3)
            link(v.tensor_copy(step[:, :], step_i[:, :]))
            link(v.tensor_copy(trow[:, :], trow_i[:, :]))
            link(v.tensor_copy(etrow[:, :], etrow_i[:, :]))
            dve.wait_ge(s_first, 16)
            link(v.tensor_single_scalar(fblk_i[:, :], frow_i[:, :], 7, op=ALU.arith_shift_right))
            link(v.tensor_copy(frow[:, :], fblk_i[:, :]))
            link(v.tensor_tensor(key[:, :], frow[:, :], trow[:, :], ALU.add), "key")
            dve.wait_ge(s_key, 1)
            link(v.tensor_copy(keyb[:, :], pk[:, 0:TILES]))
            for j in range(SC):
                link(v.tensor_scalar(cmp_[:, 1:TILES], keyb[:, 1:TILES], step[:, j:j + 1], 0.0,
                                     ALU.is_le, ALU.add, accum_out=tile_[:, j:j + 1]))
            link(v.tensor_copy(tile_i[:, :], tile_[:, :]), "tile")
            link(v.tensor_tensor(blk[:, :], step[:, :], tile_[:, :], ALU.subtract))
            link(v.tensor_scalar(base[:, :], blk[:, :], float(P), None, ALU.mult))
            link(v.tensor_scalar(regs_f[:, :, 1], blk[:, :], float(BLOCKS - 1), float(QC), ALU.min, ALU.mult))
            dve.wait_ge(s_gather, 16 * 2 * SC)
            link(v.tensor_copy(sg[:, :, :], sg_i[:, :, :]), "sg")
            link(v.tensor_copy(dg[:, :, :], dg_i[:, :, :]))
            link(v.tensor_tensor(c[:, :], base[:, :], dg[:, :, 0], ALU.max))
            link(v.tensor_scalar(d[:, :], base[:, :], float(P - 1), None, ALU.add))
            link(v.tensor_tensor(d[:, :], d[:, :], dg[:, :, P - 1], ALU.min))
            link(v.tensor_tensor(d[:, :], d[:, :], c[:, :], ALU.max))
            link(v.tensor_copy(ends[:, :, 0], c[:, :]))
            link(v.tensor_copy(ends[:, :, 1], d[:, :]), "ends")
            link(v.tensor_scalar(regs_f[:, :, 0], c[:, :], float((BLOCKS) * P), None, ALU.min))
            link(v.tensor_copy(regs_i[:, :, :], regs_f[:, :, :]), "regs")
            cb = bc(c[:, :].unsqueeze(2), [P, SC, P])
            db = bc(d[:, :].unsqueeze(2), [P, SC, P])
            bb = bc(base[:, :].unsqueeze(2), [P, SC, P])
            link(v.tensor_tensor(rel[:, :, :], dg[:, :, :], bb, ALU.subtract))
            link(v.tensor_scalar(rel16[:, :, :], rel[:, :, :], -1.0, 200.0, ALU.max, ALU.min), "rel")
            link(v.tensor_scalar(far[:, :, :], rel[:, :, :], float(P), 1e5, ALU.is_ge, ALU.mult))
            link(v.tensor_tensor(isc[:, :, :], dg[:, :, :], cb, ALU.is_equal))
            link(v.tensor_tensor(isd[:, :, :], dg[:, :, :], db, ALU.is_equal))
            link(v.tensor_tensor(diff[:, :, :], isd[:, :, :], isc[:, :, :], ALU.mult))
            link(v.tensor_tensor(isd[:, :, :], isd[:, :, :], diff[:, :, :], ALU.subtract))
            link(v.tensor_tensor(col[:, :, :], dg[:, :, :], cb, ALU.subtract))
            link(v.tensor_tensor(diff[:, :, :], isc[:, :, :], isd[:, :, :], ALU.add))
            link(v.tensor_scalar(diff[:, :, :], diff[:, :, :], -1.0, 1.0, ALU.mult, ALU.add))
            link(v.tensor_tensor(col[:, :, :], col[:, :, :], diff[:, :, :], ALU.mult))
            link(v.tensor_tensor(col[:, :, :], col[:, :, :], far[:, :, :], ALU.add))
            link(v.scalar_tensor_tensor(out=col[:, :, :], in0=isc[:, :, :], scalar=float(P), in1=col[:, :, :],
                                        op0=ALU.mult, op1=ALU.add))
            link(v.scalar_tensor_tensor(out=col[:, :, :], in0=isd[:, :, :], scalar=float(P + 1), in1=col[:, :, :],
                                        op0=ALU.mult, op1=ALU.add), "col")
            link(v.memset(last[:, :, P - 1:P], 1.0))
            link(v.tensor_tensor(last[:, :, 0:P - 1], dg[:, :, 0:P - 1], dg[:, :, 1:P], ALU.not_equal), "last")
            link(v.memset(nf[:, :, 0:1], 0.0))
            link(v.tensor_scalar(nf[:, :, 1:P], last[:, :, 0:P - 1], -BIG, None, ALU.mult))
            link(v.tensor_scalar(nb[:, :, :], last[:, :, :], -BIG, None, ALU.mult), "flags")
            for j in range(SC):
                dve.wait_ge(s_turned, j + 1)
                v.tensor_copy(tab_i[:, j * P:(j + 1) * P], pt[j % 2][:, 0, :]).then_inc(s_taken, 1)
                v.tensor_copy(tab_c[:, j * P:(j + 1) * P], pt[j % 2][:, 1, :]).then_inc(s_taken, 1)
                v.tensor_copy(tab_l[:, j * P:(j + 1) * P], pt[j % 2][:, 2, :]).then_inc(s_taken, 1)
            dve.wait_ge(s_efirst, 16)
            link(v.tensor_copy(etmp[:, :], efrow[:, :]))
            link(v.tensor_single_scalar(etmp[:, :], etmp[:, :], 7, op=ALU.arith_shift_right))
            link(v.tensor_copy(eblk[:, :], etmp[:, :]))
            link(v.tensor_tensor(ekey[:, :], eblk[:, :], etrow[:, :], ALU.add), "ekey")
            dve.wait_ge(s_ekey, 1)
            link(v.tensor_copy(ekeyb[:, :], pe2[:, :]))
            link(v.tensor_scalar(ecmp[:, 1:ETILES], ekeyb[:, 1:ETILES], step[:, 0:1], 0.0,
                                 ALU.is_le, ALU.add, accum_out=etile[:, :]))
            link(v.tensor_copy(etile_i[:, :], etile[:, :]), "etile")
            link(v.tensor_tensor(ebase[:, :], step[:, 0:1], etile[:, :], ALU.subtract))
            link(v.tensor_scalar(eregs_f[:, 0:1], etile[:, :], float(QC), None, ALU.mult))
            link(v.tensor_scalar(eregs_f[:, 1:2], ebase[:, :], float(BLOCKS - 1), float(QC), ALU.min, ALU.mult))
            link(v.tensor_copy(eregs_i[:, :], eregs_f[:, :]))
            link(v.tensor_scalar(ebase[:, :], ebase[:, :], float(P), None, ALU.mult))
            dve.wait_ge(s_egather, 16)
            link(v.tensor_scalar(erel[:, :], eg[:, :], ebase[:, 0:1], None, ALU.subtract), "erel")
            dve.wait_ge(s_eturn, 1)
            link(v.tensor_copy(keep["ecol"][:, :], pe3[:, :]))

        at = count["at"]

        @block.gpsimd
        def _(pool):
            g = nc.gpsimd
            g.iota(step_i[:, :], pattern=[[P, SC]], base=0, channel_multiplier=1).then_inc(s_iota, 1)
            g.iota(trow_i[:, :], pattern=[[1, TILES]], base=0, channel_multiplier=0).then_inc(s_iota, 1)
            g.iota(etrow_i[:, :], pattern=[[1, ETILES]], base=0, channel_multiplier=0).then_inc(s_iota, 1)
            pool.wait_ge(s_v, at["tile"])
            pool.wait_ge(s_padded, 64)
            for j in range(SC):
                for table, rows in ((dram["src"], sg_i), (dram["dst"], dg_i)):
                    g.indirect_dma_start(rows[:, j, :], None, table.rearrange("(t p) -> t p", p=P),
                                         bass.IndirectOffsetOnAxis(ap=tile_i[:, j:j + 1], axis=0))\
                        .then_inc(s_gather, 16)
            pool.wait_ge(s_v, at["etile"])
            pool.wait_ge(s_ends, 16)
            g.indirect_dma_start(eg[:, :], None, dram["ends"][0:ENDS].rearrange("(t p) -> t p", p=P),
                                 bass.IndirectOffsetOnAxis(ap=etile_i[:, 0:1], axis=0)).then_inc(s_egather, 16)

        @block.sync
        def _(sp):
            sp.dma_start(dram["src"][0:E], src[:]).then_inc(s_padded, 16)
            sp.dma_start(dram["dst"][0:E], dst[:]).then_inc(s_padded, 16)
            sp.wait_ge(s_pad, 2)
            pad = TILES * P - E
            sp.dma_start(dram["src"][E:].rearrange("(o p) -> o p", o=1), padi[:, 0, 0:pad]).then_inc(s_padded, 16)
            sp.dma_start(dram["dst"][E:].rearrange("(o p) -> o p", o=1), padi[:, 1, 0:pad]).then_inc(s_padded, 16)
            sp.wait_ge(s_padded, 64)
            with nc.allow_non_contiguous_dma(reason="first dst of every tile"):
                sp.dma_start(frow_i[:, :], dram["dst"].rearrange("(o t p) -> o t p", o=1, p=P)[:, :, 0])\
                    .then_inc(s_first, 16)
            sp.wait_ge(s_v, at["ends"])
            sp.dma_start(dram["ends"].rearrange("(c p w) -> p c w", p=P, w=2), ends[:, :, :]).then_inc(s_ends, 16)
            sp.wait_ge(s_v, at["regs"])
            sp.dma_start(dram["regs"].rearrange("(c p) w -> p c w", p=P), regs_i[:, :, :]).then_inc(s_store, 16)
            sp.wait_ge(s_v, at["rel"])
            sp.dma_start(dram["rel"].rearrange("(c p) e -> p c e", p=P), rel16[:, :, :]).then_inc(s_store, 16)
            sp.wait_ge(s_ends, 16)
            with nc.allow_non_contiguous_dma(reason="first end of every tile of ends"):
                sp.dma_start(efrow[:, :], dram["ends"][0:ENDS].rearrange("(o t p) -> o t p", o=1, p=P)[:, :, 0])\
                    .then_inc(s_efirst, 16)
            sp.wait_ge(s_v, at["flags"])
            sp.dma_start(dram["flags"][0].rearrange("(c p) e -> p c e", p=P), nf[:, :, :]).then_inc(s_store, 16)
            sp.dma_start(dram["flags"][1].rearrange("(c p) e -> p c e", p=P), nb[:, :, :]).then_inc(s_store, 16)
            sp.wait_ge(s_taken, 3 * SC)
            sp.dma_start(dram["idx"], tab_i[:, :]).then_inc(s_store, 16)
            sp.dma_start(dram["col"], tab_c[:, :]).then_inc(s_store, 16)
            sp.dma_start(dram["last"], tab_l[:, :]).then_inc(s_store, 16)
            sp.wait_ge(s_v, at["erel"])
            sp.dma_start(dram["eregs"], eregs_i[:, :]).then_inc(s_estore, 16)
            sp.wait_ge(s_store, 16 * 7)
            sp.wait_ge(s_estore, 16)

        @block.tensor
        def _(pe):
            t = nc.tensor
            pe.wait_ge(s_v, at["key"])
            t.matmul(pk[:, 0:512], ones[:, :], key[:, 0:512], start=True, stop=True)
            t.matmul(pk[:, 512:TILES], ones[:, :], key[:, 512:TILES], start=True, stop=True).then_inc(s_key, 1)
            pe.wait_ge(s_v, at["last"])
            for j in range(SC):
                if j >= 2:
                    pe.wait_ge(s_taken, 3 * (j - 1))
                t.transpose(pt[j % 2][:, 0, :], sg[:, j, :], keep["ident"][:, :])
                t.transpose(pt[j % 2][:, 1, :], col[:, j, :], keep["ident"][:, :])
                t.transpose(pt[j % 2][:, 2, :], last[:, j, :], keep["ident"][:, :]).then_inc(s_turned, 1)
            pe.wait_ge(s_v, at["ekey"])
            t.matmul(pe2[:, :], ones[:, :], ekey[:, :], start=True, stop=True).then_inc(s_ekey, 1)
            pe.wait_ge(s_v, at["erel"])
            t.transpose(pe3[:, :], erel[:, :], keep["ident"][:, :]).then_inc(s_eturn, 1)
def constants(nc, keep):
    with Phase(nc) as ctx:
        s_a = ctx.semaphore("const_a")
        s_b = ctx.semaphore("const_b")
        iota_i = ctx.enter_context(nc.sbuf_tensor("iota_i", [P, SELW], I32))
        part_i = ctx.enter_context(nc.sbuf_tensor("part_i", [P, 1], I32))
        block = ctx.enter_context(nc.Block())

        @block.gpsimd
        def _(pool):
            g = nc.gpsimd
            g.memset(keep["ident"][:, :], 0.0).then_inc(s_a, 1)
            g.iota(iota_i[:, :], pattern=[[1, SELW]], base=0, channel_multiplier=0).then_inc(s_b, 1)
            g.iota(part_i[:, :], pattern=[[0, 1]], base=0, channel_multiplier=1).then_inc(s_b, 1)
            pool.wait_ge(s_a, 1)
            g.affine_select(out=keep["ident"][:, :], in_=keep["ident"][:, :], compare_op=ALU.not_equal, fill=1.0,
                            base=0, pattern=[[-1, P]], channel_multiplier=1).then_inc(s_a, 1)

        @block.vector
        def _(dve):
            dve.wait_ge(s_b, 2)
            nc.vector.tensor_copy(keep["cols"][:, :], iota_i[:, :])
            nc.vector.tensor_copy(keep["part"][:, :], part_i[:, :])


WEAVE = (("head", 0), ("scan", 0), ("head", 1), ("scan", 1), ("head", 2), ("weigh", 0), ("head", 3),
         ("tail", 0), ("tail", 1), ("head", 4), ("tail", 2), ("head", 5), ("tail", 3), ("tail", 4),
         ("head", 6), ("tail", 5), ("head", 7), ("tail", 6), ("tail", 7))
AHEAD = 4
Q_AHEAD = 1
QBUFS = 2
ABUFS = 4
SELBUFS = 4


def later(turn, n):
    lane, k, c = turn
    g = 4 * c + lane + n
    return (g % 4, k, g // 4)


def is_first(turn):
    return turn[1] is None and turn[0] == 0 and turn[2] == 0


def edge_pass(nc, layer, dram, keep):
    with Phase(nc) as ctx:
        def sb(name, shape, dt=F32):
            return ctx.enter_context(nc.sbuf_tensor(f"edge{layer}_{name}", shape, dt))

        def ps(name, shape, dt=F32):
            return ctx.enter_context(nc.psum_tensor(f"edge{layer}_{name}", shape, dt))

        def sem(name):
            return ctx.semaphore(f"edge{layer}_{name}")

        acc, ends, qc = keep["acc"], keep["ends"], keep["qc"]
        kv = sb("kv", [P, 2, G, KV])
        idx = sb("idx", [P, 2, G], I32)
        rel = sb("rel", [P, 2, G * P], BF16)
        flags = sb("flags", [G * H, 2, 2, P])
        col = sb("col", [P, 4, G])
        last = sb("last", [P, 4, G])
        regs = sb("regs", [1, 4, 2 * G], I32)
        spread = sb("spread", [P, 4, P])
        sel = sb("sel", [P, SELBUFS, SELW])
        score = sb("score", [P, 2, G * H])
        up = sb("up", [G * H, P])
        top = sb("top", [G * H, P])
        below = sb("below", [P, G * H])
        wm = sb("wm", [P, 2, G, ZM])
        psq = [ps(f"q{i}", [P, 512]) for i in range(QBUFS)]
        turned = ps("turned", [P, 512])
        pst = turned[0:G * H, 0:P]
        psm = turned[:, P:P + G * H]
        psa = [ps(f"sums{i}", [P, 512]) for i in range(ABUFS)]

        s_clear = sem("cleared")
        s_idx = [sem(f"idx{i}") for i in range(2)]
        s_rel = [sem(f"rel{i}") for i in range(2)]
        s_flags = [sem(f"flags{i}") for i in range(2)]
        s_table = [sem(f"table{i}") for i in range(4)]
        s_row = [[sem(f"rows{i}_{j}") for j in range(G)] for i in range(2)]

        dve_p = Progress(nc, ctx, f"edge{layer}_dve", 4)
        act_p = Progress(nc, ctx, f"edge{layer}_act", 4)
        pe_p = Progress(nc, ctx, f"edge{layer}_pe", 4)
        heads, tails = [], []
        dve_steps = [f"spread{j}" for j in range(AHEAD)]
        for j in range(G):
            dve_steps += [f"product{j}"] + ([f"spread{j + AHEAD}"] if j + AHEAD < G else []) + [f"score{j}"]
        dve_steps += ["up", "top", "below", "maxima"]
        for j in range(G):
            dve_steps += [f"sel{j}", f"value{j}"]
        dve_p.begin(dve_steps)
        pe_p.begin([f"q{j}" for j in range(G)] + ["score_t", "max_t"] + [f"sums{j}" for j in range(G)])
        act_p.begin(["weights"] + [f"{n}{j}" for j in range(G) for n in ("acc", "ends")])

        def fill(sems, depth, turn):
            lane, k, c = turn
            if depth == 4:
                return sems[lane], (16 * (c + 1) if k is None else k * 16 + 16 * (c + 1))
            n = 2 * c + lane // 2
            return sems[lane % 2], (16 * (n + 1) if k is None else k * 32 + 16 * (n + 1))

        def groups_of(eng, body):
            body((0, None, 0), first=True)
            body((1, None, 0))
            body((2, None, 0))
            body((3, None, 0))
            with eng.Fori(0, GROUPS // 4 - 2) as k:
                for r in range(4):
                    body((r, k, 1))
            for g in range(GROUPS - 4, GROUPS):
                body((g % 4, None, g // 4), end=g == GROUPS - 1)

        def number(turn, scale):
            lane, k, c = turn
            g = (4 * c + lane) * scale
            return g if k is None else k * (4 * scale) + g

        block = ctx.enter_context(nc.Block())

        @block.sync
        def _(sp):
            def load_idx(turn, wait=True):
                if wait:
                    before = later(turn, -2)
                    for j in range(G):
                        wait_beside(sp, s_clear, *fill([s_row[0][j], s_row[1][j]], 2, before))
                sp.dma_start(idx[:, turn[0] % 2, :], dram["idx"][:, bass.ds(number(turn, G), G)])\
                    .then_inc(fill(s_idx, 2, turn)[0], 16)

            def load_rel(turn, wait=True):
                if wait:
                    dve_p.wait(sp, later(turn, -2), f"spread{G - 1}", beside=s_clear)
                sp.dma_start(rel[:, turn[0] % 2, :],
                             dram["rel"].rearrange("s e -> (s e)")[bass.ds(number(turn, G * P), G * P)]
                             .partition_broadcast(P)).then_inc(fill(s_rel, 2, turn)[0], 16)

            def load_rest(turn, wait=True):
                if wait:
                    before = later(turn, -4)
                    dve_p.wait(sp, before, f"value{G - 1}", beside=s_clear)
                    act_p.wait(sp, before, f"ends{G - 1}", beside=s_clear)
                slot = turn[0]
                s = s_table[slot]
                for tab, name in ((col, "col"), (last, "last")):
                    sp.dma_start(tab[:, slot, :], dram[name][:, bass.ds(number(turn, G), G)]).then_inc(s, 16)
                sp.dma_start(regs[:, slot, :],
                             dram["regs"].rearrange("(o s) w -> o (s w)", o=1)[:, bass.ds(number(turn, 2 * G), 2 * G)])\
                    .then_inc(s, 16)

            def load_flags(turn, wait=True):
                if wait:
                    dve_p.wait(sp, later(turn, -2), "top", beside=s_clear)
                s = fill(s_flags, 2, turn)[0]
                for w in range(2):
                    rows = dram["flags"][w][bass.ds(number(turn, G), G), :].unsqueeze(1)
                    sp.dma_start(flags[:, turn[0] % 2, w, :], bc(rows, [G, H, P])).then_inc(s, 16)

            for g in range(4):
                turn = (g, None, 0)
                if g < 2:
                    load_idx(turn, False)
                    load_rel(turn, False)
                    load_flags(turn, False)
                load_rest(turn, False)

            def body(turn, first=False, end=False):
                pass

            def one(turn, four=True):
                load_idx(later(turn, 2))
                load_rel(later(turn, 2))
                load_flags(later(turn, 2))
                if four:
                    load_rest(later(turn, 4))

            with sp.Fori(0, GROUPS // 4 - 1) as k:
                for r in range(4):
                    one((r, k, 0))
            for g in range(GROUPS - 4, GROUPS - 2):
                one((g % 4, None, g // 4), four=False)

        @block.gpsimd
        def _(pool):
            def rows(turn, first=False):
                lane = turn[0] % 2
                for j in range(G):
                    if j == 0:
                        wait_beside(pool, s_clear, *fill(s_idx, 2, turn))
                    if not first:
                        pe_p.wait(pool, later(turn, -2), f"sums{j}", beside=s_clear)
                    nc.gpsimd.indirect_dma_start(
                        kv[:, lane, j, :], None, dram["kv"],
                        bass.IndirectOffsetOnAxis(ap=idx[:, lane, j:j + 1], axis=0)).then_inc(s_row[lane][j], 16)

            rows((0, None, 0), True)
            rows((1, None, 0), True)
            rows((2, None, 0))
            rows((3, None, 0))
            with pool.Fori(0, GROUPS // 4 - 1) as k:
                for r in range(4):
                    rows((r, k, 1))

        @block.vector
        def _(dve):
            v = nc.vector
            v.memset(wm[:, :, :, :], 0.0).then_inc(s_clear, 1)
            for i in range(ABUFS):
                v.memset(psa[i][:, :], 0.0).then_inc(s_clear, 1)
            dve.wait_ge(s_clear, 1 + ABUFS)

            def spread_of(turn, j, first=False):
                dve.wait_ge(*fill(s_rel, 2, turn))
                if not first:
                    user, step = (turn, j - 4) if j >= 4 else (later(turn, -1), j + 4)
                    pe_p.wait(dve, user, f"q{step}")
                dve_p.tick(v.tensor_scalar(spread[:, j % 4, :], rel[:, turn[0] % 2, j * P:(j + 1) * P],
                                           keep["part"][:, 0:1], None, ALU.is_equal), turn, f"spread{j}")

            def table(turn, times=3):
                lane, k, c = turn
                value = 48 * (c + 1)
                dve.wait_ge(s_table[lane], value if k is None else k * 48 + value)

            def body(turn, first=False, end=False):
                before = None if first else later(turn, -1)
                for what, j in WEAVE:
                    lane = turn[0] % 2
                    if what == "head":
                        pe_p.wait(dve, turn, f"q{j}")
                        dve.wait_ge(*fill([s_row[0][j], s_row[1][j]], 2, turn))
                        k_rows = kv[:, lane, j, 0:D]
                        dve_p.tick(v.tensor_tensor(k_rows, k_rows, psq[j % QBUFS][:, 0:D], ALU.mult),
                                   turn, f"product{j}")
                        if j + AHEAD < G:
                            spread_of(turn, j + AHEAD)
                        elif not end:
                            spread_of(later(turn, 1), j + AHEAD - G)
                        dve_p.wait(dve, turn, f"product{j}")
                        dve_p.tick(v.tensor_reduce(score[:, lane, j * H:(j + 1) * H],
                                                   k_rows.rearrange("p (h d) -> p h d", h=H), AX.X, ALU.add),
                                   turn, f"score{j}")
                    elif first:
                        continue
                    else:
                        rest(before, what, j, is_first(before))

            def rest(turn, what, j, earliest=False):
                lane = turn[0] % 2
                if what == "scan" and j == 0:
                    lane_, k, c = turn
                    n = 2 * c + lane_ // 2
                    value = 32 * (n + 1)
                    dve.wait_ge(s_flags[lane], value if k is None else k * 64 + value)
                    pe_p.wait(dve, turn, "score_t")
                    dve_p.tick(v.tensor_tensor_scan(up[:, :], flags[:, lane, 0, :], pst[:, :], -BIG,
                                                    ALU.add, ALU.max), turn, "up")
                elif what == "scan":
                    dve_p.wait(dve, turn, "up")
                    dve_p.tick(v.tensor_tensor_scan(top[:, ::-1], flags[:, lane, 1, ::-1], up[:, ::-1], -BIG,
                                                    ALU.add, ALU.max), turn, "top")
                elif what == "weigh":
                    table(turn)
                    pe_p.wait(dve, turn, "max_t")
                    dve_p.tick(v.tensor_tensor(below[:, :], score[:, lane, :], psm[:, :], ALU.subtract),
                               turn, "below")
                    dve_p.tick(v.tensor_tensor(wm[:, lane, :, 32:ZM], psm[:, :].rearrange("p (j h) -> p j h", h=H),
                                               bc(last[:, turn[0], :].unsqueeze(2), [P, G, H]), ALU.mult),
                               turn, "maxima")
                else:
                    if j >= SELBUFS:
                        pe_p.wait(dve, turn, f"sums{j - SELBUFS}")
                    elif not earliest:
                        pe_p.wait(dve, later(turn, -1), f"sums{j + G - SELBUFS}")
                    dve_p.tick(v.tensor_scalar(sel[:, j % SELBUFS, :], keep["cols"][:, :],
                                               col[:, turn[0], j:j + 1], None, ALU.is_equal), turn, f"sel{j}")
                    if j == 0:
                        act_p.wait(dve, turn, "weights")
                    values = kv[:, lane, j, D:KV].rearrange("p (h d) -> p h d", h=H)
                    dve_p.tick(v.tensor_tensor(values, values,
                                               bc(wm[:, lane, j, 0:H].unsqueeze(2), [P, H, DH]), ALU.mult),
                               turn, f"value{j}")

            for j in range(AHEAD):
                spread_of((0, None, 0), j, True)
            groups_of(dve, body)
            final = (3, None, GROUPS // 4 - 1)
            for what, j in WEAVE:
                if what != "head":
                    rest(final, what, j)

        @block.tensor
        def _(pe):
            t = nc.tensor
            pe.wait_ge(s_clear, 1 + ABUFS)

            def spread_q(turn, j, first=False):
                if j >= QBUFS:
                    dve_p.wait(pe, turn, dve_p.last_of(f"spread{j}", f"product{j - QBUFS}"), beside=s_clear)
                else:
                    dve_p.wait(pe, turn, f"spread{j}", beside=s_clear)
                    if not first:
                        dve_p.wait(pe, later(turn, -1), f"product{j + G - QBUFS}", beside=s_clear)
                if j == 0:
                    lane, k, c = turn
                    value = 48 * (c + 1)
                    wait_beside(pe, s_clear, s_table[lane], value if k is None else k * 48 + value)
                at = pe.value_load(regs[0:1, turn[0], 2 * j + 1:2 * j + 2], min_val=0, max_val=(BLOCKS - 1) * QC)
                pe_p.tick(t.matmul(psq[j % QBUFS][:, 0:D], spread[:, j % 4, :], qc[:, bass.ds(at, D)],
                                   start=True, stop=True), turn, f"q{j}")

            def body(turn, first=False, end=False):
                for what, j in WEAVE:
                    if what == "head":
                        if j + Q_AHEAD < G:
                            spread_q(turn, j + Q_AHEAD, first and j + Q_AHEAD < QBUFS)
                        elif not end:
                            spread_q(later(turn, 1), j + Q_AHEAD - G)
                    elif not first:
                        rest(later(turn, -1), what, j, is_first(later(turn, -1)))

            def rest(turn, what, j, earliest=False):
                lane = turn[0] % 2
                if what == "scan" and j == 0:
                    dve_p.wait(pe, turn, f"score{G - 1}", beside=s_clear)
                    pe_p.tick(t.transpose(pst[:, :], score[:, lane, :], keep["ident"][:, :]), turn, "score_t")
                elif what == "scan":
                    dve_p.wait(pe, turn, "top", beside=s_clear)
                    pe_p.tick(t.transpose(psm[:, :], top[:, :], keep["ident"][0:G * H, 0:G * H]), turn, "max_t")
                elif what == "tail":
                    if j >= ABUFS:
                        act_p.wait(pe, turn, f"ends{j - ABUFS}")
                    elif not earliest:
                        act_p.wait(pe, later(turn, -1), f"ends{j + G - ABUFS}")
                    dve_p.wait(pe, turn, f"value{j}")
                    one_hot = sel[:, j % SELBUFS, :]
                    out = psa[j % ABUFS]
                    for half in range(2):
                        t.matmul(out[:, half * SELW:(half + 1) * SELW],
                                 kv[:, lane, j, D + half * P:D + (half + 1) * P], one_hot, start=True, stop=True)
                    pe_p.tick(t.matmul(out[0:ZM, 2 * SELW:3 * SELW], wm[:, lane, j, :], one_hot,
                                       start=True, stop=True), turn, f"sums{j}")

            for j in range(Q_AHEAD):
                spread_q((0, None, 0), j, True)
            groups_of(pe, body)
            final = (3, None, GROUPS // 4 - 1)
            for what, j in WEAVE:
                if what != "head":
                    rest(final, what, j)

        @block.scalar
        def _(act):
            s = nc.scalar

            def rest(turn, what, j, earliest=False):
                lane = turn[0] % 2
                if what == "weigh":
                    dve_p.wait(act, turn, "below")
                    act_p.tick(s.activation(wm[:, lane, :, 0:H], below[:, :].rearrange("p (j h) -> p j h", h=H),
                                            ACT.Exp, scale=SCALE), turn, "weights")
                elif what == "tail":
                    if j == 0:
                        lane_, k, c = turn
                        value = 48 * (c + 1)
                        wait_beside(act, s_clear, s_table[lane_], value if k is None else k * 48 + value)
                    at = act.value_load(regs[0:1, turn[0], 2 * j:2 * j + 1], min_val=0, max_val=BLOCKS * P)
                    if j > 0 or not earliest:
                        act_p.wait(act, turn if j else later(turn, -1), f"acc{(j - 1) % G}")
                    pe_p.wait(act, turn, f"sums{j}")
                    out = psa[j % ABUFS][:, 0:3 * SELW].rearrange("p (c n) -> p c n", c=3)
                    act_p.tick(s.copy(acc[:, :, bass.ds(at, P)], out[:, :, 0:P]), turn, f"acc{j}")
                    act_p.tick(s.copy(ends[:, :, bass.ds(number(turn, 2 * G) + 2 * j, 2)], out[:, :, P:SELW]),
                               turn, f"ends{j}")

            def body(turn, first=False, end=False):
                if not first:
                    for what, j in WEAVE:
                        rest(later(turn, -1), what, j, is_first(later(turn, -1)))

            groups_of(act, body)
            for what, j in WEAVE:
                rest((3, None, GROUPS // 4 - 1), what, j)


def merge_ends(nc, layer, dram, keep):
    with Phase(nc) as ctx:
        def sb(name, shape, dt=F32):
            return ctx.enter_context(nc.sbuf_tensor(f"merge{layer}_{name}", shape, dt))

        def ps(name, shape, dt=F32):
            return ctx.enter_context(nc.psum_tensor(f"merge{layer}_{name}", shape, dt))

        def sem(name):
            return ctx.semaphore(f"merge{layer}_{name}")

        ends, qc, ident = keep["ends"], keep["qc"], keep["ident"]
        node = sb("node", [H, ENDS])
        opens = sb("opens", [H, ENDS])
        closes = sb("closes", [H, ENDS])
        m = sb("m", [H, ENDS])
        up = sb("up", [H, ENDS])
        closing = sb("closing", [H, ENDS])
        part = sb("part", [P, 2, QC - D + H])
        rows = sb("rows", [P, ETILES * QC])
        one_hot = sb("one_hot", [P, 2, P])
        eregs = sb("eregs", [1, P, 2], I32)
        pt = [ps(f"t{i}", [P, 512]) for i in range(2)]
        pm = [ps(f"m{i}", [P, QC]) for i in range(2)]

        s_node = sem("node")
        s_regs = sem("regs")
        s_v = sem("dve")
        s_weight = sem("weight")
        s_turned = sem("turned")
        dve_p = Progress(nc, ctx, f"merge{layer}_dvep", 2)
        pe_p = Progress(nc, ctx, f"merge{layer}_pep", 2)
        dve_p.begin(["one_hot", "added"])
        pe_p.begin(["summed"])
        count = {"n": 0, "at": {}}
        block = ctx.enter_context(nc.Block())

        def pairs_of(eng, body):
            for turn in ((0, None, 0), (1, None, 0), (0, None, 1)):
                body(turn)
            with eng.Fori(1, MERGES // 2) as k:
                body((1, k, 0))
                body((0, k, 1))

        def number(turn):
            lane, k, c = turn
            return 2 * c + lane if k is None else k * 2 + (2 * c + lane)

        assert MERGES % 2 == 1

        @block.sync
        def _(sp):
            sp.dma_start(node[:, :], dram["ends"][0:ENDS].partition_broadcast(H)).then_inc(s_node, 16)
            sp.dma_start(eregs[:, :, :], dram["eregs"].rearrange("(o p) w -> o p w", o=1)).then_inc(s_regs, 16)

        @block.vector
        def _(dve):
            v = nc.vector

            def link(ins, name=None):
                ins.then_inc(s_v, 1)
                count["n"] += 1
                if name:
                    count["at"][name] = count["n"]
                dve.wait_ge(s_v, count["n"])

            link(v.memset(qc[:, :], 0.0))
            link(v.tensor_copy(m[:, :], ends[32:32 + H, 2, :]))
            link(v.memset(opens[:, 0:1], 0.0))
            link(v.memset(closes[:, ENDS - 1:ENDS], 0.0))
            dve.wait_ge(s_node, 16)
            link(v.tensor_tensor(opens[:, 1:ENDS], node[:, 1:ENDS], node[:, 0:ENDS - 1], ALU.not_equal))
            link(v.tensor_copy(closing[:, 0:ENDS - 1], opens[:, 1:ENDS]))
            link(v.memset(closing[:, ENDS - 1:ENDS], 1.0))
            link(v.tensor_scalar(opens[:, 1:ENDS], opens[:, 1:ENDS], -BIG, None, ALU.mult))
            link(v.tensor_copy(closes[:, 0:ENDS - 1], opens[:, 1:ENDS]))
            link(v.tensor_scalar(up[:, :], ends[0:H, 2, :], 0.5, -BIG, ALU.is_lt, ALU.mult))
            link(v.tensor_tensor(m[:, :], m[:, :], up[:, :], ALU.add))
            link(v.tensor_tensor_scan(up[:, :], opens[:, :], m[:, :], -BIG, ALU.add, ALU.max))
            link(v.tensor_tensor_scan(opens[:, ::-1], closes[:, ::-1], up[:, ::-1], -BIG, ALU.add, ALU.max))
            link(v.tensor_tensor(m[:, :], m[:, :], opens[:, :], ALU.subtract), "below")
            link(v.tensor_tensor(closing[:, :], closing[:, :], opens[:, :], ALU.mult), "closing")
            dve.wait_ge(s_weight, 1)
            for u in range(ETILES):
                dve.wait_ge(s_turned, u + 1)
                out = rows[:, u * QC:(u + 1) * QC]
                t = pt[u % 2]
                link(v.tensor_copy(part[:, u % 2, :], t[:, D:D + 3 * H]))
                weight = bc(part[:, u % 2, 2 * H:3 * H].unsqueeze(2), [P, H, DH])
                v.tensor_tensor(out[:, 0:D].rearrange("p (h d) -> p h d", h=H),
                                t[:, 0:D].rearrange("p (h d) -> p h d", h=H), weight, ALU.mult).then_inc(s_v, 1)
                v.tensor_tensor(out[:, D:D + H], part[:, u % 2, 0:H], part[:, u % 2, 2 * H:3 * H], ALU.mult)\
                    .then_inc(s_v, 1)
                count["n"] += 2
                link(v.tensor_copy(out[:, D + H:QC], part[:, u % 2, H:2 * H]), f"row{u}")

            def body(turn):
                lane = turn[0]
                pe_p.wait_turn(dve, turn)
                dve_p.tick(v.tensor_scalar(one_hot[:, lane, :], keep["cols"][:, 0:P],
                                           keep["ecol"][:, bass.ds(number(turn), 1)], None, ALU.is_equal),
                           turn, "one_hot")
                at = dve.value_load(eregs[0:1, bass.ds(number(turn), 1), 1:2], min_val=0, max_val=(BLOCKS - 1) * QC)
                pe_p.wait(dve, turn, "summed")
                place = qc[:, bass.ds(at, QC)]
                if lane or turn[2]:
                    dve_p.wait(dve, (0, turn[1], turn[2]) if lane else (1, turn[1], turn[2] - 1), "added")
                dve_p.tick(v.tensor_tensor(place, place, pm[lane][:, :], ALU.add), turn, "added")

            dve.wait_ge(s_regs, 16)
            pairs_of(dve, body)

        at = count["at"]

        @block.scalar
        def _(act):
            act.wait_ge(s_v, at["below"])
            nc.scalar.activation(up[:, :], m[:, :], ACT.Exp, scale=SCALE).then_inc(s_weight, 1)

        @block.tensor
        def _(pe):
            t = nc.tensor
            pe.wait_ge(s_weight, 1)
            pe.wait_ge(s_v, at["closing"])
            for u in range(ETILES):
                if u >= 2:
                    pe.wait_ge(s_v, at[f"row{u - 2}"])
                cut = slice(u * P, (u + 1) * P)
                t.transpose(pt[u % 2][:, 0:P], ends[:, 0, cut], ident[:, :])
                t.transpose(pt[u % 2][:, P:D], ends[:, 1, cut], ident[:, :])
                for i, row in enumerate((ends[0:H, 2, cut], closing[:, cut], up[:, cut])):
                    mm = t.transpose(pt[u % 2][:, D + i * H:D + (i + 1) * H], row, ident[0:H, 0:H])
                mm.then_inc(s_turned, 1)
            pe.wait_ge(s_v, at[f"row{ETILES - 1}"])
            pe.wait_ge(s_regs, 16)

            def body(turn):
                lane = turn[0]
                at_ = pe.value_load(eregs[0:1, bass.ds(number(turn), 1), 0:1], min_val=0, max_val=(ETILES - 1) * QC)
                dve_p.wait(pe, turn, "one_hot")
                pe_p.tick(t.matmul(pm[lane][:, :], one_hot[:, lane, :], rows[:, bass.ds(at_, QC)],
                                   start=True, stop=True), turn, "summed")

            pairs_of(pe, body)


RSQRT_GUESS = 0x5F3759DF
NEWTON = 3
STAGES = {
    "first": ("norm_in", "project_in", "norm_q", "qkv"),
    "middle": ("merge", "attend", "norm_ff", "ffn", "norm_q", "qkv"),
    "last": ("merge", "attend", "norm_ff", "ffn", "norm_out", "gate", "ffn_out"),
}


def node_pass(nc, kind, a, dram, keep):
    stages = STAGES[kind]
    layer = 0 if kind != "last" else 1
    nxt = 0 if kind == "first" else 1
    with Phase(nc) as ctx:
        def sb(name, shape, dt=F32):
            return ctx.enter_context(nc.sbuf_tensor(f"{kind}_{name}", shape, dt))

        def ps(name, shape, dt=F32):
            return ctx.enter_context(nc.psum_tensor(f"{kind}_{name}", shape, dt))

        def sem(name):
            return ctx.semaphore(f"{kind}_{name}")

        acc, qc, ident, self_ = keep["acc"], keep["qc"], keep["ident"], keep["self"]
        x = sb("x", [P, 2, D])
        h = sb("h", [P, 2, D])
        xn = sb("xn", [P, 2, D])
        xt = sb("xt", [P, 2, D])
        st = sb("st", [P, 2, 6])
        mv = sb("mv", [P, 2, 2])
        var = sb("var", [P, 2, 1])
        half_bits = sb("half_bits", [P, 2, 1], I32)
        yy = sb("yy", [P, 2, 1])
        rs = sb("rs", [P, 2, 1])
        tmp = sb("tmp", [P, 2, D])
        pt = [ps(f"pt{i}", [P, 512]) for i in range(2)]
        ph = [ps(f"ph{i}", [P, 1024]) for i in range(2)]
        loads = []

        def col_of(name, vec):
            n = vec.shape[0] // P
            t = sb(name, [P, n])
            loads.append((t[:, :], vec.rearrange("(c p) -> p c", p=P)))
            return t

        def row_of(name, vec, into=None):
            n = vec.shape[0]
            t = sb(name, [P, n]) if into is None else into
            loads.append((t[:, 0:n] if into is None else into, vec.partition_broadcast(P)))
            return t

        def mat_of(name, mat, into=None):
            c = mat.shape[0] // P
            t = sb(name, [P, c, mat.shape[1]])[:, :, :] if into is None else into
            loads.append((t, mat.rearrange("(c p) n -> p c n", p=P)))
            return t

        if kind == "first":
            w_in = mat_of("w_in", a["L0_gnn_w_in"])
            b_in = row_of("b_in", a["L0_gnn_b_in"])
        if kind != "last":
            w_qkv = sb("w_qkv", [P, 2, 3 * D])
            b_qkv = sb("b_qkv", [P, 3 * D])
            for i, n in enumerate("qkv"):
                mat_of("", a[f"L0_gnn_w{n}"][nxt], w_qkv[:, :, i * D:(i + 1) * D])
                row_of("", a[f"L0_gnn_b{n}"][nxt], b_qkv[:, i * D:(i + 1) * D])
            g1 = col_of("g1", a["L0_gnn_ln1_g"][nxt])
            b1n = col_of("b1n", a["L0_gnn_ln1_b"][nxt])
            kv_out = sb("kv_out", [P, 2, KV])
        if kind != "first":
            w_o = mat_of("w_o", a["L0_gnn_wo"][layer])
            b_o = row_of("b_o", a["L0_gnn_bo"][layer])
            w_1 = mat_of("w_1", a["L0_gnn_w1"][layer])
            b_1 = col_of("b_1", a["L0_gnn_b1"][layer])
            w_2 = mat_of("w_2", a["L0_gnn_w2"][layer])
            b_2 = row_of("b_2", a["L0_gnn_b2"][layer])
            g2 = col_of("g2", a["L0_gnn_ln2_g"][layer])
            b2n = col_of("b2n", a["L0_gnn_ln2_b"][layer])
            v_in = sb("v_in", [P, 2, D])
            ab = sb("ab", [P, 2, 3, P])
            agg = sb("agg", [P, 2, D])
            zm = sb("zm", [P, 2, 2 * H])
            mx = sb("mx", [P, 2, H])
            dd = sb("dd", [P, 2, 2 * H])
            ee = sb("ee", [P, 2, 2 * H])
            zz = sb("zz", [P, 2, H])
            z2 = sb("z2", [P, 2, H])
            has = sb("has", [P, 2, H])
            hid = sb("hid", [P, 2, FF])
        if kind == "last":
            f_1 = mat_of("f_1", a["L0_ffn_w1"])
            f_b1 = col_of("f_b1", a["L0_ffn_b1"])
            f_2 = mat_of("f_2", a["L0_ffn_w2"])
            f_b2 = row_of("f_b2", a["L0_ffn_b2"])
            w_r = row_of("w_r", a["L0_ffn_wr"].rearrange("d o -> (d o)"))
            b_r = row_of("b_r", a["L0_ffn_br"])
            gate = sb("gate", [P, 2, 1])

        s_weights = sem("weights")
        s_zero = sem("zero")
        s_x = [sem(f"x{i}") for i in range(2)]
        s_h = [sem(f"h{i}") for i in range(2)]
        s_v = [sem(f"v{i}") for i in range(2)]
        s_hout = [sem(f"h_out{i}") for i in range(2)]
        s_kvout = [sem(f"kv_out{i}") for i in range(2)]

        def norm_steps(tag):
            return [f"{tag}_{s}" for s in
                    ["stats", "moments", "var", "bits", "guess"] +
                    [f"{x}{n}" for n in range(NEWTON) for x in ("yy", "factor", "newton")] + ["normed"]]

        dve_steps = {
            "norm_in": norm_steps("in"), "project_in": ["h"], "norm_q": norm_steps("q"),
            "qkv": ["kv", "q", "qk", "self"],
            "merge": ["agg", "z", "m", "top", "below_m", "below_s", "has", "z_scaled", "z_sum", "z_inv", "z_has",
                      "by_m", "by_s", "agg_scaled", "v_scaled", "merged"],
            "attend": ["attended", "attended_b"], "norm_ff": norm_steps("ff"),
            "ffn": ["ffn", "ffn_b"] + (["x2"] if kind == "last" else []),
            "norm_out": norm_steps("out"), "gate": ["weighed", "gate0", "gate", "gate_kept", "base"],
            "ffn_out": ["y_b", "y"],
        }
        pe_steps = {
            "norm_in": ["in_t"], "project_in": ["in_p"], "norm_q": ["q_t"], "qkv": ["qkv"],
            "merge": ["acc_t"], "attend": ["agg_t", "attend"], "norm_ff": ["ff_t"], "ffn": ["ffn_1", "ffn_2"],
            "norm_out": ["out_t"], "gate": [], "ffn_out": ["out_1", "out_2"],
        }
        act_steps = {
            "norm_in": ["in_x"], "project_in": [], "norm_q": ["q_x0", "q_x"], "qkv": [],
            "merge": ["acc", "exp"], "attend": ["agg_x"], "norm_ff": ["ff_x0", "ff_x"],
            "ffn": [f"gelu{i}" for i in range(FF // P)], "norm_out": ["out_x"], "gate": [],
            "ffn_out": [f"gelu_out{i}" for i in range(FF // P)],
        }
        progress = {}
        for name, steps in (("dve", dve_steps), ("pe", pe_steps), ("act", act_steps)):
            progress[name] = Progress(nc, ctx, f"{kind}_{name}", 2)
            progress[name].begin([s for stage in stages for s in steps[stage]])
        dve_p, pe_p, act_p = progress["dve"], progress["pe"], progress["act"]

        def blocks_of(eng, do):
            for stage in stages:
                for lane in range(2):
                    do((lane, None, 0), stage)
            with eng.Fori(1, BLOCKS // 2) as k:
                for stage in stages:
                    for lane in range(2):
                        do((lane, k, 0), stage)
            for stage in stages:
                do((0, None, BLOCKS // 2), stage)

        assert BLOCKS % 2 == 1

        def number(turn, scale=1):
            lane, k, c = turn
            b = (2 * c + lane) * scale
            return b if k is None else k * (2 * scale) + b

        def landed(eng, sems, turn, beside=None):
            lane, k, c = turn
            value = 16 * (c + 1) if k is None else k * 16 + 16 * (c + 1)
            if beside is None:
                eng.wait_ge(sems[lane], value)
            else:
                wait_beside(eng, beside, sems[lane], value)

        def stored_before(eng, sems, turn):
            lane, k, c = turn
            eng.wait_ge(sems[lane], 16 * c if k is None else k * 16 + 16 * c)

        block = ctx.enter_context(nc.Block())

        @block.sync
        def _(sp):
            def load(turn, first=False, rows=P):
                lane = turn[0]
                before = (lane, turn[1], turn[2] - 1)
                at = bass.ds(number(turn, P), rows)
                full = bass.ds(number(turn, P), P)
                if kind != "middle":
                    if not first:
                        dve_p.wait(sp, before, "in_normed" if kind == "first" else "x2", beside=s_zero)
                    sp.dma_start(x[0:rows, lane, :], a["x"][at, :]).then_inc(s_x[lane], 16)
                if kind != "first":
                    if not first:
                        dve_p.wait(sp, before, "x2" if kind == "last" else "q_normed", beside=s_zero)
                        if kind == "middle":
                            landed(sp, s_hout, before, beside=s_zero)
                    sp.dma_start(h[:, lane, :], dram["h"][full, :]).then_inc(s_h[lane], 16)
                    sp.dma_start(v_in[:, lane, :], dram["kv"][full, D:KV]).then_inc(s_v[lane], 16)

            def store(turn):
                lane = turn[0]
                at = bass.ds(number(turn, P), P)
                if kind == "last":
                    return
                dve_p.wait(sp, turn, "h" if kind == "first" else "ffn_b", beside=s_zero)
                sp.dma_start(dram["h"][at, :], h[:, lane, :]).then_inc(s_hout[lane], 16)
                dve_p.wait(sp, turn, "kv", beside=s_zero)
                sp.dma_start(dram["kv"][at, :], kv_out[:, lane, :]).then_inc(s_kvout[lane], 16)

            sp.wait_ge(s_zero, 1)
            for i in range(2):
                load((i, None, 0), first=True)
            with sp.Fori(0, BLOCKS // 2 - 1) as k:
                for lane in range(2):
                    store((lane, k, 0))
                    load((lane, k, 1))
            store((0, None, BLOCKS // 2 - 1))
            load((0, None, BLOCKS // 2), rows=LAST)
            store((1, None, BLOCKS // 2 - 1))
            store((0, None, BLOCKS // 2))
            if kind != "last":
                for s in (s_hout, s_kvout):
                    landed(sp, s, (0, None, BLOCKS // 2))
                    landed(sp, s, (1, None, BLOCKS // 2 - 1))

        @block.gpsimd
        def _(pool):
            with nc.allow_non_contiguous_dma(reason="biases and gains as columns"):
                for tile_, source in loads:
                    pool.dma_start(tile_, source).then_inc(s_weights, 16)

        @block.vector
        def _(dve):
            v = nc.vector

            def step(ins, turn, name):
                dve_p.tick(ins, turn, name)
                dve_p.wait(dve, turn, name)

            def norm(turn, rows, tag):
                i = turn[0]
                dve_p.tick(v.bn_stats(out=st[:, i, :], in_=rows), turn, f"{tag}_stats")
                dve_p.wait(dve, turn, f"{tag}_stats", beside=s_weights)
                step(v.bn_aggr(out=mv[:, i, :], in_=st[:, i, :]), turn, f"{tag}_moments")
                step(v.tensor_scalar(var[:, i, :], mv[:, i, 1:2], EPS, None, ALU.add), turn, f"{tag}_var")
                step(v.tensor_single_scalar(half_bits[:, i, :], var[:, i, :].bitcast(I32), 1,
                                            op=ALU.logical_shift_right), turn, f"{tag}_bits")
                step(v.tensor_scalar(rs[:, i, :].bitcast(I32), half_bits[:, i, :], -1.0, float(RSQRT_GUESS),
                                     ALU.mult, ALU.add), turn, f"{tag}_guess")
                for n in range(NEWTON):
                    step(v.scalar_tensor_tensor(out=yy[:, i, :], in0=rs[:, i, :], scalar=var[:, i, 0:1],
                                                in1=rs[:, i, :], op0=ALU.mult, op1=ALU.mult), turn, f"{tag}_yy{n}")
                    step(v.tensor_scalar(yy[:, i, :], yy[:, i, :], -0.5, 1.5, ALU.mult, ALU.add),
                         turn, f"{tag}_factor{n}")
                    step(v.tensor_tensor(rs[:, i, :], rs[:, i, :], yy[:, i, :], ALU.mult), turn, f"{tag}_newton{n}")
                step(v.tensor_scalar(xn[:, i, :], rows, mv[:, i, 0:1], rs[:, i, 0:1], ALU.subtract, ALU.mult),
                     turn, f"{tag}_normed")

            def heads(ap):
                return ap.rearrange("p (h d) -> p h d", h=H)

            def per_head(ap):
                return bc(ap.unsqueeze(2), [P, H, DH])

            def do(turn, stage):
                i = turn[0]
                xi, hi, prod = x[:, i, :], h[:, i, :], pt[i][:, D:2 * D]
                if stage == "norm_in":
                    landed(dve, s_x, turn)
                    norm(turn, xi, "in")
                elif stage == "project_in":
                    stored_before(dve, s_hout, turn)
                    pe_p.wait(dve, turn, "in_p")
                    step(v.tensor_tensor(hi, prod, b_in[:, :], ALU.add), turn, "h")
                elif stage == "norm_q":
                    norm(turn, hi, "q")
                elif stage == "qkv":
                    pe_p.wait(dve, turn, "qkv")
                    stored_before(dve, s_kvout, turn)
                    q = qc[:, bass.ds(number(turn, QC), D)]
                    step(v.tensor_tensor(kv_out[:, i, :], ph[i][:, D:3 * D], b_qkv[:, D:3 * D], ALU.add), turn, "kv")
                    step(v.tensor_tensor(q, ph[i][:, 0:D], b_qkv[:, 0:D], ALU.add), turn, "q")
                    dve_p.tick(v.tensor_tensor(tmp[:, i, :], q, kv_out[:, i, 0:D], ALU.mult), turn, "qk")
                    dve_p.wait(dve, turn, "qk", beside=s_weights)
                    step(v.tensor_reduce(self_[:, bass.ds(number(turn, H), H)], heads(tmp[:, i, :]), AX.X, ALU.add),
                         turn, "self")
                elif stage == "merge":
                    landed(dve, s_h, turn)
                    landed(dve, s_v, turn)
                    pe_p.wait(dve, turn, "acc_t")
                    z, m = zm[:, i, 0:H], zm[:, i, H:2 * H]
                    own = self_[:, bass.ds(number(turn, H), H)]
                    at = number(turn, QC)
                    step(v.tensor_tensor(agg[:, i, :], pt[i][:, 0:D], qc[:, bass.ds(at, D)], ALU.add), turn, "agg")
                    step(v.tensor_tensor(z, pt[i][:, D:D + H], qc[:, bass.ds(at + D, H)], ALU.add), turn, "z")
                    step(v.tensor_tensor(m, pt[i][:, D + 32:D + ZM], qc[:, bass.ds(at + D + H, H)], ALU.add),
                         turn, "m")
                    step(v.tensor_tensor(mx[:, i, :], own, m, ALU.max), turn, "top")
                    step(v.tensor_tensor(dd[:, i, 0:H], m, mx[:, i, :], ALU.subtract), turn, "below_m")
                    step(v.tensor_tensor(dd[:, i, H:2 * H], own, mx[:, i, :], ALU.subtract), turn, "below_s")
                    step(v.tensor_scalar(has[:, i, :], z, 0.5, None, ALU.is_ge), turn, "has")
                    act_p.wait(dve, turn, "exp")
                    step(v.tensor_tensor(zz[:, i, :], z, ee[:, i, 0:H], ALU.mult), turn, "z_scaled")
                    step(v.tensor_tensor(z2[:, i, :], zz[:, i, :], ee[:, i, H:2 * H], ALU.add), turn, "z_sum")
                    step(v.reciprocal(zz[:, i, :], z2[:, i, :]), turn, "z_inv")
                    step(v.tensor_tensor(zz[:, i, :], zz[:, i, :], has[:, i, :], ALU.mult), turn, "z_has")
                    step(v.tensor_tensor(z, ee[:, i, 0:H], zz[:, i, :], ALU.mult), turn, "by_m")
                    step(v.tensor_tensor(m, ee[:, i, H:2 * H], zz[:, i, :], ALU.mult), turn, "by_s")
                    step(v.tensor_tensor(heads(agg[:, i, :]), heads(agg[:, i, :]), per_head(z), ALU.mult),
                         turn, "agg_scaled")
                    step(v.tensor_tensor(heads(v_in[:, i, :]), heads(v_in[:, i, :]), per_head(m), ALU.mult),
                         turn, "v_scaled")
                    step(v.tensor_tensor(agg[:, i, :], agg[:, i, :], v_in[:, i, :], ALU.add), turn, "merged")
                elif stage == "attend":
                    pe_p.wait(dve, turn, "attend")
                    step(v.tensor_tensor(hi, hi, prod, ALU.add), turn, "attended")
                    step(v.tensor_tensor(hi, hi, b_o[:, :], ALU.add), turn, "attended_b")
                elif stage == "norm_ff":
                    norm(turn, hi, "ff")
                elif stage == "ffn":
                    pe_p.wait(dve, turn, "ffn_2")
                    step(v.tensor_tensor(hi, hi, prod, ALU.add), turn, "ffn")
                    step(v.tensor_tensor(hi, hi, b_2[:, :], ALU.add), turn, "ffn_b")
                    if kind == "last":
                        landed(dve, s_x, turn)
                        step(v.tensor_tensor(tmp[:, i, :], hi, xi, ALU.add), turn, "x2")
                elif stage == "norm_out":
                    norm(turn, tmp[:, i, :], "out")
                elif stage == "gate":
                    step(v.tensor_tensor(agg[:, i, :], xn[:, i, :], w_r[:, :], ALU.mult), turn, "weighed")
                    step(v.tensor_reduce(gate[:, i, :], agg[:, i, :], AX.X, ALU.add), turn, "gate0")
                    step(v.tensor_tensor(gate[:, i, :], gate[:, i, :], b_r[:, :], ALU.add), turn, "gate")
                    step(v.tensor_copy(keep["gates"][:, bass.ds(number(turn), 1)], gate[:, i, :]), turn, "gate_kept")
                    step(v.tensor_tensor(qc[:, bass.ds(number(turn, QC), D)], tmp[:, i, :], xn[:, i, :], ALU.add),
                         turn, "base")
                elif stage == "ffn_out":
                    pe_p.wait(dve, turn, "out_2")
                    step(v.tensor_tensor(agg[:, i, :], prod, f_b2[:, :], ALU.add), turn, "y_b")
                    step(v.tensor_scalar(acc[:, 0:2, bass.ds(number(turn, P), P)],
                                         agg[:, i, :].rearrange("p (c n) -> p c n", c=2), gate[:, i, 0:1], None,
                                         ALU.mult), turn, "y")

            v.memset(x[:, :, :], 0.0).then_inc(s_zero, 1)
            dve.wait_ge(s_weights, 16 * len(loads))
            blocks_of(dve, do)

        @block.tensor
        def _(pe):
            t = nc.tensor

            def turn_rows(turn, rows, name):
                for half in range(2):
                    mm = t.transpose(pt[turn[0]][:, half * P:(half + 1) * P], rows[:, half * P:(half + 1) * P],
                                     ident[:, :])
                pe_p.tick(mm, turn, name)

            def project(turn, w, name):
                for half in range(2):
                    mm = t.matmul(pt[turn[0]][:, D:2 * D], xt[:, turn[0], half * P:(half + 1) * P], w[:, half, :],
                                  start=(half == 0), stop=(half == 1))
                pe_p.tick(mm, turn, name)

            def hidden(turn, w, name):
                i = turn[0]
                for c in range(FF // P):
                    for half in range(2):
                        mm = t.matmul(ph[i][:, c * P:(c + 1) * P], w[:, half, c * P:(c + 1) * P],
                                      xt[:, i, half * P:(half + 1) * P], start=(half == 0), stop=(half == 1))
                pe_p.tick(mm, turn, name)

            def output(turn, w, name, gelu):
                i = turn[0]
                for c in range(FF // P):
                    act_p.wait(pe, turn, f"{gelu}{c}")
                    mm = t.matmul(pt[i][:, D:2 * D], hid[:, i, c * P:(c + 1) * P], w[:, c, :],
                                  start=(c == 0), stop=(c == FF // P - 1))
                pe_p.tick(mm, turn, name)

            def do(turn, stage):
                i = turn[0]
                if stage in ("norm_in", "norm_q", "norm_ff", "norm_out"):
                    tag = stage[5:]
                    dve_p.wait(pe, turn, f"{tag}_normed")
                    turn_rows(turn, xn[:, i, :], f"{tag}_t")
                elif stage == "project_in":
                    act_p.wait(pe, turn, "in_x")
                    project(turn, w_in, "in_p")
                elif stage == "qkv":
                    act_p.wait(pe, turn, "q_x")
                    for at, n in ((0, 512), (512, D)):
                        for half in range(2):
                            mm = t.matmul(ph[i][:, at:at + n], xt[:, i, half * P:(half + 1) * P],
                                          w_qkv[:, half, at:at + n], start=(half == 0), stop=(half == 1))
                    pe_p.tick(mm, turn, "qkv")
                elif stage == "merge":
                    act_p.wait(pe, turn, "acc", beside=s_weights)
                    dve_p.wait_turn(pe, turn, beside=s_weights)
                    for half in range(2):
                        t.transpose(pt[i][:, half * P:(half + 1) * P], ab[:, i, half, :], ident[:, :])
                    pe_p.tick(t.transpose(pt[i][:, D:D + ZM], ab[0:ZM, i, 2, :], ident[0:ZM, 0:ZM]), turn, "acc_t")
                elif stage == "attend":
                    dve_p.wait(pe, turn, "merged")
                    turn_rows(turn, agg[:, i, :], "agg_t")
                    act_p.wait(pe, turn, "agg_x")
                    project(turn, w_o, "attend")
                elif stage == "ffn":
                    act_p.wait(pe, turn, "ff_x")
                    hidden(turn, w_1, "ffn_1")
                    output(turn, w_2, "ffn_2", "gelu")
                elif stage == "ffn_out":
                    act_p.wait(pe, turn, "out_x")
                    hidden(turn, f_1, "out_1")
                    output(turn, f_2, "out_2", "gelu_out")

            pe.wait_ge(s_weights, 16 * len(loads))
            blocks_of(pe, do)

        @block.scalar
        def _(act):
            s = nc.scalar

            def do(turn, stage):
                i = turn[0]
                if stage in ("norm_in", "norm_out", "attend"):
                    tag = {"norm_in": "in", "norm_out": "out", "attend": "agg"}[stage]
                    pe_p.wait(act, turn, f"{tag}_t")
                    act_p.tick(s.copy(xt[:, i, :], pt[i][:, 0:D]), turn, f"{tag}_x")
                elif stage in ("norm_q", "norm_ff"):
                    tag, g, b = ("q", g1, b1n) if stage == "norm_q" else ("ff", g2, b2n)
                    pe_p.wait(act, turn, f"{tag}_t")
                    for half in range(2):
                        cut = slice(half * P, (half + 1) * P)
                        act_p.tick(s.activation(xt[:, i, cut], pt[i][:, cut], ACT.Identity,
                                                bias=b[:, half:half + 1], scale=g[:, half:half + 1]),
                                   turn, f"{tag}_x" if half else f"{tag}_x0")
                elif stage == "merge":
                    pe_p.wait_turn(act, turn)
                    act_p.tick(s.copy(ab[:, i, :, :], acc[:, :, bass.ds(number(turn, P), P)]), turn, "acc")
                    dve_p.wait(act, turn, "below_s")
                    act_p.tick(s.activation(ee[:, i, :], dd[:, i, :], ACT.Exp, scale=SCALE), turn, "exp")
                elif stage in ("ffn", "ffn_out"):
                    pe_name, name, func, bias = (("ffn_1", "gelu", ACT.Gelu, b_1) if stage == "ffn" else
                                                 ("out_1", "gelu_out", ACT.Gelu_apprx_tanh, f_b1))
                    pe_p.wait(act, turn, pe_name)
                    for c in range(FF // P):
                        cut = slice(c * P, (c + 1) * P)
                        act_p.tick(s.activation(hid[:, i, cut], ph[i][:, cut], func, bias=bias[:, c:c + 1]),
                                   turn, f"{name}{c}")

            act.wait_ge(s_weights, 16 * len(loads))
            blocks_of(act, do)


def select_and_store(nc, dram, keep, out):
    with Phase(nc) as ctx:
        def sb(name, shape, dt=F32):
            return ctx.enter_context(nc.sbuf_tensor(f"final_{name}", shape, dt))

        def sem(name):
            return ctx.semaphore(f"final_{name}")

        acc, qc, gates = keep["acc"], keep["qc"], keep["gates"]
        node_i = sb("node_i", [P, BLOCKS], I32)
        valid = sb("valid", [P, BLOCKS])
        hide = sb("hide", [P, BLOCKS])
        u = sb("u", [P, BLOCKS])
        w = sb("w", [P, BLOCKS])
        cmp_ = sb("cmp", [P, BLOCKS])
        part = sb("part", [P, 1])
        ones = sb("ones", [P, P])
        before = sb("before", [P, P])
        sign = sb("sign", [P, 1])
        rank = sb("rank", [P, 1])
        cand = sb("cand", [P, 1], I32)
        theta = sb("theta", [P, 1], I32)
        bit = sb("bit", [P, 1], I32)
        take_f = sb("take_f", [P, 1])
        take_i = sb("take_i", [P, 1], I32)
        bound = sb("bound", [P, 1])
        above = sb("above", [P, BLOCKS])
        equal = sb("equal", [P, BLOCKS])
        zero = sb("zero", [P, BLOCKS])
        run = sb("run", [P, BLOCKS])
        sel = sb("sel", [P, BLOCKS])
        rows = sb("rows", [P, 7, D])
        rows2 = sb("rows2", [P, 7, D])
        total = ctx.enter_context(nc.psum_tensor("final_total", [P, 1], F32))
        cols = ctx.enter_context(nc.psum_tensor("final_cols", [P, BLOCKS], F32))
        prior = ctx.enter_context(nc.psum_tensor("final_prior", [P, BLOCKS], F32))

        s_iota = sem("iota")
        s_tri = sem("triangle")
        s_v = sem("dve")
        s_total = sem("total")
        s_prior = sem("prior")
        s_out = [sem(f"out{i}") for i in range(2)]
        count = {"n": 0, "at": {}}
        need = []
        SPAN = 7
        assert BLOCKS % SPAN == 0

        block = ctx.enter_context(nc.Block())

        @block.gpsimd
        def _(pool):
            g = nc.gpsimd
            g.iota(node_i[:, :], pattern=[[P, BLOCKS]], base=0, channel_multiplier=1).then_inc(s_iota, 1)
            g.memset(before[:, :], 1.0).then_inc(s_tri, 1)
            pool.wait_ge(s_tri, 1)
            g.affine_select(out=before[:, :], in_=before[:, :], compare_op=ALU.is_gt, fill=0.0,
                            base=0, pattern=[[1, P]], channel_multiplier=-1).then_inc(s_tri, 1)

        @block.vector
        def _(dve):
            v = nc.vector

            def link(ins, name=None):
                ins.then_inc(s_v, 1)
                count["n"] += 1
                if name:
                    count["at"][name] = count["n"]
                dve.wait_ge(s_v, count["n"])

            def count_of(in0, scalar, op):
                link(v.tensor_scalar(cmp_[:, :], in0, scalar, 0.0, op, ALU.add, accum_out=part[:, :]))
                need.append(count["n"])
                dve.wait_ge(s_total, len(need))

            link(v.memset(ones[:, :], 1.0))
            link(v.memset(zero[:, :], 1.0))
            link(v.memset(theta[:, :], 0))
            link(v.memset(bit[:, :], 1 << 30))
            dve.wait_ge(s_iota, 1)
            link(v.tensor_scalar(valid[:, :], node_i[:, :], float(N), None, ALU.is_lt))
            link(v.tensor_scalar(hide[:, :], valid[:, :], -1.0, 3e38, ALU.add, ALU.mult))
            link(v.tensor_tensor(u[:, :], gates[:, :], valid[:, :], ALU.mult))
            link(v.tensor_tensor(w[:, :], u[:, :], hide[:, :], ALU.add))
            count_of(w[:, :], 0.0, ALU.is_ge)
            link(v.tensor_scalar(take_f[:, :], total[:, :], float(TOPK), None, ALU.is_ge))
            link(v.tensor_scalar(sign[:, :], take_f[:, :], 2.0, -1.0, ALU.mult, ALU.add))
            link(v.tensor_scalar(rank[:, :], take_f[:, :], float(2 * TOPK - N - 1), float(N - TOPK + 1),
                                 ALU.mult, ALU.add))
            link(v.tensor_scalar(u[:, :], u[:, :], sign[:, 0:1], None, ALU.mult))
            link(v.tensor_tensor(u[:, :], u[:, :], hide[:, :], ALU.add))
            for _ in range(31):
                link(v.tensor_tensor(cand[:, :], theta[:, :], bit[:, :], ALU.bitwise_or))
                count_of(u[:, :], cand[:, :].bitcast(F32), ALU.is_ge)
                link(v.tensor_tensor(take_f[:, :], total[:, :], rank[:, :], ALU.is_ge))
                link(v.tensor_copy(take_i[:, :], take_f[:, :]))
                link(v.tensor_tensor(take_i[:, :], take_i[:, :], bit[:, :], ALU.mult))
                link(v.tensor_tensor(theta[:, :], theta[:, :], take_i[:, :], ALU.bitwise_or))
                link(v.tensor_single_scalar(bit[:, :], bit[:, :], 1, op=ALU.logical_shift_right))
            link(v.tensor_tensor(bound[:, :], theta[:, :].bitcast(F32), sign[:, :], ALU.mult))
            link(v.tensor_scalar(above[:, :], w[:, :], bound[:, 0:1], None, ALU.is_gt))
            link(v.tensor_scalar(equal[:, :], w[:, :], bound[:, 0:1], None, ALU.is_equal), "equal")
            count_of(w[:, :], bound[:, 0:1], ALU.is_gt)
            link(v.tensor_scalar(rank[:, :], total[:, :], -1.0, float(TOPK), ALU.mult, ALU.add))
            dve.wait_ge(s_prior, 1)
            link(v.tensor_tensor_scan(run[:, :], zero[:, :], cols[:, :], 0.0, ALU.mult, ALU.add))
            link(v.tensor_tensor(run[:, :], run[:, :], cols[:, :], ALU.subtract))
            link(v.tensor_tensor(run[:, :], run[:, :], prior[:, :], ALU.add))
            link(v.tensor_scalar(run[:, :], run[:, :], rank[:, 0:1], None, ALU.is_lt))
            link(v.tensor_tensor(equal[:, :], equal[:, :], run[:, :], ALU.mult))
            link(v.tensor_tensor(sel[:, :], above[:, :], equal[:, :], ALU.add))
            for b in range(BLOCKS):
                n = b // SPAN
                if b % SPAN == 0 and n >= 2:
                    dve.wait_ge(s_out[n % 2], 16 * (n // 2))
                o = (rows if n % 2 == 0 else rows2)[:, b % SPAN, :]
                v.scalar_tensor_tensor(out=o.rearrange("p (c n) -> p c n", c=2), in0=acc[:, 0:2, b * P:(b + 1) * P],
                                       scalar=sel[:, b:b + 1],
                                       in1=qc[:, b * QC:b * QC + D].rearrange("p (c n) -> p c n", c=2),
                                       op0=ALU.mult, op1=ALU.add).then_inc(s_v, 1)
                count["n"] += 1
                if b % SPAN == SPAN - 1:
                    count["at"][f"rows{n}"] = count["n"]

        at = count["at"]

        @block.tensor
        def _(pe):
            t = nc.tensor
            for i, n in enumerate(need):
                if i == len(need) - 1:
                    pe.wait_ge(s_tri, 2)
                    pe.wait_ge(s_v, at["equal"])
                    t.matmul(cols[:, :], ones[:, :], equal[:, :], start=True, stop=True)
                    t.matmul(prior[:, :], before[:, :], equal[:, :], start=True, stop=True).then_inc(s_prior, 1)
                pe.wait_ge(s_v, n)
                t.matmul(total[:, :], ones[:, :], part[:, :], start=True, stop=True).then_inc(s_total, 1)

        @block.sync
        def _(sp):
            for n in range(BLOCKS // SPAN):
                sp.wait_ge(s_v, at[f"rows{n}"])
                r = rows if n % 2 == 0 else rows2
                first = n * SPAN * P
                if n < BLOCKS // SPAN - 1:
                    sp.dma_start(out[first:first + SPAN * P, :].rearrange("(b p) d -> p b d", p=P), r[:, :, :])\
                        .then_inc(s_out[n % 2], 16)
                else:
                    whole = (SPAN - 1) * P
                    sp.dma_start(out[first:first + whole, :].rearrange("(b p) d -> p b d", p=P),
                                 r[:, 0:SPAN - 1, :]).then_inc(s_out[n % 2], 16)
                    sp.dma_start(out[first + whole:N, :], r[0:LAST, SPAN - 1, :]).then_inc(s_out[n % 2], 16)
            sp.wait_ge(s_out[0], 16 * 5)
            sp.wait_ge(s_out[1], 16 * 3)


def build(nc, a, out):
    with ExitStack() as ctx:
        def sb(name, shape, dt=F32):
            return ctx.enter_context(nc.sbuf_tensor(name, shape, dt))

        def dr(name, shape, dt=F32):
            return nc.dram_tensor(name, shape, dt).ap()

        keep = {"ident": sb("ident", [P, P]), "cols": sb("cols", [P, SELW]), "part": sb("part", [P, 1]),
                "ecol": sb("ecol", [P, P]), "self": sb("self", [P, BLOCKS * H]), "gates": sb("gates", [P, BLOCKS])}
        dram = {"src": dr("src_padded", (TILES * P,), I32), "dst": dr("dst_padded", (TILES * P,), I32),
                "ends": dr("step_ends", (SC * P * 2,)), "regs": dr("step_regs", (SC * P, 2), I32),
                "rel": dr("step_rel", (SC * P, P), BF16), "flags": dr("step_flags", (2, SC * P, P)),
                "idx": dr("step_src", (P, SC * P), I32), "col": dr("step_col", (P, SC * P)),
                "last": dr("step_last", (P, SC * P)), "eregs": dr("end_regs", (P, 2), I32),
                "h": dr("h", (BLOCKS * P, D)), "kv": dr("kv", (BLOCKS * P, KV))}
        constants(nc, keep)
        plan_steps(nc, a["src"], a["dst"], dram, keep)
        keep["qc"] = sb("qc", [P, BLOCKS * QC])
        keep["acc"] = sb("acc", [P, 3, (BLOCKS + 1) * P])
        clear_sums(nc, keep)
        node_pass(nc, "first", a, dram, keep)
        for layer in range(LAYERS):
            with nc.sbuf_tensor(f"ends{layer}", [P, 3, ENDS], F32) as ends:
                keep["ends"] = ends
                edge_pass(nc, layer, dram, keep)
                merge_ends(nc, layer, dram, keep)
            node_pass(nc, "middle" if layer < LAYERS - 1 else "last", a, dram, keep)
        select_and_store(nc, dram, keep, out)


def clear_sums(nc, keep):
    with nc.Block() as block:
        @block.vector
        def _(dve):
            nc.vector.memset(keep["acc"][:, :, :], 0.0)


_OUT = ((N, D), "float32")


def kernel(**inputs):
    import numpy as _np
    import concourse.bacc as _bacc
    from concourse.bass_utils import run_bass_kernel_spmd as _run

    nc = _bacc.Bacc("TRN2", target_bir_lowering=False, num_devices=1)
    arrays, args = {}, {}
    for name, value in inputs.items():
        a = _np.ascontiguousarray(value)
        arrays[f"in_{name}"] = a
        args[name] = nc.dram_tensor(f"in_{name}", a.shape, mybir.dt.from_np(a.dtype), kind="ExternalInput").ap()
    out = nc.dram_tensor("out_0", _OUT[0], F32, kind="ExternalOutput").ap()
    build(nc, args, out)
    r = _run(nc, [arrays], core_ids=[0])
    return r.results[0]["out_0"]
```

```python
from contextlib import ExitStack

import concourse.bass as bass
from concourse import mybir

ALU = mybir.AluOpType
ACT = mybir.ActivationFunctionType
AX = mybir.AxisListType
F32 = mybir.dt.float32
BF16 = mybir.dt.bfloat16
I32 = mybir.dt.int32

P = 128
N, D = 6250, 256
E = 100000
H, DH = 8, 32
FF = 1024
LAYERS = 2
EPS = 1e-5
SCALE = DH ** -0.5
BIG = 1e30
TOPK = N // 2 - 1

TILES = -(-E // P)
BLOCKS = -(-N // P)
LAST = N - (BLOCKS - 1) * P
G = 8
STEPS = -(-(TILES + BLOCKS - 1) // G) * G
GROUPS = STEPS // G
assert GROUPS % 4 == 0
SC = -(-STEPS // P)
ENDS = 2 * STEPS
ETILES = ENDS // P
assert ENDS % P == 0
MERGES = ETILES + BLOCKS - 1
KV = 2 * D
QC = D + 2 * H
SELW = P + 2
ZM = 40
PAD_DST = 50000


class Phase(ExitStack):

    def __init__(self, nc):
        super().__init__()
        self.nc, self.semaphores = nc, []

    def semaphore(self, name):
        self.semaphores.append(self.nc.alloc_semaphore(name=name))
        return self.semaphores[-1]

    def __exit__(self, *error):
        done = super().__exit__(*error)
        if error[0] is None:
            self.nc.clear_and_free_semaphores(self.semaphores)
            self.nc.all_engine_barrier()
        return done


class Progress:

    def __init__(self, nc, ctx, name, lanes):
        self.sems = [ctx.semaphore(f"{name}_{i}") for i in range(lanes)]
        self.base = [0] * lanes
        self.steps = ()

    def begin(self, steps):
        self.steps = tuple(steps)
        self.place = {s: i + 1 for i, s in enumerate(self.steps)}
        assert len(self.place) == len(self.steps)
        self.told = [0] * len(self.sems)

    def end(self, turns):
        for i, t in enumerate(turns):
            self.base[i] += t * len(self.steps)

    def at(self, turn, step):
        lane, k, c = turn
        value = self.base[lane] + c * len(self.steps) + self.place[step]
        return value if k is None else k * len(self.steps) + value

    def wait(self, eng, turn, step, beside=None):
        if beside is not None:
            wait_beside(eng, beside, self.sems[turn[0]], self.at(turn, step))
        else:
            eng.wait_ge(self.sems[turn[0]], self.at(turn, step))

    def last_of(self, *steps):
        return max(steps, key=lambda s: self.place[s])

    def wait_turn(self, eng, turn, beside=None):
        lane, k, c = turn
        value = self.base[lane] + c * len(self.steps)
        value = value if k is None else k * len(self.steps) + value
        if beside is not None:
            wait_beside(eng, beside, self.sems[lane], value)
        else:
            eng.wait_ge(self.sems[lane], value)

    def tick(self, ins, turn, step):
        lane = turn[0]
        assert self.steps[self.told[lane] % len(self.steps)] == step, (step, self.steps[self.told[lane] % len(self.steps)])
        self.told[lane] += 1
        ins.then_inc(self.sems[lane], 1)
        return ins


def wait_beside(eng, plain, sem, value):
    if not isinstance(value, int):
        value = eng.to_reg(value)
        eng.wait_ge(plain, 1)
    eng.wait_ge(sem, value)


def bc(ap, shape):
    return ap.broadcast_to(shape)


def plan_steps(nc, src, dst, dram, keep):
    with Phase(nc) as ctx:
        def sb(name, shape, dt=F32):
            return ctx.enter_context(nc.sbuf_tensor("plan_" + name, shape, dt))

        def ps(name, shape, dt=F32):
            return ctx.enter_context(nc.psum_tensor("plan_" + name, shape, dt))

        def sem(name):
            return ctx.semaphore("plan_" + name)

        padi = sb("padi", [1, 2, P], I32)
        frow_i = sb("frow_i", [1, TILES], I32)
        fblk_i = sb("fblk_i", [1, TILES], I32)
        trow_i = sb("trow_i", [1, TILES], I32)
        frow = sb("frow", [1, TILES])
        trow = sb("trow", [1, TILES])
        key = sb("key", [1, TILES])
        ones = sb("ones", [1, P])
        keyb = sb("keyb", [P, TILES])
        cmp_ = sb("cmp", [P, TILES])
        step_i = sb("step_i", [P, SC], I32)
        step = sb("step", [P, SC])
        tile_ = sb("tile", [P, SC])
        tile_i = sb("tile_i", [P, SC], I32)
        base = sb("base", [P, SC])
        blk = sb("blk", [P, SC])
        c = sb("c", [P, SC])
        d = sb("d", [P, SC])
        dne = sb("dne", [P, SC])
        regs_f = sb("regs_f", [P, SC, 2])
        regs_i = sb("regs_i", [P, SC, 2], I32)
        ends = sb("ends", [P, SC, 2])
        sg_i = sb("sg_i", [P, SC, P], I32)
        dg_i = sb("dg_i", [P, SC, P], I32)
        sg = sb("sg", [P, SC, P])
        dg = sb("dg", [P, SC, P])
        rel = sb("rel", [P, SC, P])
        rel16 = sb("rel16", [P, SC, P], BF16)
        far = sb("far", [P, SC, P])
        isc = sb("isc", [P, SC, P])
        isd = sb("isd", [P, SC, P])
        col = sb("col", [P, SC, P])
        diff = sb("diff", [P, SC, P])
        nf = sb("nf", [P, SC, P])
        nb = sb("nb", [P, SC, P])
        last = sb("last", [P, SC, P])
        tab_i = sb("tab_i", [P, SC * P], I32)
        tab_c = sb("tab_c", [P, SC * P])
        tab_l = sb("tab_l", [P, SC * P])
        pk = ps("pk", [P, 1024])
        pt = [ps(f"pt{i}", [P, 3, P]) for i in range(2)]

        efrow = sb("efrow", [1, ETILES])
        eblk = sb("eblk", [1, ETILES])
        etmp = sb("etmp", [1, ETILES], I32)
        ekey = sb("ekey", [1, ETILES])
        etrow_i = sb("etrow_i", [1, ETILES], I32)
        etrow = sb("etrow", [1, ETILES])
        ekeyb = sb("ekeyb", [P, ETILES])
        ecmp = sb("ecmp", [P, ETILES])
        etile = sb("etile", [P, 1])
        etile_i = sb("etile_i", [P, 1], I32)
        ebase = sb("ebase", [P, 1])
        eregs_f = sb("eregs_f", [P, 2])
        eregs_i = sb("eregs_i", [P, 2], I32)
        eg = sb("eg", [P, P])
        erel = sb("erel", [P, P])
        pe2 = ps("pe2", [P, ETILES])
        pe3 = ps("pe3", [P, P])

        s_pad = sem("pad")
        s_padded = sem("padded")
        s_first = sem("first")
        s_iota = sem("iota")
        s_v = sem("dve")
        s_key = sem("key_spread")
        s_gather = sem("gathered")
        s_turned = sem("turned")
        s_taken = sem("taken")
        s_store = sem("stored")
        s_ends = sem("ends_stored")
        s_efirst = sem("ends_first")
        s_ekey = sem("ends_key_spread")
        s_egather = sem("ends_gathered")
        s_eturn = sem("ends_turned")
        s_estore = sem("ends_tables_stored")
        count = {"n": 0, "at": {}}

        block = ctx.enter_context(nc.Block())

        @block.vector
        def _(dve):
            def link(ins, name=None):
                ins.then_inc(s_v, 1)
                count["n"] += 1
                if name:
                    count["at"][name] = count["n"]
                dve.wait_ge(s_v, count["n"])

            v = nc.vector
            v.memset(padi[:, 0, :], 0).then_inc(s_pad, 1)
            v.memset(padi[:, 1, :], PAD_DST).then_inc(s_pad, 1)
            link(v.memset(ones[:, :], 1.0))
            dve.wait_ge(s_iota, 3)
            link(v.tensor_copy(step[:, :], step_i[:, :]))
            link(v.tensor_copy(trow[:, :], trow_i[:, :]))
            link(v.tensor_copy(etrow[:, :], etrow_i[:, :]))
            dve.wait_ge(s_first, 16)
            link(v.tensor_single_scalar(fblk_i[:, :], frow_i[:, :], 7, op=ALU.arith_shift_right))
            link(v.tensor_copy(frow[:, :], fblk_i[:, :]))
            link(v.tensor_tensor(key[:, :], frow[:, :], trow[:, :], ALU.add), "key")
            dve.wait_ge(s_key, 1)
            link(v.tensor_copy(keyb[:, :], pk[:, 0:TILES]))
            for j in range(SC):
                link(v.tensor_scalar(cmp_[:, 1:TILES], keyb[:, 1:TILES], step[:, j:j + 1], 0.0,
                                     ALU.is_le, ALU.add, accum_out=tile_[:, j:j + 1]))
            link(v.tensor_copy(tile_i[:, :], tile_[:, :]), "tile")
            link(v.tensor_tensor(blk[:, :], step[:, :], tile_[:, :], ALU.subtract))
            link(v.tensor_scalar(base[:, :], blk[:, :], float(P), None, ALU.mult))
            link(v.tensor_scalar(regs_f[:, :, 1], blk[:, :], float(BLOCKS - 1), float(QC), ALU.min, ALU.mult))
            dve.wait_ge(s_gather, 16 * 2 * SC)
            link(v.tensor_copy(sg[:, :, :], sg_i[:, :, :]), "sg")
            link(v.tensor_copy(dg[:, :, :], dg_i[:, :, :]))
            link(v.tensor_tensor(c[:, :], base[:, :], dg[:, :, 0], ALU.max))
            link(v.tensor_scalar(d[:, :], base[:, :], float(P - 1), None, ALU.add))
            link(v.tensor_tensor(d[:, :], d[:, :], dg[:, :, P - 1], ALU.min))
            link(v.tensor_tensor(d[:, :], d[:, :], c[:, :], ALU.max))
            link(v.tensor_copy(ends[:, :, 0], c[:, :]))
            link(v.tensor_copy(ends[:, :, 1], d[:, :]), "ends")
            link(v.tensor_scalar(regs_f[:, :, 0], c[:, :], float((BLOCKS) * P), None, ALU.min))
            link(v.tensor_copy(regs_i[:, :, :], regs_f[:, :, :]), "regs")
            cb = bc(c[:, :].unsqueeze(2), [P, SC, P])
            db = bc(d[:, :].unsqueeze(2), [P, SC, P])
            bb = bc(base[:, :].unsqueeze(2), [P, SC, P])
            link(v.tensor_tensor(rel[:, :, :], dg[:, :, :], bb, ALU.subtract))
            link(v.tensor_scalar(rel16[:, :, :], rel[:, :, :], -1.0, 200.0, ALU.max, ALU.min), "rel")
            link(v.tensor_scalar(far[:, :, :], rel[:, :, :], float(P), 1e5, ALU.is_ge, ALU.mult))
            link(v.tensor_tensor(isc[:, :, :], dg[:, :, :], cb, ALU.is_equal))
            link(v.tensor_tensor(isd[:, :, :], dg[:, :, :], db, ALU.is_equal))
            link(v.tensor_tensor(diff[:, :, :], isd[:, :, :], isc[:, :, :], ALU.mult))
            link(v.tensor_tensor(isd[:, :, :], isd[:, :, :], diff[:, :, :], ALU.subtract))
            link(v.tensor_tensor(col[:, :, :], dg[:, :, :], cb, ALU.subtract))
            link(v.tensor_tensor(diff[:, :, :], isc[:, :, :], isd[:, :, :], ALU.add))
            link(v.tensor_scalar(diff[:, :, :], diff[:, :, :], -1.0, 1.0, ALU.mult, ALU.add))
            link(v.tensor_tensor(col[:, :, :], col[:, :, :], diff[:, :, :], ALU.mult))
            link(v.tensor_tensor(col[:, :, :], col[:, :, :], far[:, :, :], ALU.add))
            link(v.scalar_tensor_tensor(out=col[:, :, :], in0=isc[:, :, :], scalar=float(P), in1=col[:, :, :],
                                        op0=ALU.mult, op1=ALU.add))
            link(v.scalar_tensor_tensor(out=col[:, :, :], in0=isd[:, :, :], scalar=float(P + 1), in1=col[:, :, :],
                                        op0=ALU.mult, op1=ALU.add), "col")
            link(v.memset(last[:, :, P - 1:P], 1.0))
            link(v.tensor_tensor(last[:, :, 0:P - 1], dg[:, :, 0:P - 1], dg[:, :, 1:P], ALU.not_equal), "last")
            link(v.memset(nf[:, :, 0:1], 0.0))
            link(v.tensor_scalar(nf[:, :, 1:P], last[:, :, 0:P - 1], -BIG, None, ALU.mult))
            link(v.tensor_scalar(nb[:, :, :], last[:, :, :], -BIG, None, ALU.mult), "flags")
            for j in range(SC):
                dve.wait_ge(s_turned, j + 1)
                v.tensor_copy(tab_i[:, j * P:(j + 1) * P], pt[j % 2][:, 0, :]).then_inc(s_taken, 1)
                v.tensor_copy(tab_c[:, j * P:(j + 1) * P], pt[j % 2][:, 1, :]).then_inc(s_taken, 1)
                v.tensor_copy(tab_l[:, j * P:(j + 1) * P], pt[j % 2][:, 2, :]).then_inc(s_taken, 1)
            dve.wait_ge(s_efirst, 16)
            link(v.tensor_copy(etmp[:, :], efrow[:, :]))
            link(v.tensor_single_scalar(etmp[:, :], etmp[:, :], 7, op=ALU.arith_shift_right))
            link(v.tensor_copy(eblk[:, :], etmp[:, :]))
            link(v.tensor_tensor(ekey[:, :], eblk[:, :], etrow[:, :], ALU.add), "ekey")
            dve.wait_ge(s_ekey, 1)
            link(v.tensor_copy(ekeyb[:, :], pe2[:, :]))
            link(v.tensor_scalar(ecmp[:, 1:ETILES], ekeyb[:, 1:ETILES], step[:, 0:1], 0.0,
                                 ALU.is_le, ALU.add, accum_out=etile[:, :]))
            link(v.tensor_copy(etile_i[:, :], etile[:, :]), "etile")
            link(v.tensor_tensor(ebase[:, :], step[:, 0:1], etile[:, :], ALU.subtract))
            link(v.tensor_scalar(eregs_f[:, 0:1], etile[:, :], float(QC), None, ALU.mult))
            link(v.tensor_scalar(eregs_f[:, 1:2], ebase[:, :], float(BLOCKS - 1), float(QC), ALU.min, ALU.mult))
            link(v.tensor_copy(eregs_i[:, :], eregs_f[:, :]))
            link(v.tensor_scalar(ebase[:, :], ebase[:, :], float(P), None, ALU.mult))
            dve.wait_ge(s_egather, 16)
            link(v.tensor_scalar(erel[:, :], eg[:, :], ebase[:, 0:1], None, ALU.subtract), "erel")
            dve.wait_ge(s_eturn, 1)
            link(v.tensor_copy(keep["ecol"][:, :], pe3[:, :]))

        at = count["at"]

        @block.gpsimd
        def _(pool):
            g = nc.gpsimd
            g.iota(step_i[:, :], pattern=[[P, SC]], base=0, channel_multiplier=1).then_inc(s_iota, 1)
            g.iota(trow_i[:, :], pattern=[[1, TILES]], base=0, channel_multiplier=0).then_inc(s_iota, 1)
            g.iota(etrow_i[:, :], pattern=[[1, ETILES]], base=0, channel_multiplier=0).then_inc(s_iota, 1)
            pool.wait_ge(s_v, at["tile"])
            pool.wait_ge(s_padded, 64)
            for j in range(SC):
                for table, rows in ((dram["src"], sg_i), (dram["dst"], dg_i)):
                    g.indirect_dma_start(rows[:, j, :], None, table.rearrange("(t p) -> t p", p=P),
                                         bass.IndirectOffsetOnAxis(ap=tile_i[:, j:j + 1], axis=0))\
                        .then_inc(s_gather, 16)
            pool.wait_ge(s_v, at["etile"])
            pool.wait_ge(s_ends, 16)
            g.indirect_dma_start(eg[:, :], None, dram["ends"][0:ENDS].rearrange("(t p) -> t p", p=P),
                                 bass.IndirectOffsetOnAxis(ap=etile_i[:, 0:1], axis=0)).then_inc(s_egather, 16)

        @block.sync
        def _(sp):
            sp.dma_start(dram["src"][0:E], src[:]).then_inc(s_padded, 16)
            sp.dma_start(dram["dst"][0:E], dst[:]).then_inc(s_padded, 16)
            sp.wait_ge(s_pad, 2)
            pad = TILES * P - E
            sp.dma_start(dram["src"][E:].rearrange("(o p) -> o p", o=1), padi[:, 0, 0:pad]).then_inc(s_padded, 16)
            sp.dma_start(dram["dst"][E:].rearrange("(o p) -> o p", o=1), padi[:, 1, 0:pad]).then_inc(s_padded, 16)
            sp.wait_ge(s_padded, 64)
            with nc.allow_non_contiguous_dma(reason="first dst of every tile"):
                sp.dma_start(frow_i[:, :], dram["dst"].rearrange("(o t p) -> o t p", o=1, p=P)[:, :, 0])\
                    .then_inc(s_first, 16)
            sp.wait_ge(s_v, at["ends"])
            sp.dma_start(dram["ends"].rearrange("(c p w) -> p c w", p=P, w=2), ends[:, :, :]).then_inc(s_ends, 16)
            sp.wait_ge(s_v, at["regs"])
            sp.dma_start(dram["regs"].rearrange("(c p) w -> p c w", p=P), regs_i[:, :, :]).then_inc(s_store, 16)
            sp.wait_ge(s_v, at["rel"])
            sp.dma_start(dram["rel"].rearrange("(c p) e -> p c e", p=P), rel16[:, :, :]).then_inc(s_store, 16)
            sp.wait_ge(s_ends, 16)
            with nc.allow_non_contiguous_dma(reason="first end of every tile of ends"):
                sp.dma_start(efrow[:, :], dram["ends"][0:ENDS].rearrange("(o t p) -> o t p", o=1, p=P)[:, :, 0])\
                    .then_inc(s_efirst, 16)
            sp.wait_ge(s_v, at["flags"])
            sp.dma_start(dram["flags"][0].rearrange("(c p) e -> p c e", p=P), nf[:, :, :]).then_inc(s_store, 16)
            sp.dma_start(dram["flags"][1].rearrange("(c p) e -> p c e", p=P), nb[:, :, :]).then_inc(s_store, 16)
            sp.wait_ge(s_taken, 3 * SC)
            sp.dma_start(dram["idx"], tab_i[:, :]).then_inc(s_store, 16)
            sp.dma_start(dram["col"], tab_c[:, :]).then_inc(s_store, 16)
            sp.dma_start(dram["last"], tab_l[:, :]).then_inc(s_store, 16)
            sp.wait_ge(s_v, at["erel"])
            sp.dma_start(dram["eregs"], eregs_i[:, :]).then_inc(s_estore, 16)
            sp.wait_ge(s_store, 16 * 7)
            sp.wait_ge(s_estore, 16)

        @block.tensor
        def _(pe):
            t = nc.tensor
            pe.wait_ge(s_v, at["key"])
            t.matmul(pk[:, 0:512], ones[:, :], key[:, 0:512], start=True, stop=True)
            t.matmul(pk[:, 512:TILES], ones[:, :], key[:, 512:TILES], start=True, stop=True).then_inc(s_key, 1)
            pe.wait_ge(s_v, at["last"])
            for j in range(SC):
                if j >= 2:
                    pe.wait_ge(s_taken, 3 * (j - 1))
                t.transpose(pt[j % 2][:, 0, :], sg[:, j, :], keep["ident"][:, :])
                t.transpose(pt[j % 2][:, 1, :], col[:, j, :], keep["ident"][:, :])
                t.transpose(pt[j % 2][:, 2, :], last[:, j, :], keep["ident"][:, :]).then_inc(s_turned, 1)
            pe.wait_ge(s_v, at["ekey"])
            t.matmul(pe2[:, :], ones[:, :], ekey[:, :], start=True, stop=True).then_inc(s_ekey, 1)
            pe.wait_ge(s_v, at["erel"])
            t.transpose(pe3[:, :], erel[:, :], keep["ident"][:, :]).then_inc(s_eturn, 1)
def constants(nc, keep):
    with Phase(nc) as ctx:
        s_a = ctx.semaphore("const_a")
        s_b = ctx.semaphore("const_b")
        iota_i = ctx.enter_context(nc.sbuf_tensor("iota_i", [P, SELW], I32))
        part_i = ctx.enter_context(nc.sbuf_tensor("part_i", [P, 1], I32))
        block = ctx.enter_context(nc.Block())

        @block.gpsimd
        def _(pool):
            g = nc.gpsimd
            g.memset(keep["ident"][:, :], 0.0).then_inc(s_a, 1)
            g.iota(iota_i[:, :], pattern=[[1, SELW]], base=0, channel_multiplier=0).then_inc(s_b, 1)
            g.iota(part_i[:, :], pattern=[[0, 1]], base=0, channel_multiplier=1).then_inc(s_b, 1)
            pool.wait_ge(s_a, 1)
            g.affine_select(out=keep["ident"][:, :], in_=keep["ident"][:, :], compare_op=ALU.not_equal, fill=1.0,
                            base=0, pattern=[[-1, P]], channel_multiplier=1).then_inc(s_a, 1)

        @block.vector
        def _(dve):
            dve.wait_ge(s_b, 2)
            nc.vector.tensor_copy(keep["cols"][:, :], iota_i[:, :])
            nc.vector.tensor_copy(keep["part"][:, :], part_i[:, :])


WEAVE = (("product", 0), ("up", 0), ("score", 0), ("top", 0), ("product", 1), ("weigh", 0), ("score", 1),
         ("product", 2), ("tail", 0), ("score", 2), ("product", 3), ("tail", 1), ("score", 3),
         ("turn", 0), ("tail", 2), ("tail", 3))
PAIRS = G // 2
QBUFS = 2
ABUFS = 4


def later(turn, n):
    lane, k, c = turn
    g = 4 * c + lane + n
    return (g % 4, k, g // 4)


def is_first(turn):
    return turn[1] is None and turn[0] == 0 and turn[2] == 0


def edge_pass(nc, layer, dram, keep):
    with Phase(nc) as ctx:
        def sb(name, shape, dt=F32):
            return ctx.enter_context(nc.sbuf_tensor(f"edge{layer}_{name}", shape, dt))

        def ps(name, shape, dt=F32):
            return ctx.enter_context(nc.psum_tensor(f"edge{layer}_{name}", shape, dt))

        def sem(name):
            return ctx.semaphore(f"edge{layer}_{name}")

        acc, ends, qc = keep["acc"], keep["ends"], keep["qc"]
        kv = sb("kv", [P, 2, G, KV])
        idx = sb("idx", [P, 4, G], I32)
        rel = sb("rel", [P, 2, G * P], BF16)
        flags = sb("flags", [G * H, 2, 2, P])
        col = sb("col", [P, 4, G])
        last = sb("last", [P, 4, G])
        regs = sb("regs", [1, 4, 2 * G], I32)
        spread = sb("spread", [P, 2, G * P])
        sel = sb("sel", [P, G, SELW])
        score = sb("score", [P, 2, G * H])
        up = sb("up", [G * H, P])
        top = sb("top", [G * H, P])
        below = sb("below", [P, G * H])
        wm = sb("wm", [P, 2, G, ZM])
        psq = [ps(f"q{i}", [P, 2, D]) for i in range(QBUFS)]
        turned = ps("turned", [P, 512])
        pst = turned[0:G * H, 0:P]
        psm = turned[:, P:P + G * H]
        psa = [ps(f"sums{i}", [P, 512]) for i in range(ABUFS)]

        s_clear = sem("cleared")
        s_idx = [sem(f"idx{i}") for i in range(4)]
        s_rel = [sem(f"rel{i}") for i in range(2)]
        s_flags = [sem(f"flags{i}") for i in range(2)]
        s_table = [sem(f"table{i}") for i in range(4)]
        s_row = [[sem(f"rows{i}_{j}") for j in range(G)] for i in range(2)]

        dve_p = Progress(nc, ctx, f"edge{layer}_dve", 4)
        act_p = Progress(nc, ctx, f"edge{layer}_act", 4)
        pe_p = Progress(nc, ctx, f"edge{layer}_pe", 4)
        dve_steps = ["spread"]
        for m in range(PAIRS):
            dve_steps += [f"product{m}", f"score{m}"]
        dve_steps += ["up", "top", "below", "maxima"]
        for m in range(PAIRS):
            dve_steps += [f"sel{m}", f"value{m}"]
        dve_p.begin(dve_steps)
        pe_p.begin([f"q{m}" for m in range(PAIRS)] + ["score_t", "max_t"] + [f"sums{j}" for j in range(G)])
        act_p.begin(["weights"] + [f"{n}{j}" for j in range(G) for n in ("acc", "ends")])

        def fill(sems, depth, turn):
            lane, k, c = turn
            if depth == 4:
                return sems[lane], (16 * (c + 1) if k is None else k * 16 + 16 * (c + 1))
            n = 2 * c + lane // 2
            return sems[lane % 2], (16 * (n + 1) if k is None else k * 32 + 16 * (n + 1))

        def groups_of(eng, body):
            body((0, None, 0), first=True)
            body((1, None, 0))
            body((2, None, 0))
            body((3, None, 0))
            with eng.Fori(0, GROUPS // 4 - 2) as k:
                for r in range(4):
                    body((r, k, 1))
            for g in range(GROUPS - 4, GROUPS):
                body((g % 4, None, g // 4), end=g == GROUPS - 1)

        def number(turn, scale):
            lane, k, c = turn
            g = (4 * c + lane) * scale
            return g if k is None else k * (4 * scale) + g

        block = ctx.enter_context(nc.Block())

        @block.sync
        def _(sp):
            def load_idx(turn, wait=True):
                if wait:
                    before = later(turn, -4)
                    for j in range(G):
                        wait_beside(sp, s_clear, *fill([s_row[0][j], s_row[1][j]], 2, before))
                sp.dma_start(idx[:, turn[0], :], dram["idx"][:, bass.ds(number(turn, G), G)])\
                    .then_inc(s_idx[turn[0]], 16)

            def load_rel(turn, wait=True):
                if wait:
                    dve_p.wait(sp, later(turn, -2), "spread", beside=s_clear)
                sp.dma_start(rel[:, turn[0] % 2, :],
                             dram["rel"].rearrange("s e -> (s e)")[bass.ds(number(turn, G * P), G * P)]
                             .partition_broadcast(P)).then_inc(fill(s_rel, 2, turn)[0], 16)

            def load_rest(turn, wait=True):
                if wait:
                    before = later(turn, -4)
                    dve_p.wait(sp, before, f"value{PAIRS - 1}", beside=s_clear)
                    act_p.wait(sp, before, f"ends{G - 1}", beside=s_clear)
                slot = turn[0]
                s = s_table[slot]
                for tab, name in ((col, "col"), (last, "last")):
                    sp.dma_start(tab[:, slot, :], dram[name][:, bass.ds(number(turn, G), G)]).then_inc(s, 16)
                sp.dma_start(regs[:, slot, :],
                             dram["regs"].rearrange("(o s) w -> o (s w)", o=1)[:, bass.ds(number(turn, 2 * G), 2 * G)])\
                    .then_inc(s, 16)

            def load_flags(turn, wait=True):
                if wait:
                    dve_p.wait(sp, later(turn, -2), "top", beside=s_clear)
                s = fill(s_flags, 2, turn)[0]
                for w in range(2):
                    rows = dram["flags"][w][bass.ds(number(turn, G), G), :].unsqueeze(1)
                    sp.dma_start(flags[:, turn[0] % 2, w, :], bc(rows, [G, H, P])).then_inc(s, 16)

            for g in range(4):
                turn = (g, None, 0)
                load_idx(turn, False)
                if g < 2:
                    load_rel(turn, False)
                    load_flags(turn, False)
                load_rest(turn, False)
            load_rel((2, None, 0))

            def one(turn, g=None):
                if g is None or g + 4 < GROUPS:
                    load_idx(later(turn, 4))
                if g is None or g + 3 < GROUPS:
                    load_rel(later(turn, 3))
                if g is None or 2 <= g and g + 2 < GROUPS:
                    load_rest(later(turn, 2))
                if g is None or 1 <= g and g + 1 < GROUPS:
                    load_flags(later(turn, 1))

            for g in range(4):
                one((g, None, 0), g)
            with sp.Fori(0, GROUPS // 4 - 2) as k:
                for r in range(4):
                    one((r, k, 1))
            for g in range(GROUPS - 4, GROUPS):
                one((g % 4, None, g // 4), g)

        @block.gpsimd
        def _(pool):
            def rows(turn, first=False):
                lane = turn[0] % 2
                for j in range(G):
                    if j == 0:
                        wait_beside(pool, s_clear, *fill(s_idx, 4, turn))
                    if not first:
                        pe_p.wait(pool, later(turn, -2), f"sums{j}", beside=s_clear)
                    nc.gpsimd.indirect_dma_start(
                        kv[:, lane, j, :], None, dram["kv"],
                        bass.IndirectOffsetOnAxis(ap=idx[:, turn[0], j:j + 1], axis=0)).then_inc(s_row[lane][j], 16)

            rows((0, None, 0), True)
            rows((1, None, 0), True)
            rows((2, None, 0))
            rows((3, None, 0))
            with pool.Fori(0, GROUPS // 4 - 1) as k:
                for r in range(4):
                    rows((r, k, 1))

        @block.vector
        def _(dve):
            v = nc.vector
            v.memset(wm[:, :, :, :], 0.0).then_inc(s_clear, 1)
            for i in range(ABUFS):
                v.memset(psa[i][:, :], 0.0).then_inc(s_clear, 1)
            dve.wait_ge(s_clear, 1 + ABUFS)

            def spread_of(turn, first=False):
                if not first:
                    pe_p.wait(dve, later(turn, -2), f"q{PAIRS - 1}")
                dve.wait_ge(*fill(s_rel, 2, turn))
                dve_p.tick(v.tensor_scalar(spread[:, turn[0] % 2, :], rel[:, turn[0] % 2, :],
                                           keep["part"][:, 0:1], None, ALU.is_equal), turn, "spread")

            def table(turn, times=3):
                lane, k, c = turn
                value = 48 * (c + 1)
                dve.wait_ge(s_table[lane], value if k is None else k * 48 + value)

            def body(turn, first=False, end=False):
                before = None if first else later(turn, -1)
                for what, m in WEAVE:
                    lane = turn[0] % 2
                    if what == "product":
                        pe_p.wait(dve, turn, f"q{m}")
                        for j in (2 * m, 2 * m + 1):
                            dve.wait_ge(*fill([s_row[0][j], s_row[1][j]], 2, turn))
                        k_rows = kv[:, lane, 2 * m:2 * m + 2, 0:D]
                        dve_p.tick(v.tensor_tensor(k_rows, k_rows, psq[m % QBUFS][:, :, :], ALU.mult),
                                   turn, f"product{m}")
                        if m == 0 and not end:
                            spread_of(later(turn, 1), first)
                    elif what == "score":
                        k_rows = kv[:, lane, 2 * m:2 * m + 2, 0:D]
                        dve_p.wait(dve, turn, f"product{m}")
                        dve_p.tick(v.tensor_reduce(
                            score[:, lane, 2 * m * H:2 * (m + 1) * H].rearrange("p (j h) -> p j h", h=H),
                            k_rows.rearrange("p j (h d) -> p j h d", h=H), AX.X, ALU.add), turn, f"score{m}")
                    elif what == "up":
                        if not first:
                            scan_up(before)
                    elif not first:
                        rest(before, what, m, is_first(before))

            def scan_up(turn):
                lane, k, c = turn
                n = 2 * c + lane // 2
                value = 32 * (n + 1)
                dve.wait_ge(s_flags[lane % 2], value if k is None else k * 64 + value)
                pe_p.wait(dve, turn, "score_t")
                dve_p.tick(v.tensor_tensor_scan(up[:, :], flags[:, lane % 2, 0, :], pst, -BIG, ALU.add, ALU.max),
                           turn, "up")

            def rest(turn, what, m, earliest=False):
                lane = turn[0] % 2
                if what == "top":
                    dve_p.wait(dve, turn, "up")
                    dve_p.tick(v.tensor_tensor_scan(top[:, ::-1], flags[:, lane, 1, ::-1], up[:, ::-1], -BIG,
                                                    ALU.add, ALU.max), turn, "top")
                elif what == "weigh":
                    table(turn)
                    pe_p.wait(dve, turn, "max_t")
                    dve_p.tick(v.tensor_tensor(below[:, :], score[:, lane, :], psm, ALU.subtract), turn, "below")
                    dve_p.tick(v.tensor_tensor(wm[:, lane, :, 32:ZM], psm.rearrange("p (j h) -> p j h", h=H),
                                               bc(last[:, turn[0], :].unsqueeze(2), [P, G, H]), ALU.mult),
                               turn, "maxima")
                elif what == "tail":
                    if not earliest:
                        pe_p.wait(dve, later(turn, -1), f"sums{2 * m + 1}")
                    at = 2 * m
                    dve_p.tick(v.tensor_tensor(sel[:, at:at + 2, :], bc(keep["cols"][:, :].unsqueeze(1), [P, 2, SELW]),
                                               bc(col[:, turn[0], 2 * m:2 * m + 2].unsqueeze(2), [P, 2, SELW]),
                                               ALU.is_equal), turn, f"sel{m}")
                    if m == 0:
                        act_p.wait(dve, turn, "weights")
                    values = kv[:, lane, 2 * m:2 * m + 2, D:KV].rearrange("p j (h d) -> p j h d", h=H)
                    dve_p.tick(v.tensor_tensor(values, values,
                                               bc(wm[:, lane, 2 * m:2 * m + 2, 0:H].unsqueeze(3), [P, 2, H, DH]),
                                               ALU.mult), turn, f"value{m}")

            spread_of((0, None, 0), True)
            groups_of(dve, body)
            scan_up((3, None, GROUPS // 4 - 1))
            for what, m in WEAVE:
                rest((3, None, GROUPS // 4 - 1), what, m)

        @block.tensor
        def _(pe):
            t = nc.tensor
            pe.wait_ge(s_clear, 1 + ABUFS)

            def q_at(turn, m):
                if m == 0:
                    lane, k, c = turn
                    value = 48 * (c + 1)
                    wait_beside(pe, s_clear, s_table[lane], value if k is None else k * 48 + value)
                at = [pe.value_load(regs[0:1, turn[0], 2 * j + 1:2 * j + 2], min_val=0, max_val=(BLOCKS - 1) * QC)
                      for j in (2 * m, 2 * m + 1)]
                return at

            def spread_q(turn, m, at, first=False):
                if m == 0:
                    dve_p.wait(pe, turn, "spread")
                if m >= QBUFS:
                    dve_p.wait(pe, turn, f"product{m - QBUFS}")
                elif not first:
                    dve_p.wait(pe, later(turn, -1), f"product{m + PAIRS - QBUFS}")
                for j in (2 * m, 2 * m + 1):
                    mm = t.matmul(psq[m % QBUFS][:, j % 2, :], spread[:, turn[0] % 2, j * P:(j + 1) * P],
                                  qc[:, bass.ds(at[j % 2], D)], start=True, stop=True)
                pe_p.tick(mm, turn, f"q{m}")

            def body(turn, first=False, end=False):
                for what, m in WEAVE:
                    owner, pair = (turn, m + QBUFS) if m + QBUFS < PAIRS else (later(turn, 1), m + QBUFS - PAIRS)
                    ahead, next_pair = (turn, pair + 1) if owner == turn and pair + 1 < PAIRS else \
                        (later(turn, 1), (pair + 1) % PAIRS)
                    if what == "product" and not (end and owner != turn):
                        if m == 0:
                            at = q_at(owner, pair)
                        spread_q(owner, pair, at)
                    elif what == "score" and m + 1 < PAIRS and not (end and ahead != turn):
                        at = q_at(ahead, next_pair)
                    elif what == "turn":
                        dve_p.wait(pe, turn, f"score{PAIRS - 1}", beside=s_clear)
                        pe_p.tick(t.transpose(pst, score[:, turn[0] % 2, :], keep["ident"][:, :]), turn, "score_t")
                    elif not first:
                        rest(later(turn, -1), what, m, is_first(later(turn, -1)))

            def rest(turn, what, m, earliest=False):
                lane = turn[0] % 2
                if what == "top":
                    dve_p.wait(pe, turn, "top", beside=s_clear)
                    pe_p.tick(t.transpose(psm, top[:, :], keep["ident"][0:G * H, 0:G * H]), turn, "max_t")
                elif what == "tail":
                    dve_p.wait(pe, turn, f"value{m}")
                    for j in (2 * m, 2 * m + 1):
                        if j >= ABUFS:
                            act_p.wait(pe, turn, f"ends{j - ABUFS}")
                        elif not earliest:
                            act_p.wait(pe, later(turn, -1), f"ends{j + G - ABUFS}")
                        one_hot = sel[:, j, :]
                        out = psa[j % ABUFS]
                        for half in range(2):
                            t.matmul(out[:, half * SELW:(half + 1) * SELW],
                                     kv[:, lane, j, D + half * P:D + (half + 1) * P], one_hot, start=True, stop=True)
                        pe_p.tick(t.matmul(out[0:ZM, 2 * SELW:3 * SELW], wm[:, lane, j, :], one_hot,
                                           start=True, stop=True), turn, f"sums{j}")

            for m in range(QBUFS):
                spread_q((0, None, 0), m, q_at((0, None, 0), m), True)
            groups_of(pe, body)
            for what, m in WEAVE:
                if what != "up":
                    rest((3, None, GROUPS // 4 - 1), what, m)

        @block.scalar
        def _(act):
            s = nc.scalar
            act.wait_ge(s_clear, 1 + ABUFS)

            def columns_at(turn, m):
                return [act.value_load(regs[0:1, turn[0], 2 * j:2 * j + 1], min_val=0, max_val=BLOCKS * P)
                        for j in (2 * m, 2 * m + 1)]

            def rest(turn, what, m, places, earliest=False):
                lane = turn[0] % 2
                if what == "top":
                    lane_, k, c = turn
                    value = 48 * (c + 1)
                    wait_beside(act, s_clear, s_table[lane_], value if k is None else k * 48 + value)
                    places[0] = columns_at(turn, 0)
                elif what == "weigh":
                    dve_p.wait(act, turn, "below")
                    act_p.tick(s.activation(wm[:, lane, :, 0:H], below[:, :].rearrange("p (j h) -> p j h", h=H),
                                            ACT.Exp, scale=SCALE), turn, "weights")
                elif what == "tail":
                    if m + 1 < PAIRS:
                        places[m + 1] = columns_at(turn, m + 1)
                    for j in (2 * m, 2 * m + 1):
                        at = places[m][j % 2]
                        if j > 0 or not earliest:
                            act_p.wait(act, turn if j else later(turn, -1), f"acc{(j - 1) % G}")
                        pe_p.wait(act, turn, f"sums{j}")
                        out = psa[j % ABUFS][:, 0:3 * SELW].rearrange("p (c n) -> p c n", c=3)
                        act_p.tick(s.copy(acc[:, :, bass.ds(at, P)], out[:, :, 0:P]), turn, f"acc{j}")
                        act_p.tick(s.copy(ends[:, :, bass.ds(number(turn, 2 * G) + 2 * j, 2)], out[:, :, P:SELW]),
                                   turn, f"ends{j}")

            def body(turn, first=False, end=False):
                if not first:
                    places = {}
                    for what, m in WEAVE:
                        rest(later(turn, -1), what, m, places, is_first(later(turn, -1)))

            groups_of(act, body)
            places = {}
            for what, m in WEAVE:
                rest((3, None, GROUPS // 4 - 1), what, m, places)


def merge_ends(nc, layer, dram, keep):
    with Phase(nc) as ctx:
        def sb(name, shape, dt=F32):
            return ctx.enter_context(nc.sbuf_tensor(f"merge{layer}_{name}", shape, dt))

        def ps(name, shape, dt=F32):
            return ctx.enter_context(nc.psum_tensor(f"merge{layer}_{name}", shape, dt))

        def sem(name):
            return ctx.semaphore(f"merge{layer}_{name}")

        ends, qc, ident = keep["ends"], keep["qc"], keep["ident"]
        node = sb("node", [H, ENDS])
        opens = sb("opens", [H, ENDS])
        closes = sb("closes", [H, ENDS])
        m = sb("m", [H, ENDS])
        up = sb("up", [H, ENDS])
        closing = sb("closing", [H, ENDS])
        part = sb("part", [P, 2, QC - D + H])
        rows = sb("rows", [P, ETILES * QC])
        one_hot = sb("one_hot", [P, 2, P])
        eregs = sb("eregs", [1, P, 2], I32)
        pt = [ps(f"t{i}", [P, 512]) for i in range(2)]
        pm = [ps(f"m{i}", [P, QC]) for i in range(2)]

        s_node = sem("node")
        s_regs = sem("regs")
        s_v = sem("dve")
        s_weight = sem("weight")
        s_turned = sem("turned")
        dve_p = Progress(nc, ctx, f"merge{layer}_dvep", 2)
        pe_p = Progress(nc, ctx, f"merge{layer}_pep", 2)
        dve_p.begin(["one_hot", "added"])
        pe_p.begin(["summed"])
        count = {"n": 0, "at": {}}
        block = ctx.enter_context(nc.Block())

        def pairs_of(eng, body):
            for turn in ((0, None, 0), (1, None, 0), (0, None, 1)):
                body(turn)
            with eng.Fori(1, MERGES // 2) as k:
                body((1, k, 0))
                body((0, k, 1))

        def number(turn):
            lane, k, c = turn
            return 2 * c + lane if k is None else k * 2 + (2 * c + lane)

        assert MERGES % 2 == 1

        @block.sync
        def _(sp):
            sp.dma_start(node[:, :], dram["ends"][0:ENDS].partition_broadcast(H)).then_inc(s_node, 16)
            sp.dma_start(eregs[:, :, :], dram["eregs"].rearrange("(o p) w -> o p w", o=1)).then_inc(s_regs, 16)

        @block.vector
        def _(dve):
            v = nc.vector

            def link(ins, name=None):
                ins.then_inc(s_v, 1)
                count["n"] += 1
                if name:
                    count["at"][name] = count["n"]
                dve.wait_ge(s_v, count["n"])

            link(v.memset(qc[:, :], 0.0))
            link(v.tensor_copy(m[:, :], ends[32:32 + H, 2, :]))
            link(v.memset(opens[:, 0:1], 0.0))
            link(v.memset(closes[:, ENDS - 1:ENDS], 0.0))
            dve.wait_ge(s_node, 16)
            link(v.tensor_tensor(opens[:, 1:ENDS], node[:, 1:ENDS], node[:, 0:ENDS - 1], ALU.not_equal))
            link(v.tensor_copy(closing[:, 0:ENDS - 1], opens[:, 1:ENDS]))
            link(v.memset(closing[:, ENDS - 1:ENDS], 1.0))
            link(v.tensor_scalar(opens[:, 1:ENDS], opens[:, 1:ENDS], -BIG, None, ALU.mult))
            link(v.tensor_copy(closes[:, 0:ENDS - 1], opens[:, 1:ENDS]))
            link(v.tensor_scalar(up[:, :], ends[0:H, 2, :], 0.5, -BIG, ALU.is_lt, ALU.mult))
            link(v.tensor_tensor(m[:, :], m[:, :], up[:, :], ALU.add))
            link(v.tensor_tensor_scan(up[:, :], opens[:, :], m[:, :], -BIG, ALU.add, ALU.max))
            link(v.tensor_tensor_scan(opens[:, ::-1], closes[:, ::-1], up[:, ::-1], -BIG, ALU.add, ALU.max))
            link(v.tensor_tensor(m[:, :], m[:, :], opens[:, :], ALU.subtract), "below")
            link(v.tensor_tensor(closing[:, :], closing[:, :], opens[:, :], ALU.mult), "closing")
            dve.wait_ge(s_weight, 1)
            for u in range(ETILES):
                dve.wait_ge(s_turned, u + 1)
                out = rows[:, u * QC:(u + 1) * QC]
                t = pt[u % 2]
                link(v.tensor_copy(part[:, u % 2, :], t[:, D:D + 3 * H]))
                weight = bc(part[:, u % 2, 2 * H:3 * H].unsqueeze(2), [P, H, DH])
                v.tensor_tensor(out[:, 0:D].rearrange("p (h d) -> p h d", h=H),
                                t[:, 0:D].rearrange("p (h d) -> p h d", h=H), weight, ALU.mult).then_inc(s_v, 1)
                v.tensor_tensor(out[:, D:D + H], part[:, u % 2, 0:H], part[:, u % 2, 2 * H:3 * H], ALU.mult)\
                    .then_inc(s_v, 1)
                count["n"] += 2
                link(v.tensor_copy(out[:, D + H:QC], part[:, u % 2, H:2 * H]), f"row{u}")

            def body(turn):
                lane = turn[0]
                pe_p.wait_turn(dve, turn)
                dve_p.tick(v.tensor_scalar(one_hot[:, lane, :], keep["cols"][:, 0:P],
                                           keep["ecol"][:, bass.ds(number(turn), 1)], None, ALU.is_equal),
                           turn, "one_hot")
                at = dve.value_load(eregs[0:1, bass.ds(number(turn), 1), 1:2], min_val=0, max_val=(BLOCKS - 1) * QC)
                pe_p.wait(dve, turn, "summed")
                place = qc[:, bass.ds(at, QC)]
                if lane or turn[2]:
                    dve_p.wait(dve, (0, turn[1], turn[2]) if lane else (1, turn[1], turn[2] - 1), "added")
                dve_p.tick(v.tensor_tensor(place, place, pm[lane][:, :], ALU.add), turn, "added")

            dve.wait_ge(s_regs, 16)
            pairs_of(dve, body)

        at = count["at"]

        @block.scalar
        def _(act):
            act.wait_ge(s_v, at["below"])
            nc.scalar.activation(up[:, :], m[:, :], ACT.Exp, scale=SCALE).then_inc(s_weight, 1)

        @block.tensor
        def _(pe):
            t = nc.tensor
            pe.wait_ge(s_weight, 1)
            pe.wait_ge(s_v, at["closing"])
            for u in range(ETILES):
                if u >= 2:
                    pe.wait_ge(s_v, at[f"row{u - 2}"])
                cut = slice(u * P, (u + 1) * P)
                t.transpose(pt[u % 2][:, 0:P], ends[:, 0, cut], ident[:, :])
                t.transpose(pt[u % 2][:, P:D], ends[:, 1, cut], ident[:, :])
                for i, row in enumerate((ends[0:H, 2, cut], closing[:, cut], up[:, cut])):
                    mm = t.transpose(pt[u % 2][:, D + i * H:D + (i + 1) * H], row, ident[0:H, 0:H])
                mm.then_inc(s_turned, 1)
            pe.wait_ge(s_v, at[f"row{ETILES - 1}"])
            pe.wait_ge(s_regs, 16)

            def body(turn):
                lane = turn[0]
                at_ = pe.value_load(eregs[0:1, bass.ds(number(turn), 1), 0:1], min_val=0, max_val=(ETILES - 1) * QC)
                dve_p.wait(pe, turn, "one_hot")
                pe_p.tick(t.matmul(pm[lane][:, :], one_hot[:, lane, :], rows[:, bass.ds(at_, QC)],
                                   start=True, stop=True), turn, "summed")

            pairs_of(pe, body)


RSQRT_GUESS = 0x5F3759DF
NEWTON = 3
BANK = 4
WEAVES = {
    "first": (("old", "norm_q"), ("old", "qkv"), ("new", "norm_in"), ("old", "qkv_out"), ("new", "project_in")),
    "middle": (("new", "sums_in"), ("old", "ffn_2"), ("new", "merge"), ("old", "ffn_out"), ("new", "turn_agg"),
               ("new", "attend"), ("old", "norm_q"), ("new", "attended"), ("old", "qkv"), ("new", "norm_ff"),
               ("new", "ffn_1"), ("old", "qkv_out")),
    "last": (("new", "sums_in"), ("old", "ffn_2"), ("new", "merge"), ("old", "ffn_out"), ("new", "turn_agg"),
             ("new", "attend"), ("old", "norm_out"), ("new", "attended"), ("old", "out_1"), ("new", "norm_ff"),
             ("old", "gate"), ("old", "out_2"), ("old", "y_out"), ("new", "ffn_1")),
}


def node_pass(nc, kind, a, dram, keep):
    weave = WEAVES[kind]
    stages = [stage for part in ("new", "old") for which, stage in weave if which == part]
    layer = 0 if kind != "last" else 1
    nxt = 0 if kind == "first" else 1
    with Phase(nc) as ctx:
        def sb(name, shape, dt=F32):
            return ctx.enter_context(nc.sbuf_tensor(f"{kind}_{name}", shape, dt))

        def ps(name, shape, dt=F32):
            return ctx.enter_context(nc.psum_tensor(f"{kind}_{name}", shape, dt))

        def sem(name):
            return ctx.semaphore(f"{kind}_{name}")

        acc, qc, ident, self_ = keep["acc"], keep["qc"], keep["ident"], keep["self"]
        x = sb("x", [P, 2, D])
        h = sb("h", [P, 2, D])
        xn = sb("xn", [P, 2, D])
        xt = sb("xt", [P, 2, D])
        st = sb("st", [P, 2, 6])
        mv = sb("mv", [P, 2, 2])
        var = sb("var", [P, 2, 1])
        minus_half = sb("minus_half", [P, 2, 1])
        half_bits = sb("half_bits", [P, 2, 1], I32)
        yy = sb("yy", [P, 2, 1])
        rs = sb("rs", [P, 2, 1])
        tmp = sb("tmp", [P, 2, D])
        pt = [ps(f"pt{i}", [P, 512]) for i in range(2)]
        ph = [ps(f"ph{i}", [P, 1024]) for i in range(2)]
        loads = []

        def col_of(name, vec):
            n = vec.shape[0] // P
            t = sb(name, [P, n])
            loads.append((t[:, :], vec.rearrange("(c p) -> p c", p=P)))
            return t

        def row_of(name, vec, into=None):
            n = vec.shape[0]
            t = sb(name, [P, n]) if into is None else into
            loads.append((t[:, 0:n] if into is None else into, vec.partition_broadcast(P)))
            return t

        def mat_of(name, mat, into=None):
            c = mat.shape[0] // P
            t = sb(name, [P, c, mat.shape[1]])[:, :, :] if into is None else into
            loads.append((t, mat.rearrange("(c p) n -> p c n", p=P)))
            return t

        if kind == "first":
            w_in = mat_of("w_in", a["L0_gnn_w_in"])
            b_in = row_of("b_in", a["L0_gnn_b_in"])
        if kind != "last":
            w_qkv = sb("w_qkv", [P, 2, 3 * D])
            b_qkv = sb("b_qkv", [P, 3 * D])
            for i, n in enumerate("qkv"):
                mat_of("", a[f"L0_gnn_w{n}"][nxt], w_qkv[:, :, i * D:(i + 1) * D])
                row_of("", a[f"L0_gnn_b{n}"][nxt], b_qkv[:, i * D:(i + 1) * D])
            g1 = col_of("g1", a["L0_gnn_ln1_g"][nxt])
            b1n = col_of("b1n", a["L0_gnn_ln1_b"][nxt])
            kv_out = sb("kv_out", [P, 2, KV])
        if kind != "first":
            w_o = mat_of("w_o", a["L0_gnn_wo"][layer])
            b_o = row_of("b_o", a["L0_gnn_bo"][layer])
            w_1 = mat_of("w_1", a["L0_gnn_w1"][layer])
            b_1 = col_of("b_1", a["L0_gnn_b1"][layer])
            w_2 = mat_of("w_2", a["L0_gnn_w2"][layer])
            b_2 = row_of("b_2", a["L0_gnn_b2"][layer])
            g2 = col_of("g2", a["L0_gnn_ln2_g"][layer])
            b2n = col_of("b2n", a["L0_gnn_ln2_b"][layer])
            h_in = sb("h_in", [P, 2, D])
            v_in = sb("v_in", [P, 2, D])
            ab = sb("ab", [P, 2, 3, P])
            agg = sb("agg", [P, 2, D])
            zm = sb("zm", [P, 2, 2 * H])
            mx = sb("mx", [P, 2, H])
            dd = sb("dd", [P, 2, 2 * H])
            ee = sb("ee", [P, 2, 2 * H])
            eh = sb("eh", [P, 2, 2 * H])
            zz = sb("zz", [P, 2, H])
            z2 = sb("z2", [P, 2, H])
            has = sb("has", [P, 2, H])
            hid = sb("hid", [P, 2, FF])
        if kind == "last":
            f_1 = mat_of("f_1", a["L0_ffn_w1"])
            f_b1 = col_of("f_b1", a["L0_ffn_b1"])
            f_2 = mat_of("f_2", a["L0_ffn_w2"])
            f_b2 = row_of("f_b2", a["L0_ffn_b2"])
            w_r = row_of("w_r", a["L0_ffn_wr"].rearrange("d o -> (d o)"))
            b_r = row_of("b_r", a["L0_ffn_br"])
            gate = sb("gate", [P, 2, 1])

        s_weights = sem("weights")
        s_zero = sem("zero")
        s_x = [sem(f"x{i}") for i in range(2)]
        s_h = [sem(f"h{i}") for i in range(2)]
        s_v = [sem(f"v{i}") for i in range(2)]
        s_hout = [sem(f"h_out{i}") for i in range(2)]
        s_kvout = [sem(f"kv_out{i}") for i in range(2)]

        def norm_steps(tag):
            return [f"{tag}_{s}" for s in
                    ["stats", "moments", "var", "minus_half", "bits", "guess"] +
                    [f"{x}{n}" for n in range(NEWTON) for x in ("square", "newton")] + ["normed"]]

        dve_steps = {
            "norm_in": norm_steps("in"), "project_in": ["h"], "norm_q": norm_steps("q"),
            "qkv_out": ["kv", "q", "qk", "self"],
            "sums_in": ["h_b", "agg", "zm", "top", "has", "below_m", "below_s"],
            "merge": ["z_scaled", "e_has", "z_sum", "z_inv", "by", "agg_scaled", "v_scaled", "merged"],
            "attended": ["attended"],
            "norm_ff": norm_steps("ff") + ["h_b2"] + (["h_x"] if kind == "last" else []),
            "ffn_out": ["ffn"], "norm_out": norm_steps("out"),
            "gate": ["weighed", "base", "gate0", "gate", "gate_kept"], "y_out": ["y_b", "y"],
        }
        pe_steps = {
            "norm_in": ["in_t"], "project_in": ["in_p"], "norm_q": ["q_t"], "qkv": ["qkv"],
            "sums_in": ["acc_t"], "turn_agg": ["agg_t"], "attend": ["attend"], "norm_ff": ["ff_t"],
            "ffn_1": ["ffn_1_0", "ffn_1_1"], "ffn_2": ["ffn_2"],
            "norm_out": ["out_t"], "out_1": ["out_1_0", "out_1_1"], "out_2": ["out_2"],
        }
        act_steps = {
            "norm_in": ["in_x"], "norm_q": ["q_x0", "q_x"],
            "sums_in": ["acc", "exp"], "turn_agg": ["agg_x"], "norm_ff": ["ff_x0", "ff_x"],
            "ffn_1": [f"gelu{i}" for i in range(FF // P)], "norm_out": ["out_x"],
            "out_1": [f"gelu_out{i}" for i in range(FF // P)],
        }
        progress = {}
        for name, steps in (("dve", dve_steps), ("pe", pe_steps), ("act", act_steps)):
            progress[name] = Progress(nc, ctx, f"{kind}_{name}", 2)
            progress[name].begin([s for stage in stages for s in steps.get(stage, ())])
        dve_p, pe_p, act_p = progress["dve"], progress["pe"], progress["act"]

        def later(turn, n):
            lane, k, c = turn
            b = 2 * c + lane + n
            return (b % 2, k, b // 2)

        def woven(do, new, old):
            for which, stage in weave:
                turn = new if which == "new" else old
                if turn is not None:
                    do(turn, stage)

        def blocks_of(eng, do):
            woven(do, (0, None, 0), None)
            for b in range(1, 4):
                woven(do, later((0, None, 0), b), later((0, None, 0), b - 1))
            with eng.Fori(2, BLOCKS // 2) as k:
                for lane in range(2):
                    woven(do, (lane, k, 0), later((lane, k, 0), -1))
            final = (0, None, BLOCKS // 2)
            woven(do, final, later(final, -1))
            woven(do, None, final)

        assert BLOCKS % 2 == 1

        def number(turn, scale=1):
            lane, k, c = turn
            b = (2 * c + lane) * scale
            return b if k is None else k * (2 * scale) + b

        def landed(eng, sems, turn, beside=None):
            lane, k, c = turn
            value = 16 * (c + 1) if k is None else k * 16 + 16 * (c + 1)
            if beside is None:
                eng.wait_ge(sems[lane], value)
            else:
                wait_beside(eng, beside, sems[lane], value)

        def stored_before(eng, sems, turn):
            lane, k, c = turn
            if k is not None or c > 0:
                eng.wait_ge(sems[lane], 16 * c if k is None else k * 16 + 16 * c)

        block = ctx.enter_context(nc.Block())

        @block.sync
        def _(sp):
            def load(turn, first=False, rows=P):
                lane = turn[0]
                before = later(turn, -2)
                at = bass.ds(number(turn, P), rows)
                full = bass.ds(number(turn, P), P)
                if kind != "middle":
                    if not first:
                        dve_p.wait(sp, before, "in_normed" if kind == "first" else "h_x", beside=s_zero)
                    sp.dma_start(x[0:rows, lane, :], a["x"][at, :]).then_inc(s_x[lane], 16)
                if kind != "first":
                    if not first:
                        dve_p.wait(sp, before, "merged", beside=s_zero)
                    sp.dma_start(h_in[:, lane, :], dram["h"][full, :]).then_inc(s_h[lane], 16)
                    sp.dma_start(v_in[:, lane, :], dram["kv"][full, D:KV]).then_inc(s_v[lane], 16)

            def store(turn):
                lane = turn[0]
                at = bass.ds(number(turn, P), P)
                if kind == "last":
                    return
                dve_p.wait(sp, turn, "h" if kind == "first" else "ffn", beside=s_zero)
                sp.dma_start(dram["h"][at, :], h[:, lane, :]).then_inc(s_hout[lane], 16)
                dve_p.wait(sp, turn, "kv", beside=s_zero)
                sp.dma_start(dram["kv"][at, :], kv_out[:, lane, :]).then_inc(s_kvout[lane], 16)

            def one(turn, b=None):
                if b is None or b + 1 < BLOCKS:
                    load(later(turn, 1), first=b == 0, rows=LAST if b == BLOCKS - 2 else P)
                if b is None or b > 0:
                    store(later(turn, -1))

            sp.wait_ge(s_zero, 1)
            load((0, None, 0), first=True)
            for b in range(4):
                one(later((0, None, 0), b), b)
            with sp.Fori(2, BLOCKS // 2 - 1) as k:
                for lane in range(2):
                    one((lane, k, 0))
            for b in range(BLOCKS - 3, BLOCKS + 1):
                one(later((0, None, 0), b), b)
            if kind != "last":
                for s in (s_hout, s_kvout):
                    landed(sp, s, (0, None, BLOCKS // 2))
                    landed(sp, s, (1, None, BLOCKS // 2 - 1))

        @block.gpsimd
        def _(pool):
            with nc.allow_non_contiguous_dma(reason="biases and gains as columns"):
                for tile_, source in loads:
                    pool.dma_start(tile_, source).then_inc(s_weights, 16)

        @block.vector
        def _(dve):
            v = nc.vector

            def step(ins, turn, name):
                dve_p.tick(ins, turn, name)
                dve_p.wait(dve, turn, name)

            def norm(turn, rows, tag):
                i = turn[0]
                dve_p.tick(v.bn_stats(out=st[:, i, :], in_=rows), turn, f"{tag}_stats")
                dve_p.wait(dve, turn, f"{tag}_stats", beside=s_weights)
                step(v.bn_aggr(out=mv[:, i, :], in_=st[:, i, :]), turn, f"{tag}_moments")
                dve_p.tick(v.tensor_scalar(var[:, i, :], mv[:, i, 1:2], EPS, None, ALU.add), turn, f"{tag}_var")
                step(v.tensor_scalar(minus_half[:, i, :], mv[:, i, 1:2], EPS, -0.5, ALU.add, ALU.mult),
                     turn, f"{tag}_minus_half")
                step(v.tensor_single_scalar(half_bits[:, i, :], var[:, i, :].bitcast(I32), 1,
                                            op=ALU.logical_shift_right), turn, f"{tag}_bits")
                step(v.tensor_scalar(rs[:, i, :].bitcast(I32), half_bits[:, i, :], -1.0, float(RSQRT_GUESS),
                                     ALU.mult, ALU.add), turn, f"{tag}_guess")
                for n in range(NEWTON):
                    step(v.scalar_tensor_tensor(out=yy[:, i, :], in0=rs[:, i, :], scalar=minus_half[:, i, 0:1],
                                                in1=rs[:, i, :], op0=ALU.mult, op1=ALU.mult),
                         turn, f"{tag}_square{n}")
                    step(v.scalar_tensor_tensor(out=rs[:, i, :], in0=yy[:, i, :], scalar=1.5, in1=rs[:, i, :],
                                                op0=ALU.add, op1=ALU.mult), turn, f"{tag}_newton{n}")
                step(v.tensor_scalar(xn[:, i, :], rows, mv[:, i, 0:1], rs[:, i, 0:1], ALU.subtract, ALU.mult),
                     turn, f"{tag}_normed")

            def heads(ap):
                return ap.rearrange("p (h d) -> p h d", h=H)

            def per_head(ap):
                return bc(ap.unsqueeze(2), [P, H, DH])

            def do(turn, stage):
                i = turn[0]
                xi, hi, prod = x[:, i, :], h[:, i, :], pt[i][:, D:2 * D]
                if stage == "norm_in":
                    landed(dve, s_x, turn)
                    norm(turn, xi, "in")
                elif stage == "project_in":
                    stored_before(dve, s_hout, turn)
                    pe_p.wait(dve, turn, "in_p")
                    step(v.tensor_tensor(hi, prod, b_in[:, :], ALU.add), turn, "h")
                elif stage == "norm_q":
                    norm(turn, hi, "q")
                elif stage == "qkv_out":
                    pe_p.wait(dve, turn, "qkv")
                    stored_before(dve, s_kvout, turn)
                    q = qc[:, bass.ds(number(turn, QC), D)]
                    dve_p.tick(v.tensor_tensor(kv_out[:, i, :], ph[i][:, D:3 * D], b_qkv[:, D:3 * D], ALU.add),
                               turn, "kv")
                    step(v.tensor_tensor(q, ph[i][:, 0:D], b_qkv[:, 0:D], ALU.add), turn, "q")
                    dve_p.tick(v.tensor_tensor(tmp[:, i, :], q, kv_out[:, i, 0:D], ALU.mult), turn, "qk")
                    dve_p.wait(dve, turn, "qk", beside=s_weights)
                    step(v.tensor_reduce(self_[:, bass.ds(number(turn, H), H)], heads(tmp[:, i, :]), AX.X, ALU.add),
                         turn, "self")
                elif stage == "sums_in":
                    landed(dve, s_h, turn)
                    if kind == "middle":
                        stored_before(dve, s_hout, turn)
                    dve_p.tick(v.tensor_tensor(hi, h_in[:, i, :], b_o[:, :], ALU.add), turn, "h_b")
                    pe_p.wait(dve, turn, "acc_t")
                    z, m = zm[:, i, 0:H], zm[:, i, H:2 * H]
                    own = self_[:, bass.ds(number(turn, H), H)]
                    at = number(turn, QC)
                    dve_p.tick(v.tensor_tensor(agg[:, i, :], pt[i][:, 0:D], qc[:, bass.ds(at, D)], ALU.add),
                               turn, "agg")
                    step(v.tensor_tensor(zm[:, i, :].rearrange("p (c h) -> p c h", c=2),
                                         pt[i][:, D:D + 64].rearrange("p (c n) -> p c n", c=2)[:, :, 0:H],
                                         qc[:, bass.ds(at + D, 2 * H)].rearrange("p (c h) -> p c h", c=2), ALU.add),
                         turn, "zm")
                    dve_p.tick(v.tensor_tensor(mx[:, i, :], own, m, ALU.max), turn, "top")
                    step(v.tensor_scalar(has[:, i, :], z, 0.5, None, ALU.is_ge), turn, "has")
                    dve_p.tick(v.tensor_tensor(dd[:, i, 0:H], m, mx[:, i, :], ALU.subtract), turn, "below_m")
                    dve_p.tick(v.tensor_tensor(dd[:, i, H:2 * H], own, mx[:, i, :], ALU.subtract), turn, "below_s")
                elif stage == "merge":
                    def both(ap):
                        return ap.rearrange("p (c h) -> p c h", c=2)

                    z, m = zm[:, i, 0:H], zm[:, i, H:2 * H]
                    act_p.wait(dve, turn, "exp")
                    dve_p.tick(v.tensor_tensor(zz[:, i, :], z, ee[:, i, 0:H], ALU.mult), turn, "z_scaled")
                    step(v.tensor_tensor(both(eh[:, i, :]), both(ee[:, i, :]), bc(has[:, i, :].unsqueeze(1), [P, 2, H]),
                                         ALU.mult), turn, "e_has")
                    step(v.tensor_tensor(z2[:, i, :], zz[:, i, :], ee[:, i, H:2 * H], ALU.add), turn, "z_sum")
                    step(v.reciprocal(zz[:, i, :], z2[:, i, :]), turn, "z_inv")
                    step(v.tensor_tensor(both(zm[:, i, :]), both(eh[:, i, :]), bc(zz[:, i, :].unsqueeze(1), [P, 2, H]),
                                         ALU.mult), turn, "by")
                    landed(dve, s_v, turn)
                    dve_p.tick(v.tensor_tensor(heads(agg[:, i, :]), heads(agg[:, i, :]), per_head(z), ALU.mult),
                               turn, "agg_scaled")
                    step(v.tensor_tensor(heads(v_in[:, i, :]), heads(v_in[:, i, :]), per_head(m), ALU.mult),
                         turn, "v_scaled")
                    step(v.tensor_tensor(agg[:, i, :], agg[:, i, :], v_in[:, i, :], ALU.add), turn, "merged")
                elif stage == "attended":
                    pe_p.wait(dve, turn, "attend")
                    step(v.tensor_tensor(hi, hi, prod, ALU.add), turn, "attended")
                elif stage == "norm_ff":
                    norm(turn, hi, "ff")
                    step(v.tensor_tensor(hi, hi, b_2[:, :], ALU.add), turn, "h_b2")
                    if kind == "last":
                        landed(dve, s_x, turn)
                        dve_p.tick(v.tensor_tensor(hi, hi, xi, ALU.add), turn, "h_x")
                elif stage == "ffn_out":
                    pe_p.wait(dve, turn, "ffn_2")
                    if kind == "last":
                        dve_p.wait(dve, turn, "h_x")
                        step(v.tensor_tensor(tmp[:, i, :], hi, prod, ALU.add), turn, "ffn")
                    else:
                        step(v.tensor_tensor(hi, hi, prod, ALU.add), turn, "ffn")
                elif stage == "norm_out":
                    norm(turn, tmp[:, i, :], "out")
                elif stage == "gate":
                    dve_p.tick(v.tensor_tensor(agg[:, i, :], xn[:, i, :], w_r[:, :], ALU.mult), turn, "weighed")
                    dve_p.tick(v.tensor_tensor(qc[:, bass.ds(number(turn, QC), D)], tmp[:, i, :], xn[:, i, :],
                                               ALU.add), turn, "base")
                    dve_p.wait(dve, turn, "weighed")
                    step(v.tensor_reduce(gate[:, i, :], agg[:, i, :], AX.X, ALU.add), turn, "gate0")
                    step(v.tensor_tensor(gate[:, i, :], gate[:, i, :], b_r[:, :], ALU.add), turn, "gate")
                    dve_p.tick(v.tensor_copy(keep["gates"][:, bass.ds(number(turn), 1)], gate[:, i, :]),
                               turn, "gate_kept")
                elif stage == "y_out":
                    pe_p.wait(dve, turn, "out_2")
                    step(v.tensor_tensor(agg[:, i, :], prod, f_b2[:, :], ALU.add), turn, "y_b")
                    step(v.tensor_scalar(acc[:, 0:2, bass.ds(number(turn, P), P)],
                                         agg[:, i, :].rearrange("p (c n) -> p c n", c=2), gate[:, i, 0:1], None,
                                         ALU.mult), turn, "y")

            v.memset(x[:, :, :], 0.0).then_inc(s_zero, 1)
            dve.wait_ge(s_weights, 16 * len(loads))
            blocks_of(dve, do)

        @block.tensor
        def _(pe):
            t = nc.tensor

            def turn_rows(turn, rows, name):
                for half in range(2):
                    mm = t.transpose(pt[turn[0]][:, half * P:(half + 1) * P], rows[:, half * P:(half + 1) * P],
                                     ident[:, :])
                pe_p.tick(mm, turn, name)

            def project(turn, w, name):
                for half in range(2):
                    mm = t.matmul(pt[turn[0]][:, D:2 * D], xt[:, turn[0], half * P:(half + 1) * P], w[:, half, :],
                                  start=(half == 0), stop=(half == 1))
                pe_p.tick(mm, turn, name)

            def hidden(turn, w, name):
                i = turn[0]
                for c in range(FF // P):
                    for half in range(2):
                        mm = t.matmul(ph[i][:, c * P:(c + 1) * P], w[:, half, c * P:(c + 1) * P],
                                      xt[:, i, half * P:(half + 1) * P], start=(half == 0), stop=(half == 1))
                    if c % BANK == BANK - 1:
                        pe_p.tick(mm, turn, f"{name}_{c // BANK}")

            def output(turn, w, name, gelu):
                i = turn[0]
                for c in range(FF // P):
                    act_p.wait(pe, turn, f"{gelu}{c}")
                    mm = t.matmul(pt[i][:, D:2 * D], hid[:, i, c * P:(c + 1) * P], w[:, c, :],
                                  start=(c == 0), stop=(c == FF // P - 1))
                pe_p.tick(mm, turn, name)

            def do(turn, stage):
                i = turn[0]
                if stage in ("norm_in", "norm_q", "norm_ff", "norm_out"):
                    tag = stage[5:]
                    dve_p.wait(pe, turn, f"{tag}_normed")
                    turn_rows(turn, xn[:, i, :], f"{tag}_t")
                elif stage == "project_in":
                    act_p.wait(pe, turn, "in_x")
                    project(turn, w_in, "in_p")
                elif stage == "qkv":
                    act_p.wait(pe, turn, "q_x")
                    for at, n in ((0, 512), (512, D)):
                        for half in range(2):
                            mm = t.matmul(ph[i][:, at:at + n], xt[:, i, half * P:(half + 1) * P],
                                          w_qkv[:, half, at:at + n], start=(half == 0), stop=(half == 1))
                    pe_p.tick(mm, turn, "qkv")
                elif stage == "sums_in":
                    act_p.wait(pe, turn, "acc", beside=s_weights)
                    dve_p.wait_turn(pe, turn, beside=s_weights)
                    for half in range(2):
                        t.transpose(pt[i][:, half * P:(half + 1) * P], ab[:, i, half, :], ident[:, :])
                    pe_p.tick(t.transpose(pt[i][:, D:D + ZM], ab[0:ZM, i, 2, :], ident[0:ZM, 0:ZM]), turn, "acc_t")
                elif stage == "turn_agg":
                    dve_p.wait(pe, turn, "merged")
                    turn_rows(turn, agg[:, i, :], "agg_t")
                elif stage == "attend":
                    act_p.wait(pe, turn, "agg_x")
                    project(turn, w_o, "attend")
                elif stage == "ffn_1":
                    act_p.wait(pe, turn, "ff_x")
                    hidden(turn, w_1, "ffn_1")
                elif stage == "ffn_2":
                    output(turn, w_2, "ffn_2", "gelu")
                elif stage == "out_1":
                    act_p.wait(pe, turn, "out_x")
                    hidden(turn, f_1, "out_1")
                elif stage == "out_2":
                    output(turn, f_2, "out_2", "gelu_out")

            pe.wait_ge(s_weights, 16 * len(loads))
            blocks_of(pe, do)

        @block.scalar
        def _(act):
            s = nc.scalar

            def do(turn, stage):
                i = turn[0]
                if stage in ("norm_in", "norm_out", "turn_agg"):
                    tag = {"norm_in": "in", "norm_out": "out", "turn_agg": "agg"}[stage]
                    pe_p.wait(act, turn, f"{tag}_t")
                    act_p.tick(s.copy(xt[:, i, :], pt[i][:, 0:D]), turn, f"{tag}_x")
                elif stage in ("norm_q", "norm_ff"):
                    tag, g, b = ("q", g1, b1n) if stage == "norm_q" else ("ff", g2, b2n)
                    pe_p.wait(act, turn, f"{tag}_t")
                    for half in range(2):
                        cut = slice(half * P, (half + 1) * P)
                        act_p.tick(s.activation(xt[:, i, cut], pt[i][:, cut], ACT.Identity,
                                                bias=b[:, half:half + 1], scale=g[:, half:half + 1]),
                                   turn, f"{tag}_x" if half else f"{tag}_x0")
                elif stage == "sums_in":
                    pe_p.wait_turn(act, turn)
                    act_p.tick(s.copy(ab[:, i, :, :], acc[:, :, bass.ds(number(turn, P), P)]), turn, "acc")
                    dve_p.wait(act, turn, "below_s")
                    act_p.tick(s.activation(ee[:, i, :], dd[:, i, :], ACT.Exp, scale=SCALE), turn, "exp")
                elif stage in ("ffn_1", "out_1"):
                    name, func, bias = (("gelu", ACT.Gelu, b_1) if stage == "ffn_1" else
                                        ("gelu_out", ACT.Gelu_apprx_tanh, f_b1))
                    for c in range(FF // P):
                        if c % BANK == 0:
                            pe_p.wait(act, turn, f"{stage}_{c // BANK}")
                        cut = slice(c * P, (c + 1) * P)
                        act_p.tick(s.activation(hid[:, i, cut], ph[i][:, cut], func, bias=bias[:, c:c + 1]),
                                   turn, f"{name}{c}")

            act.wait_ge(s_weights, 16 * len(loads))
            blocks_of(act, do)


def select_and_store(nc, dram, keep, out):
    with Phase(nc) as ctx:
        def sb(name, shape, dt=F32):
            return ctx.enter_context(nc.sbuf_tensor(f"final_{name}", shape, dt))

        def sem(name):
            return ctx.semaphore(f"final_{name}")

        acc, qc, gates = keep["acc"], keep["qc"], keep["gates"]
        node_i = sb("node_i", [P, BLOCKS], I32)
        valid = sb("valid", [P, BLOCKS])
        hide = sb("hide", [P, BLOCKS])
        u = sb("u", [P, BLOCKS])
        w = sb("w", [P, BLOCKS])
        cmp_ = sb("cmp", [P, BLOCKS])
        part = sb("part", [P, 1])
        ones = sb("ones", [P, P])
        before = sb("before", [P, P])
        sign = sb("sign", [P, 1])
        rank = sb("rank", [P, 1])
        cand = sb("cand", [P, 1], I32)
        theta = sb("theta", [P, 1], I32)
        bit = sb("bit", [P, 1], I32)
        take_f = sb("take_f", [P, 1])
        take_i = sb("take_i", [P, 1], I32)
        bound = sb("bound", [P, 1])
        above = sb("above", [P, BLOCKS])
        equal = sb("equal", [P, BLOCKS])
        zero = sb("zero", [P, BLOCKS])
        run = sb("run", [P, BLOCKS])
        sel = sb("sel", [P, BLOCKS])
        rows = sb("rows", [P, 7, D])
        rows2 = sb("rows2", [P, 7, D])
        total = ctx.enter_context(nc.psum_tensor("final_total", [P, 1], F32))
        cols = ctx.enter_context(nc.psum_tensor("final_cols", [P, BLOCKS], F32))
        prior = ctx.enter_context(nc.psum_tensor("final_prior", [P, BLOCKS], F32))

        s_iota = sem("iota")
        s_tri = sem("triangle")
        s_v = sem("dve")
        s_total = sem("total")
        s_prior = sem("prior")
        s_out = [sem(f"out{i}") for i in range(2)]
        count = {"n": 0, "at": {}}
        need = []
        SPAN = 7
        assert BLOCKS % SPAN == 0

        block = ctx.enter_context(nc.Block())

        @block.gpsimd
        def _(pool):
            g = nc.gpsimd
            g.iota(node_i[:, :], pattern=[[P, BLOCKS]], base=0, channel_multiplier=1).then_inc(s_iota, 1)
            g.memset(before[:, :], 1.0).then_inc(s_tri, 1)
            pool.wait_ge(s_tri, 1)
            g.affine_select(out=before[:, :], in_=before[:, :], compare_op=ALU.is_gt, fill=0.0,
                            base=0, pattern=[[1, P]], channel_multiplier=-1).then_inc(s_tri, 1)

        @block.vector
        def _(dve):
            v = nc.vector

            def link(ins, name=None):
                ins.then_inc(s_v, 1)
                count["n"] += 1
                if name:
                    count["at"][name] = count["n"]
                dve.wait_ge(s_v, count["n"])

            def count_of(in0, scalar, op):
                link(v.tensor_scalar(cmp_[:, :], in0, scalar, 0.0, op, ALU.add, accum_out=part[:, :]))
                need.append(count["n"])
                dve.wait_ge(s_total, len(need))

            link(v.memset(ones[:, :], 1.0))
            link(v.memset(zero[:, :], 1.0))
            link(v.memset(theta[:, :], 0))
            link(v.memset(bit[:, :], 1 << 30))
            dve.wait_ge(s_iota, 1)
            link(v.tensor_scalar(valid[:, :], node_i[:, :], float(N), None, ALU.is_lt))
            link(v.tensor_scalar(hide[:, :], valid[:, :], -1.0, 3e38, ALU.add, ALU.mult))
            link(v.tensor_tensor(u[:, :], gates[:, :], valid[:, :], ALU.mult))
            link(v.tensor_tensor(w[:, :], u[:, :], hide[:, :], ALU.add))
            count_of(w[:, :], 0.0, ALU.is_ge)
            link(v.tensor_scalar(take_f[:, :], total[:, :], float(TOPK), None, ALU.is_ge))
            link(v.tensor_scalar(sign[:, :], take_f[:, :], 2.0, -1.0, ALU.mult, ALU.add))
            link(v.tensor_scalar(rank[:, :], take_f[:, :], float(2 * TOPK - N - 1), float(N - TOPK + 1),
                                 ALU.mult, ALU.add))
            link(v.tensor_scalar(u[:, :], u[:, :], sign[:, 0:1], None, ALU.mult))
            link(v.tensor_tensor(u[:, :], u[:, :], hide[:, :], ALU.add))
            for _ in range(31):
                link(v.tensor_tensor(cand[:, :], theta[:, :], bit[:, :], ALU.bitwise_or))
                count_of(u[:, :], cand[:, :].bitcast(F32), ALU.is_ge)
                link(v.tensor_tensor(take_f[:, :], total[:, :], rank[:, :], ALU.is_ge))
                link(v.tensor_copy(take_i[:, :], take_f[:, :]))
                link(v.tensor_tensor(take_i[:, :], take_i[:, :], bit[:, :], ALU.mult))
                link(v.tensor_tensor(theta[:, :], theta[:, :], take_i[:, :], ALU.bitwise_or))
                link(v.tensor_single_scalar(bit[:, :], bit[:, :], 1, op=ALU.logical_shift_right))
            link(v.tensor_tensor(bound[:, :], theta[:, :].bitcast(F32), sign[:, :], ALU.mult))
            link(v.tensor_scalar(above[:, :], w[:, :], bound[:, 0:1], None, ALU.is_gt))
            link(v.tensor_scalar(equal[:, :], w[:, :], bound[:, 0:1], None, ALU.is_equal), "equal")
            count_of(w[:, :], bound[:, 0:1], ALU.is_gt)
            link(v.tensor_scalar(rank[:, :], total[:, :], -1.0, float(TOPK), ALU.mult, ALU.add))
            dve.wait_ge(s_prior, 1)
            link(v.tensor_tensor_scan(run[:, :], zero[:, :], cols[:, :], 0.0, ALU.mult, ALU.add))
            link(v.tensor_tensor(run[:, :], run[:, :], cols[:, :], ALU.subtract))
            link(v.tensor_tensor(run[:, :], run[:, :], prior[:, :], ALU.add))
            link(v.tensor_scalar(run[:, :], run[:, :], rank[:, 0:1], None, ALU.is_lt))
            link(v.tensor_tensor(equal[:, :], equal[:, :], run[:, :], ALU.mult))
            link(v.tensor_tensor(sel[:, :], above[:, :], equal[:, :], ALU.add))
            for b in range(BLOCKS):
                n = b // SPAN
                if b % SPAN == 0 and n >= 2:
                    dve.wait_ge(s_out[n % 2], 16 * (n // 2))
                o = (rows if n % 2 == 0 else rows2)[:, b % SPAN, :]
                v.scalar_tensor_tensor(out=o.rearrange("p (c n) -> p c n", c=2), in0=acc[:, 0:2, b * P:(b + 1) * P],
                                       scalar=sel[:, b:b + 1],
                                       in1=qc[:, b * QC:b * QC + D].rearrange("p (c n) -> p c n", c=2),
                                       op0=ALU.mult, op1=ALU.add).then_inc(s_v, 1)
                count["n"] += 1
                if b % SPAN == SPAN - 1:
                    count["at"][f"rows{n}"] = count["n"]

        at = count["at"]

        @block.tensor
        def _(pe):
            t = nc.tensor
            for i, n in enumerate(need):
                if i == len(need) - 1:
                    pe.wait_ge(s_tri, 2)
                    pe.wait_ge(s_v, at["equal"])
                    t.matmul(cols[:, :], ones[:, :], equal[:, :], start=True, stop=True)
                    t.matmul(prior[:, :], before[:, :], equal[:, :], start=True, stop=True).then_inc(s_prior, 1)
                pe.wait_ge(s_v, n)
                t.matmul(total[:, :], ones[:, :], part[:, :], start=True, stop=True).then_inc(s_total, 1)

        @block.sync
        def _(sp):
            for n in range(BLOCKS // SPAN):
                sp.wait_ge(s_v, at[f"rows{n}"])
                r = rows if n % 2 == 0 else rows2
                first = n * SPAN * P
                if n < BLOCKS // SPAN - 1:
                    sp.dma_start(out[first:first + SPAN * P, :].rearrange("(b p) d -> p b d", p=P), r[:, :, :])\
                        .then_inc(s_out[n % 2], 16)
                else:
                    whole = (SPAN - 1) * P
                    sp.dma_start(out[first:first + whole, :].rearrange("(b p) d -> p b d", p=P),
                                 r[:, 0:SPAN - 1, :]).then_inc(s_out[n % 2], 16)
                    sp.dma_start(out[first + whole:N, :], r[0:LAST, SPAN - 1, :]).then_inc(s_out[n % 2], 16)
            sp.wait_ge(s_out[0], 16 * 5)
            sp.wait_ge(s_out[1], 16 * 3)


def build(nc, a, out):
    with ExitStack() as ctx:
        def sb(name, shape, dt=F32):
            return ctx.enter_context(nc.sbuf_tensor(name, shape, dt))

        def dr(name, shape, dt=F32):
            return nc.dram_tensor(name, shape, dt).ap()

        keep = {"ident": sb("ident", [P, P]), "cols": sb("cols", [P, SELW]), "part": sb("part", [P, 1]),
                "ecol": sb("ecol", [P, P]), "self": sb("self", [P, BLOCKS * H]), "gates": sb("gates", [P, BLOCKS])}
        dram = {"src": dr("src_padded", (TILES * P,), I32), "dst": dr("dst_padded", (TILES * P,), I32),
                "ends": dr("step_ends", (SC * P * 2,)), "regs": dr("step_regs", (SC * P, 2), I32),
                "rel": dr("step_rel", (SC * P, P), BF16), "flags": dr("step_flags", (2, SC * P, P)),
                "idx": dr("step_src", (P, SC * P), I32), "col": dr("step_col", (P, SC * P)),
                "last": dr("step_last", (P, SC * P)), "eregs": dr("end_regs", (P, 2), I32),
                "h": dr("h", (BLOCKS * P, D)), "kv": dr("kv", (BLOCKS * P, KV))}
        constants(nc, keep)
        plan_steps(nc, a["src"], a["dst"], dram, keep)
        keep["qc"] = sb("qc", [P, BLOCKS * QC])
        keep["acc"] = sb("acc", [P, 3, (BLOCKS + 1) * P])
        clear_sums(nc, keep)
        node_pass(nc, "first", a, dram, keep)
        for layer in range(LAYERS):
            with nc.sbuf_tensor(f"ends{layer}", [P, 3, ENDS], F32) as ends:
                keep["ends"] = ends
                edge_pass(nc, layer, dram, keep)
                merge_ends(nc, layer, dram, keep)
            node_pass(nc, "middle" if layer < LAYERS - 1 else "last", a, dram, keep)
        select_and_store(nc, dram, keep, out)


def clear_sums(nc, keep):
    with nc.Block() as block:
        @block.vector
        def _(dve):
            nc.vector.memset(keep["acc"][:, :, :], 0.0)


_OUT = ((N, D), "float32")


def kernel(**inputs):
    import numpy as _np
    import concourse.bacc as _bacc
    from concourse.bass_utils import run_bass_kernel_spmd as _run

    nc = _bacc.Bacc("TRN2", target_bir_lowering=False, num_devices=1)
    arrays, args = {}, {}
    for name, value in inputs.items():
        a = _np.ascontiguousarray(value)
        arrays[f"in_{name}"] = a
        args[name] = nc.dram_tensor(f"in_{name}", a.shape, mybir.dt.from_np(a.dtype), kind="ExternalInput").ap()
    out = nc.dram_tensor("out_0", _OUT[0], F32, kind="ExternalOutput").ap()
    build(nc, args, out)
    r = _run(nc, [arrays], core_ids=[0])
    return r.results[0]["out_0"]
```

```python
from contextlib import ExitStack

import concourse.bass as bass
from concourse import mybir

ALU = mybir.AluOpType
ACT = mybir.ActivationFunctionType
AX = mybir.AxisListType
F32 = mybir.dt.float32
BF16 = mybir.dt.bfloat16
I32 = mybir.dt.int32

P = 128
N, D = 6250, 256
E = 100000
H, DH = 8, 32
FF = 1024
LAYERS = 2
EPS = 1e-5
SCALE = DH ** -0.5
BIG = 1e30
TOPK = N // 2 - 1

TILES = -(-E // P)
BLOCKS = -(-N // P)
LAST = N - (BLOCKS - 1) * P
G = 8
STEPS = -(-(TILES + BLOCKS - 1) // G) * G
GROUPS = STEPS // G
assert GROUPS % 4 == 0
SC = -(-STEPS // P)
ENDS = 2 * STEPS
ETILES = ENDS // P
assert ENDS % P == 0
MERGES = ETILES + BLOCKS - 1
KV = 2 * D
QC = D + 2 * H
SELW = P + 2
ZM = 40
PAD_DST = 50000


class Phase(ExitStack):

    def __init__(self, nc):
        super().__init__()
        self.nc, self.semaphores = nc, []

    def semaphore(self, name):
        self.semaphores.append(self.nc.alloc_semaphore(name=name))
        return self.semaphores[-1]

    def __exit__(self, *error):
        done = super().__exit__(*error)
        if error[0] is None:
            self.nc.clear_and_free_semaphores(self.semaphores)
            self.nc.all_engine_barrier()
        return done


class Progress:

    def __init__(self, nc, ctx, name, lanes):
        self.sems = [ctx.semaphore(f"{name}_{i}") for i in range(lanes)]
        self.base = [0] * lanes
        self.steps = ()

    def begin(self, steps):
        self.steps = tuple(steps)
        self.place = {s: i + 1 for i, s in enumerate(self.steps)}
        assert len(self.place) == len(self.steps)
        self.told = [0] * len(self.sems)

    def end(self, turns):
        for i, t in enumerate(turns):
            self.base[i] += t * len(self.steps)

    def at(self, turn, step):
        lane, k, c = turn
        value = self.base[lane] + c * len(self.steps) + self.place[step]
        return value if k is None else k * len(self.steps) + value

    def wait(self, eng, turn, step, beside=None):
        if beside is not None:
            wait_beside(eng, beside, self.sems[turn[0]], self.at(turn, step))
        else:
            eng.wait_ge(self.sems[turn[0]], self.at(turn, step))

    def last_of(self, *steps):
        return max(steps, key=lambda s: self.place[s])

    def wait_turn(self, eng, turn, beside=None):
        lane, k, c = turn
        value = self.base[lane] + c * len(self.steps)
        value = value if k is None else k * len(self.steps) + value
        if beside is not None:
            wait_beside(eng, beside, self.sems[lane], value)
        else:
            eng.wait_ge(self.sems[lane], value)

    def tick(self, ins, turn, step):
        lane = turn[0]
        assert self.steps[self.told[lane] % len(self.steps)] == step, (step, self.steps[self.told[lane] % len(self.steps)])
        self.told[lane] += 1
        ins.then_inc(self.sems[lane], 1)
        return ins


def wait_beside(eng, plain, sem, value):
    if not isinstance(value, int):
        value = eng.to_reg(value)
        eng.wait_ge(plain, 1)
    eng.wait_ge(sem, value)


def bc(ap, shape):
    return ap.broadcast_to(shape)


def plan_steps(nc, src, dst, dram, keep):
    with Phase(nc) as ctx:
        def sb(name, shape, dt=F32):
            return ctx.enter_context(nc.sbuf_tensor("plan_" + name, shape, dt))

        def ps(name, shape, dt=F32):
            return ctx.enter_context(nc.psum_tensor("plan_" + name, shape, dt))

        def sem(name):
            return ctx.semaphore("plan_" + name)

        padi = sb("padi", [1, 2, P], I32)
        frow_i = sb("frow_i", [1, TILES], I32)
        fblk_i = sb("fblk_i", [1, TILES], I32)
        trow_i = sb("trow_i", [1, TILES], I32)
        frow = sb("frow", [1, TILES])
        trow = sb("trow", [1, TILES])
        key = sb("key", [1, TILES])
        ones = sb("ones", [1, P])
        keyb = sb("keyb", [P, TILES])
        cmp_ = sb("cmp", [P, TILES])
        step_i = sb("step_i", [P, SC], I32)
        step = sb("step", [P, SC])
        tile_ = sb("tile", [P, SC])
        tile_i = sb("tile_i", [P, SC], I32)
        base = sb("base", [P, SC])
        blk = sb("blk", [P, SC])
        c = sb("c", [P, SC])
        d = sb("d", [P, SC])
        dne = sb("dne", [P, SC])
        regs_f = sb("regs_f", [P, SC, 2])
        regs_i = sb("regs_i", [P, SC, 2], I32)
        ends = sb("ends", [P, SC, 2])
        sg_i = sb("sg_i", [P, SC, P], I32)
        dg_i = sb("dg_i", [P, SC, P], I32)
        sg = sb("sg", [P, SC, P])
        dg = sb("dg", [P, SC, P])
        rel = sb("rel", [P, SC, P])
        rel16 = sb("rel16", [P, SC, P], BF16)
        far = sb("far", [P, SC, P])
        isc = sb("isc", [P, SC, P])
        isd = sb("isd", [P, SC, P])
        col = sb("col", [P, SC, P])
        diff = sb("diff", [P, SC, P])
        nf = sb("nf", [P, SC, P])
        nb = sb("nb", [P, SC, P])
        last = sb("last", [P, SC, P])
        tab_i = sb("tab_i", [P, SC * P], I32)
        tab_c = sb("tab_c", [P, SC * P])
        tab_l = sb("tab_l", [P, SC * P])
        pk = ps("pk", [P, 1024])
        pt = [ps(f"pt{i}", [P, 3, P]) for i in range(2)]

        efrow = sb("efrow", [1, ETILES])
        eblk = sb("eblk", [1, ETILES])
        etmp = sb("etmp", [1, ETILES], I32)
        ekey = sb("ekey", [1, ETILES])
        etrow_i = sb("etrow_i", [1, ETILES], I32)
        etrow = sb("etrow", [1, ETILES])
        ekeyb = sb("ekeyb", [P, ETILES])
        ecmp = sb("ecmp", [P, ETILES])
        etile = sb("etile", [P, 1])
        etile_i = sb("etile_i", [P, 1], I32)
        ebase = sb("ebase", [P, 1])
        eregs_f = sb("eregs_f", [P, 2])
        eregs_i = sb("eregs_i", [P, 2], I32)
        eg = sb("eg", [P, P])
        erel = sb("erel", [P, P])
        pe2 = ps("pe2", [P, ETILES])
        pe3 = ps("pe3", [P, P])

        s_pad = sem("pad")
        s_padded = sem("padded")
        s_first = sem("first")
        s_iota = sem("iota")
        s_v = sem("dve")
        s_key = sem("key_spread")
        s_gather = sem("gathered")
        s_turned = sem("turned")
        s_taken = sem("taken")
        s_store = sem("stored")
        s_ends = sem("ends_stored")
        s_efirst = sem("ends_first")
        s_ekey = sem("ends_key_spread")
        s_egather = sem("ends_gathered")
        s_eturn = sem("ends_turned")
        s_estore = sem("ends_tables_stored")
        count = {"n": 0, "at": {}}

        block = ctx.enter_context(nc.Block())

        @block.vector
        def _(dve):
            def link(ins, name=None):
                ins.then_inc(s_v, 1)
                count["n"] += 1
                if name:
                    count["at"][name] = count["n"]
                dve.wait_ge(s_v, count["n"])

            v = nc.vector
            v.memset(padi[:, 0, :], 0).then_inc(s_pad, 1)
            v.memset(padi[:, 1, :], PAD_DST).then_inc(s_pad, 1)
            link(v.memset(ones[:, :], 1.0))
            dve.wait_ge(s_iota, 3)
            link(v.tensor_copy(step[:, :], step_i[:, :]))
            link(v.tensor_copy(trow[:, :], trow_i[:, :]))
            link(v.tensor_copy(etrow[:, :], etrow_i[:, :]))
            dve.wait_ge(s_first, 16)
            link(v.tensor_single_scalar(fblk_i[:, :], frow_i[:, :], 7, op=ALU.arith_shift_right))
            link(v.tensor_copy(frow[:, :], fblk_i[:, :]))
            link(v.tensor_tensor(key[:, :], frow[:, :], trow[:, :], ALU.add), "key")
            dve.wait_ge(s_key, 1)
            link(v.tensor_copy(keyb[:, :], pk[:, 0:TILES]))
            for j in range(SC):
                link(v.tensor_scalar(cmp_[:, 1:TILES], keyb[:, 1:TILES], step[:, j:j + 1], 0.0,
                                     ALU.is_le, ALU.add, accum_out=tile_[:, j:j + 1]))
            link(v.tensor_copy(tile_i[:, :], tile_[:, :]), "tile")
            link(v.tensor_tensor(blk[:, :], step[:, :], tile_[:, :], ALU.subtract))
            link(v.tensor_scalar(base[:, :], blk[:, :], float(P), None, ALU.mult))
            link(v.tensor_scalar(regs_f[:, :, 1], blk[:, :], float(BLOCKS - 1), float(QC), ALU.min, ALU.mult))
            dve.wait_ge(s_gather, 16 * 2 * SC)
            link(v.tensor_copy(sg[:, :, :], sg_i[:, :, :]), "sg")
            link(v.tensor_copy(dg[:, :, :], dg_i[:, :, :]))
            link(v.tensor_tensor(c[:, :], base[:, :], dg[:, :, 0], ALU.max))
            link(v.tensor_scalar(d[:, :], base[:, :], float(P - 1), None, ALU.add))
            link(v.tensor_tensor(d[:, :], d[:, :], dg[:, :, P - 1], ALU.min))
            link(v.tensor_tensor(d[:, :], d[:, :], c[:, :], ALU.max))
            link(v.tensor_copy(ends[:, :, 0], c[:, :]))
            link(v.tensor_copy(ends[:, :, 1], d[:, :]), "ends")
            link(v.tensor_scalar(regs_f[:, :, 0], c[:, :], float((BLOCKS) * P), None, ALU.min))
            link(v.tensor_copy(regs_i[:, :, :], regs_f[:, :, :]), "regs")
            cb = bc(c[:, :].unsqueeze(2), [P, SC, P])
            db = bc(d[:, :].unsqueeze(2), [P, SC, P])
            bb = bc(base[:, :].unsqueeze(2), [P, SC, P])
            link(v.tensor_tensor(rel[:, :, :], dg[:, :, :], bb, ALU.subtract))
            link(v.tensor_scalar(rel16[:, :, :], rel[:, :, :], -1.0, 200.0, ALU.max, ALU.min), "rel")
            link(v.tensor_scalar(far[:, :, :], rel[:, :, :], float(P), 1e5, ALU.is_ge, ALU.mult))
            link(v.tensor_tensor(isc[:, :, :], dg[:, :, :], cb, ALU.is_equal))
            link(v.tensor_tensor(isd[:, :, :], dg[:, :, :], db, ALU.is_equal))
            link(v.tensor_tensor(diff[:, :, :], isd[:, :, :], isc[:, :, :], ALU.mult))
            link(v.tensor_tensor(isd[:, :, :], isd[:, :, :], diff[:, :, :], ALU.subtract))
            link(v.tensor_tensor(col[:, :, :], dg[:, :, :], cb, ALU.subtract))
            link(v.tensor_tensor(diff[:, :, :], isc[:, :, :], isd[:, :, :], ALU.add))
            link(v.tensor_scalar(diff[:, :, :], diff[:, :, :], -1.0, 1.0, ALU.mult, ALU.add))
            link(v.tensor_tensor(col[:, :, :], col[:, :, :], diff[:, :, :], ALU.mult))
            link(v.tensor_tensor(col[:, :, :], col[:, :, :], far[:, :, :], ALU.add))
            link(v.scalar_tensor_tensor(out=col[:, :, :], in0=isc[:, :, :], scalar=float(P), in1=col[:, :, :],
                                        op0=ALU.mult, op1=ALU.add))
            link(v.scalar_tensor_tensor(out=col[:, :, :], in0=isd[:, :, :], scalar=float(P + 1), in1=col[:, :, :],
                                        op0=ALU.mult, op1=ALU.add), "col")
            link(v.memset(last[:, :, P - 1:P], 1.0))
            link(v.tensor_tensor(last[:, :, 0:P - 1], dg[:, :, 0:P - 1], dg[:, :, 1:P], ALU.not_equal), "last")
            link(v.memset(nf[:, :, 0:1], 0.0))
            link(v.tensor_scalar(nf[:, :, 1:P], last[:, :, 0:P - 1], -BIG, None, ALU.mult))
            link(v.tensor_scalar(nb[:, :, :], last[:, :, :], -BIG, None, ALU.mult), "flags")
            for j in range(SC):
                dve.wait_ge(s_turned, j + 1)
                v.tensor_copy(tab_i[:, j * P:(j + 1) * P], pt[j % 2][:, 0, :]).then_inc(s_taken, 1)
                v.tensor_copy(tab_c[:, j * P:(j + 1) * P], pt[j % 2][:, 1, :]).then_inc(s_taken, 1)
                v.tensor_copy(tab_l[:, j * P:(j + 1) * P], pt[j % 2][:, 2, :]).then_inc(s_taken, 1)
            dve.wait_ge(s_efirst, 16)
            link(v.tensor_copy(etmp[:, :], efrow[:, :]))
            link(v.tensor_single_scalar(etmp[:, :], etmp[:, :], 7, op=ALU.arith_shift_right))
            link(v.tensor_copy(eblk[:, :], etmp[:, :]))
            link(v.tensor_tensor(ekey[:, :], eblk[:, :], etrow[:, :], ALU.add), "ekey")
            dve.wait_ge(s_ekey, 1)
            link(v.tensor_copy(ekeyb[:, :], pe2[:, :]))
            link(v.tensor_scalar(ecmp[:, 1:ETILES], ekeyb[:, 1:ETILES], step[:, 0:1], 0.0,
                                 ALU.is_le, ALU.add, accum_out=etile[:, :]))
            link(v.tensor_copy(etile_i[:, :], etile[:, :]), "etile")
            link(v.tensor_tensor(ebase[:, :], step[:, 0:1], etile[:, :], ALU.subtract))
            link(v.tensor_scalar(eregs_f[:, 0:1], etile[:, :], float(QC), None, ALU.mult))
            link(v.tensor_scalar(eregs_f[:, 1:2], ebase[:, :], float(BLOCKS - 1), float(QC), ALU.min, ALU.mult))
            link(v.tensor_copy(eregs_i[:, :], eregs_f[:, :]))
            link(v.tensor_scalar(ebase[:, :], ebase[:, :], float(P), None, ALU.mult))
            dve.wait_ge(s_egather, 16)
            link(v.tensor_scalar(erel[:, :], eg[:, :], ebase[:, 0:1], None, ALU.subtract), "erel")
            dve.wait_ge(s_eturn, 1)
            link(v.tensor_copy(keep["ecol"][:, :], pe3[:, :]))

        at = count["at"]

        @block.gpsimd
        def _(pool):
            g = nc.gpsimd
            g.iota(step_i[:, :], pattern=[[P, SC]], base=0, channel_multiplier=1).then_inc(s_iota, 1)
            g.iota(trow_i[:, :], pattern=[[1, TILES]], base=0, channel_multiplier=0).then_inc(s_iota, 1)
            g.iota(etrow_i[:, :], pattern=[[1, ETILES]], base=0, channel_multiplier=0).then_inc(s_iota, 1)
            pool.wait_ge(s_v, at["tile"])
            pool.wait_ge(s_padded, 64)
            for j in range(SC):
                for table, rows in ((dram["src"], sg_i), (dram["dst"], dg_i)):
                    g.indirect_dma_start(rows[:, j, :], None, table.rearrange("(t p) -> t p", p=P),
                                         bass.IndirectOffsetOnAxis(ap=tile_i[:, j:j + 1], axis=0))\
                        .then_inc(s_gather, 16)
            pool.wait_ge(s_v, at["etile"])
            pool.wait_ge(s_ends, 16)
            g.indirect_dma_start(eg[:, :], None, dram["ends"][0:ENDS].rearrange("(t p) -> t p", p=P),
                                 bass.IndirectOffsetOnAxis(ap=etile_i[:, 0:1], axis=0)).then_inc(s_egather, 16)

        @block.sync
        def _(sp):
            sp.dma_start(dram["src"][0:E], src[:]).then_inc(s_padded, 16)
            sp.dma_start(dram["dst"][0:E], dst[:]).then_inc(s_padded, 16)
            sp.wait_ge(s_pad, 2)
            pad = TILES * P - E
            sp.dma_start(dram["src"][E:].rearrange("(o p) -> o p", o=1), padi[:, 0, 0:pad]).then_inc(s_padded, 16)
            sp.dma_start(dram["dst"][E:].rearrange("(o p) -> o p", o=1), padi[:, 1, 0:pad]).then_inc(s_padded, 16)
            sp.wait_ge(s_padded, 64)
            with nc.allow_non_contiguous_dma(reason="first dst of every tile"):
                sp.dma_start(frow_i[:, :], dram["dst"].rearrange("(o t p) -> o t p", o=1, p=P)[:, :, 0])\
                    .then_inc(s_first, 16)
            sp.wait_ge(s_v, at["ends"])
            sp.dma_start(dram["ends"].rearrange("(c p w) -> p c w", p=P, w=2), ends[:, :, :]).then_inc(s_ends, 16)
            sp.wait_ge(s_v, at["regs"])
            sp.dma_start(dram["regs"].rearrange("(c p) w -> p c w", p=P), regs_i[:, :, :]).then_inc(s_store, 16)
            sp.wait_ge(s_v, at["rel"])
            sp.dma_start(dram["rel"].rearrange("(c p) e -> p c e", p=P), rel16[:, :, :]).then_inc(s_store, 16)
            sp.wait_ge(s_ends, 16)
            with nc.allow_non_contiguous_dma(reason="first end of every tile of ends"):
                sp.dma_start(efrow[:, :], dram["ends"][0:ENDS].rearrange("(o t p) -> o t p", o=1, p=P)[:, :, 0])\
                    .then_inc(s_efirst, 16)
            sp.wait_ge(s_v, at["flags"])
            sp.dma_start(dram["flags"][0].rearrange("(c p) e -> p c e", p=P), nf[:, :, :]).then_inc(s_store, 16)
            sp.dma_start(dram["flags"][1].rearrange("(c p) e -> p c e", p=P), nb[:, :, :]).then_inc(s_store, 16)
            sp.wait_ge(s_taken, 3 * SC)
            sp.dma_start(dram["idx"], tab_i[:, :]).then_inc(s_store, 16)
            sp.dma_start(dram["col"], tab_c[:, :]).then_inc(s_store, 16)
            sp.dma_start(dram["last"], tab_l[:, :]).then_inc(s_store, 16)
            sp.wait_ge(s_v, at["erel"])
            sp.dma_start(dram["eregs"], eregs_i[:, :]).then_inc(s_estore, 16)
            sp.wait_ge(s_store, 16 * 7)
            sp.wait_ge(s_estore, 16)

        @block.tensor
        def _(pe):
            t = nc.tensor
            pe.wait_ge(s_v, at["key"])
            t.matmul(pk[:, 0:512], ones[:, :], key[:, 0:512], start=True, stop=True)
            t.matmul(pk[:, 512:TILES], ones[:, :], key[:, 512:TILES], start=True, stop=True).then_inc(s_key, 1)
            pe.wait_ge(s_v, at["last"])
            for j in range(SC):
                if j >= 2:
                    pe.wait_ge(s_taken, 3 * (j - 1))
                t.transpose(pt[j % 2][:, 0, :], sg[:, j, :], keep["ident"][:, :])
                t.transpose(pt[j % 2][:, 1, :], col[:, j, :], keep["ident"][:, :])
                t.transpose(pt[j % 2][:, 2, :], last[:, j, :], keep["ident"][:, :]).then_inc(s_turned, 1)
            pe.wait_ge(s_v, at["ekey"])
            t.matmul(pe2[:, :], ones[:, :], ekey[:, :], start=True, stop=True).then_inc(s_ekey, 1)
            pe.wait_ge(s_v, at["erel"])
            t.transpose(pe3[:, :], erel[:, :], keep["ident"][:, :]).then_inc(s_eturn, 1)
def constants(nc, keep):
    with Phase(nc) as ctx:
        s_a = ctx.semaphore("const_a")
        s_b = ctx.semaphore("const_b")
        iota_i = ctx.enter_context(nc.sbuf_tensor("iota_i", [P, SELW], I32))
        part_i = ctx.enter_context(nc.sbuf_tensor("part_i", [P, 1], I32))
        block = ctx.enter_context(nc.Block())

        @block.gpsimd
        def _(pool):
            g = nc.gpsimd
            g.memset(keep["ident"][:, :], 0.0).then_inc(s_a, 1)
            g.iota(iota_i[:, :], pattern=[[1, SELW]], base=0, channel_multiplier=0).then_inc(s_b, 1)
            g.iota(part_i[:, :], pattern=[[0, 1]], base=0, channel_multiplier=1).then_inc(s_b, 1)
            pool.wait_ge(s_a, 1)
            g.affine_select(out=keep["ident"][:, :], in_=keep["ident"][:, :], compare_op=ALU.not_equal, fill=1.0,
                            base=0, pattern=[[-1, P]], channel_multiplier=1).then_inc(s_a, 1)

        @block.vector
        def _(dve):
            dve.wait_ge(s_b, 2)
            nc.vector.tensor_copy(keep["cols"][:, :], iota_i[:, :])
            nc.vector.tensor_copy(keep["part"][:, :], part_i[:, :])


WEAVE = (("product", 0), ("up", 0), ("score", 0), ("top", 0), ("product", 1), ("weigh", 0), ("tail", 0),
         ("score", 1), ("tail", 1), ("product", 2), ("tail", 2), ("score", 2), ("product", 3), ("tail", 3),
         ("score", 3), ("turn", 0))
PAIRS = G // 2
QBUFS = 2
ABUFS = 4


def later(turn, n):
    lane, k, c = turn
    g = 4 * c + lane + n
    return (g % 4, k, g // 4)


def is_first(turn):
    return turn[1] is None and turn[0] == 0 and turn[2] == 0


def edge_pass(nc, layer, dram, keep):
    with Phase(nc) as ctx:
        def sb(name, shape, dt=F32):
            return ctx.enter_context(nc.sbuf_tensor(f"edge{layer}_{name}", shape, dt))

        def ps(name, shape, dt=F32):
            return ctx.enter_context(nc.psum_tensor(f"edge{layer}_{name}", shape, dt))

        def sem(name):
            return ctx.semaphore(f"edge{layer}_{name}")

        acc, ends, qc = keep["acc"], keep["ends"], keep["qc"]
        kv = sb("kv", [P, 2, G, KV])
        idx = sb("idx", [P, 4, G], I32)
        rel = sb("rel", [P, 2, G * P], BF16)
        flags = sb("flags", [G * H, 2, 2, P])
        col = sb("col", [P, 4, G])
        last = sb("last", [P, 4, G])
        regs = sb("regs", [1, 4, 2 * G], I32)
        spread = sb("spread", [P, 2, G * P])
        sel = sb("sel", [P, G, SELW])
        score = sb("score", [P, 2, G * H])
        up = sb("up", [G * H, P])
        top = sb("top", [G * H, P])
        below = sb("below", [P, G * H])
        wm = sb("wm", [P, 2, G, ZM])
        psq = [ps(f"q{i}", [P, 2, D]) for i in range(QBUFS)]
        turned = ps("turned", [P, 512])
        pst = turned[0:G * H, 0:P]
        psm = turned[:, P:P + G * H]
        psa = [ps(f"sums{i}", [P, 512]) for i in range(ABUFS)]

        s_clear = sem("cleared")
        s_idx = [sem(f"idx{i}") for i in range(4)]
        s_rel = [sem(f"rel{i}") for i in range(2)]
        s_flags = [sem(f"flags{i}") for i in range(2)]
        s_table = [sem(f"table{i}") for i in range(4)]
        s_row = [[sem(f"rows{i}_{j}") for j in range(G)] for i in range(2)]

        dve_p = Progress(nc, ctx, f"edge{layer}_dve", 4)
        act_p = Progress(nc, ctx, f"edge{layer}_act", 4)
        pe_p = Progress(nc, ctx, f"edge{layer}_pe", 4)
        dve_steps = ["spread"]
        for m in range(PAIRS):
            dve_steps += [f"product{m}", f"score{m}"]
        dve_steps += ["up", "top", "below", "maxima"]
        for m in range(PAIRS):
            dve_steps += [f"sel{m}", f"value{m}"]
        dve_p.begin(dve_steps)
        pe_p.begin([f"q{m}" for m in range(PAIRS)] + ["score_t", "max_t"] + [f"sums{j}" for j in range(G)])
        act_p.begin(["weights"] + [f"{n}{j}" for j in range(G) for n in ("acc", "ends")])

        def fill(sems, depth, turn):
            lane, k, c = turn
            if depth == 4:
                return sems[lane], (16 * (c + 1) if k is None else k * 16 + 16 * (c + 1))
            n = 2 * c + lane // 2
            return sems[lane % 2], (16 * (n + 1) if k is None else k * 32 + 16 * (n + 1))

        def groups_of(eng, body):
            body((0, None, 0), first=True)
            body((1, None, 0))
            body((2, None, 0))
            body((3, None, 0))
            with eng.Fori(0, GROUPS // 4 - 2) as k:
                for r in range(4):
                    body((r, k, 1))
            for g in range(GROUPS - 4, GROUPS):
                body((g % 4, None, g // 4), end=g == GROUPS - 1)

        def number(turn, scale):
            lane, k, c = turn
            g = (4 * c + lane) * scale
            return g if k is None else k * (4 * scale) + g

        block = ctx.enter_context(nc.Block())

        @block.sync
        def _(sp):
            def load_idx(turn, wait=True):
                if wait:
                    before = later(turn, -4)
                    for j in range(G):
                        wait_beside(sp, s_clear, *fill([s_row[0][j], s_row[1][j]], 2, before))
                sp.dma_start(idx[:, turn[0], :], dram["idx"][:, bass.ds(number(turn, G), G)])\
                    .then_inc(s_idx[turn[0]], 16)

            def load_rel(turn, wait=True):
                if wait:
                    dve_p.wait(sp, later(turn, -2), "spread", beside=s_clear)
                sp.dma_start(rel[:, turn[0] % 2, :],
                             dram["rel"].rearrange("s e -> (s e)")[bass.ds(number(turn, G * P), G * P)]
                             .partition_broadcast(P)).then_inc(fill(s_rel, 2, turn)[0], 16)

            def load_rest(turn, wait=True):
                if wait:
                    before = later(turn, -4)
                    dve_p.wait(sp, before, f"value{PAIRS - 1}", beside=s_clear)
                    act_p.wait(sp, before, f"ends{G - 1}", beside=s_clear)
                slot = turn[0]
                s = s_table[slot]
                for tab, name in ((col, "col"), (last, "last")):
                    sp.dma_start(tab[:, slot, :], dram[name][:, bass.ds(number(turn, G), G)]).then_inc(s, 16)
                sp.dma_start(regs[:, slot, :],
                             dram["regs"].rearrange("(o s) w -> o (s w)", o=1)[:, bass.ds(number(turn, 2 * G), 2 * G)])\
                    .then_inc(s, 16)

            def load_flags(turn, wait=True):
                if wait:
                    dve_p.wait(sp, later(turn, -2), "top", beside=s_clear)
                s = fill(s_flags, 2, turn)[0]
                for w in range(2):
                    rows = dram["flags"][w][bass.ds(number(turn, G), G), :].unsqueeze(1)
                    sp.dma_start(flags[:, turn[0] % 2, w, :], bc(rows, [G, H, P])).then_inc(s, 16)

            for g in range(4):
                turn = (g, None, 0)
                load_idx(turn, False)
                if g < 2:
                    load_rel(turn, False)
                    load_flags(turn, False)
                load_rest(turn, False)
            load_rel((2, None, 0))

            def one(turn, g=None):
                if g is None or g + 4 < GROUPS:
                    load_idx(later(turn, 4))
                if g is None or g + 3 < GROUPS:
                    load_rel(later(turn, 3))
                if g is None or 2 <= g and g + 2 < GROUPS:
                    load_rest(later(turn, 2))
                if g is None or 1 <= g and g + 1 < GROUPS:
                    load_flags(later(turn, 1))

            for g in range(4):
                one((g, None, 0), g)
            with sp.Fori(0, GROUPS // 4 - 2) as k:
                for r in range(4):
                    one((r, k, 1))
            for g in range(GROUPS - 4, GROUPS):
                one((g % 4, None, g // 4), g)

        @block.gpsimd
        def _(pool):
            def rows(turn, first=False):
                lane = turn[0] % 2
                for j in range(G):
                    if j == 0:
                        wait_beside(pool, s_clear, *fill(s_idx, 4, turn))
                    if not first:
                        pe_p.wait(pool, later(turn, -2), f"sums{j}", beside=s_clear)
                    nc.gpsimd.indirect_dma_start(
                        kv[:, lane, j, :], None, dram["kv"],
                        bass.IndirectOffsetOnAxis(ap=idx[:, turn[0], j:j + 1], axis=0)).then_inc(s_row[lane][j], 16)

            rows((0, None, 0), True)
            rows((1, None, 0), True)
            rows((2, None, 0))
            rows((3, None, 0))
            with pool.Fori(0, GROUPS // 4 - 1) as k:
                for r in range(4):
                    rows((r, k, 1))

        @block.vector
        def _(dve):
            v = nc.vector
            v.memset(wm[:, :, :, :], 0.0).then_inc(s_clear, 1)
            for i in range(ABUFS):
                v.memset(psa[i][:, :], 0.0).then_inc(s_clear, 1)
            dve.wait_ge(s_clear, 1 + ABUFS)

            def spread_of(turn, first=False):
                if not first:
                    pe_p.wait(dve, later(turn, -2), f"q{PAIRS - 1}")
                dve.wait_ge(*fill(s_rel, 2, turn))
                dve_p.tick(v.tensor_scalar(spread[:, turn[0] % 2, :], rel[:, turn[0] % 2, :],
                                           keep["part"][:, 0:1], None, ALU.is_equal), turn, "spread")

            def table(turn):
                lane, k, c = turn
                value = 48 * (c + 1)
                dve.wait_ge(s_table[lane], value if k is None else k * 48 + value)

            def body(turn, first=False, end=False):
                before = None if first else later(turn, -1)
                for what, m in WEAVE:
                    lane = turn[0] % 2
                    if what == "product":
                        pe_p.wait(dve, turn, f"q{m}")
                        for j in (2 * m, 2 * m + 1):
                            dve.wait_ge(*fill([s_row[0][j], s_row[1][j]], 2, turn))
                        k_rows = kv[:, lane, 2 * m:2 * m + 2, 0:D]
                        dve_p.tick(v.tensor_tensor(k_rows, k_rows, psq[m % QBUFS][:, :, :], ALU.mult),
                                   turn, f"product{m}")
                        if m == 0 and not end:
                            spread_of(later(turn, 1), first)
                    elif what == "score":
                        k_rows = kv[:, lane, 2 * m:2 * m + 2, 0:D]
                        dve_p.wait(dve, turn, f"product{m}")
                        dve_p.tick(v.tensor_reduce(
                            score[:, lane, 2 * m * H:2 * (m + 1) * H].rearrange("p (j h) -> p j h", h=H),
                            k_rows.rearrange("p j (h d) -> p j h d", h=H), AX.X, ALU.add), turn, f"score{m}")
                    elif what == "up":
                        if not first:
                            scan_up(before)
                    elif not first:
                        rest(before, what, m, is_first(before))

            def scan_up(turn):
                lane, k, c = turn
                n = 2 * c + lane // 2
                value = 32 * (n + 1)
                dve.wait_ge(s_flags[lane % 2], value if k is None else k * 64 + value)
                pe_p.wait(dve, turn, "score_t")
                dve_p.tick(v.tensor_tensor_scan(up[:, :], flags[:, lane % 2, 0, :], pst, -BIG, ALU.add, ALU.max),
                           turn, "up")

            def rest(turn, what, m, earliest=False):
                lane = turn[0] % 2
                if what == "top":
                    dve_p.wait(dve, turn, "up")
                    dve_p.tick(v.tensor_tensor_scan(top[:, ::-1], flags[:, lane, 1, ::-1], up[:, ::-1], -BIG,
                                                    ALU.add, ALU.max), turn, "top")
                elif what == "weigh":
                    table(turn)
                    pe_p.wait(dve, turn, "max_t")
                    dve_p.tick(v.tensor_tensor(below[:, :], score[:, lane, :], psm, ALU.subtract), turn, "below")
                    dve_p.tick(v.tensor_tensor(wm[:, lane, :, 32:ZM], psm.rearrange("p (j h) -> p j h", h=H),
                                               bc(last[:, turn[0], :].unsqueeze(2), [P, G, H]), ALU.mult),
                               turn, "maxima")
                elif what == "tail":
                    if not earliest:
                        pe_p.wait(dve, later(turn, -1), f"sums{2 * m + 1}")
                    at = 2 * m
                    dve_p.tick(v.tensor_tensor(sel[:, at:at + 2, :], bc(keep["cols"][:, :].unsqueeze(1), [P, 2, SELW]),
                                               bc(col[:, turn[0], 2 * m:2 * m + 2].unsqueeze(2), [P, 2, SELW]),
                                               ALU.is_equal), turn, f"sel{m}")
                    if m == 0:
                        act_p.wait(dve, turn, "weights")
                    values = kv[:, lane, 2 * m:2 * m + 2, D:KV].rearrange("p j (h d) -> p j h d", h=H)
                    dve_p.tick(v.tensor_tensor(values, values,
                                               bc(wm[:, lane, 2 * m:2 * m + 2, 0:H].unsqueeze(3), [P, 2, H, DH]),
                                               ALU.mult), turn, f"value{m}")

            spread_of((0, None, 0), True)
            groups_of(dve, body)
            scan_up((3, None, GROUPS // 4 - 1))
            for what, m in WEAVE:
                rest((3, None, GROUPS // 4 - 1), what, m)

        @block.tensor
        def _(pe):
            t = nc.tensor
            pe.wait_ge(s_clear, 1 + ABUFS)

            def q_at(turn, m):
                if m == 0:
                    lane, k, c = turn
                    value = 48 * (c + 1)
                    wait_beside(pe, s_clear, s_table[lane], value if k is None else k * 48 + value)
                at = [pe.value_load(regs[0:1, turn[0], 2 * j + 1:2 * j + 2], min_val=0, max_val=(BLOCKS - 1) * QC)
                      for j in (2 * m, 2 * m + 1)]
                return at

            def spread_q(turn, m, at, first=False):
                if m == 0:
                    dve_p.wait(pe, turn, "spread")
                if m >= QBUFS:
                    dve_p.wait(pe, turn, f"product{m - QBUFS}")
                elif not first:
                    dve_p.wait(pe, later(turn, -1), f"product{m + PAIRS - QBUFS}")
                for j in (2 * m, 2 * m + 1):
                    mm = t.matmul(psq[m % QBUFS][:, j % 2, :], spread[:, turn[0] % 2, j * P:(j + 1) * P],
                                  qc[:, bass.ds(at[j % 2], D)], start=True, stop=True)
                pe_p.tick(mm, turn, f"q{m}")

            def body(turn, first=False, end=False):
                for what, m in WEAVE:
                    owner, pair = (turn, m + QBUFS) if m + QBUFS < PAIRS else (later(turn, 1), m + QBUFS - PAIRS)
                    ahead, next_pair = (turn, pair + 1) if owner == turn and pair + 1 < PAIRS else \
                        (later(turn, 1), (pair + 1) % PAIRS)
                    if what == "product" and not (end and owner != turn):
                        if m == 0:
                            at = q_at(owner, pair)
                        spread_q(owner, pair, at)
                    elif what == "score" and m + 1 < PAIRS and not (end and ahead != turn):
                        at = q_at(ahead, next_pair)
                    elif what == "turn":
                        dve_p.wait(pe, turn, f"score{PAIRS - 1}", beside=s_clear)
                        pe_p.tick(t.transpose(pst, score[:, turn[0] % 2, :], keep["ident"][:, :]), turn, "score_t")
                    elif not first:
                        rest(later(turn, -1), what, m, is_first(later(turn, -1)))

            def rest(turn, what, m, earliest=False):
                lane = turn[0] % 2
                if what == "top":
                    dve_p.wait(pe, turn, "top", beside=s_clear)
                    pe_p.tick(t.transpose(psm, top[:, :], keep["ident"][0:G * H, 0:G * H]), turn, "max_t")
                elif what == "tail":
                    dve_p.wait(pe, turn, f"value{m}")
                    for j in (2 * m, 2 * m + 1):
                        if j >= ABUFS:
                            act_p.wait(pe, turn, f"ends{j - ABUFS}")
                        elif not earliest:
                            act_p.wait(pe, later(turn, -1), f"ends{j + G - ABUFS}")
                        one_hot = sel[:, j, :]
                        out = psa[j % ABUFS]
                        for half in range(2):
                            t.matmul(out[:, half * SELW:(half + 1) * SELW],
                                     kv[:, lane, j, D + half * P:D + (half + 1) * P], one_hot, start=True, stop=True)
                        pe_p.tick(t.matmul(out[0:ZM, 2 * SELW:3 * SELW], wm[:, lane, j, :], one_hot,
                                           start=True, stop=True), turn, f"sums{j}")

            for m in range(QBUFS):
                spread_q((0, None, 0), m, q_at((0, None, 0), m), True)
            groups_of(pe, body)
            for what, m in WEAVE:
                if what != "up":
                    rest((3, None, GROUPS // 4 - 1), what, m)

        @block.scalar
        def _(act):
            s = nc.scalar
            act.wait_ge(s_clear, 1 + ABUFS)

            def columns_at(turn, m):
                return [act.value_load(regs[0:1, turn[0], 2 * j:2 * j + 1], min_val=0, max_val=BLOCKS * P)
                        for j in (2 * m, 2 * m + 1)]

            def rest(turn, what, m, places, earliest=False):
                lane = turn[0] % 2
                if what == "top":
                    lane_, k, c = turn
                    value = 48 * (c + 1)
                    wait_beside(act, s_clear, s_table[lane_], value if k is None else k * 48 + value)
                    places[0] = columns_at(turn, 0)
                elif what == "weigh":
                    dve_p.wait(act, turn, "below")
                    act_p.tick(s.activation(wm[:, lane, :, 0:H], below[:, :].rearrange("p (j h) -> p j h", h=H),
                                            ACT.Exp, scale=SCALE), turn, "weights")
                elif what == "tail":
                    if m + 1 < PAIRS:
                        places[m + 1] = columns_at(turn, m + 1)
                    for j in (2 * m, 2 * m + 1):
                        at = places[m][j % 2]
                        if j > 0 or not earliest:
                            act_p.wait(act, turn if j else later(turn, -1), f"acc{(j - 1) % G}")
                        pe_p.wait(act, turn, f"sums{j}")
                        out = psa[j % ABUFS][:, 0:3 * SELW].rearrange("p (c n) -> p c n", c=3)
                        act_p.tick(s.copy(acc[:, :, bass.ds(at, P)], out[:, :, 0:P]), turn, f"acc{j}")
                        act_p.tick(s.copy(ends[:, :, bass.ds(number(turn, 2 * G) + 2 * j, 2)], out[:, :, P:SELW]),
                                   turn, f"ends{j}")

            def body(turn, first=False, end=False):
                if not first:
                    places = {}
                    for what, m in WEAVE:
                        rest(later(turn, -1), what, m, places, is_first(later(turn, -1)))

            groups_of(act, body)
            places = {}
            for what, m in WEAVE:
                rest((3, None, GROUPS // 4 - 1), what, m, places)


LANES = 4


def merge_ends(nc, layer, dram, keep):
    with Phase(nc) as ctx:
        def sb(name, shape, dt=F32):
            return ctx.enter_context(nc.sbuf_tensor(f"merge{layer}_{name}", shape, dt))

        def ps(name, shape, dt=F32):
            return ctx.enter_context(nc.psum_tensor(f"merge{layer}_{name}", shape, dt))

        def sem(name):
            return ctx.semaphore(f"merge{layer}_{name}")

        ends, qc, ident = keep["ends"], keep["qc"], keep["ident"]
        node = sb("node", [H, ENDS])
        opens = sb("opens", [H, ENDS])
        closes = sb("closes", [H, ENDS])
        m = sb("m", [H, ENDS])
        up = sb("up", [H, ENDS])
        closing = sb("closing", [H, ENDS])
        part = sb("part", [P, 2, QC - D + H])
        rows = sb("rows", [P, ETILES * QC])
        one_hot = sb("one_hot", [P, LANES, P])
        eregs = sb("eregs", [1, P, 2], I32)
        pt = [ps(f"t{i}", [P, 512]) for i in range(2)]
        pm = [ps(f"m{i}", [P, 512]) for i in range(LANES)]

        s_node = sem("node")
        s_regs = sem("regs")
        s_v = sem("dve")
        s_weight = sem("weight")
        s_turned = sem("turned")
        dve_p = Progress(nc, ctx, f"merge{layer}_dvep", LANES)
        pe_p = Progress(nc, ctx, f"merge{layer}_pep", LANES)
        dve_p.begin(["one_hot", "added"])
        pe_p.begin(["summed"])
        count = {"n": 0, "at": {}}
        block = ctx.enter_context(nc.Block())

        def pairs_of(eng, body):
            body([(lane, None, 0) for lane in range(LANES)])
            body([(0, None, 1)])
            with eng.Fori(1, MERGES // LANES) as k:
                body([(1, k, 0), (2, k, 0), (3, k, 0), (0, k, 1)])

        def number(turn):
            lane, k, c = turn
            return LANES * c + lane if k is None else k * LANES + (LANES * c + lane)

        assert MERGES % LANES == 1

        @block.sync
        def _(sp):
            sp.dma_start(node[:, :], dram["ends"][0:ENDS].partition_broadcast(H)).then_inc(s_node, 16)
            sp.dma_start(eregs[:, :, :], dram["eregs"].rearrange("(o p) w -> o p w", o=1)).then_inc(s_regs, 16)

        @block.vector
        def _(dve):
            v = nc.vector

            def link(ins, name=None):
                ins.then_inc(s_v, 1)
                count["n"] += 1
                if name:
                    count["at"][name] = count["n"]
                dve.wait_ge(s_v, count["n"])

            link(v.memset(qc[:, :], 0.0))
            link(v.tensor_copy(m[:, :], ends[32:32 + H, 2, :]))
            link(v.memset(opens[:, 0:1], 0.0))
            link(v.memset(closes[:, ENDS - 1:ENDS], 0.0))
            dve.wait_ge(s_node, 16)
            link(v.tensor_tensor(opens[:, 1:ENDS], node[:, 1:ENDS], node[:, 0:ENDS - 1], ALU.not_equal))
            link(v.tensor_copy(closing[:, 0:ENDS - 1], opens[:, 1:ENDS]))
            link(v.memset(closing[:, ENDS - 1:ENDS], 1.0))
            link(v.tensor_scalar(opens[:, 1:ENDS], opens[:, 1:ENDS], -BIG, None, ALU.mult))
            link(v.tensor_copy(closes[:, 0:ENDS - 1], opens[:, 1:ENDS]))
            link(v.tensor_scalar(up[:, :], ends[0:H, 2, :], 0.5, -BIG, ALU.is_lt, ALU.mult))
            link(v.tensor_tensor(m[:, :], m[:, :], up[:, :], ALU.add))
            link(v.tensor_tensor_scan(up[:, :], opens[:, :], m[:, :], -BIG, ALU.add, ALU.max))
            link(v.tensor_tensor_scan(opens[:, ::-1], closes[:, ::-1], up[:, ::-1], -BIG, ALU.add, ALU.max))
            link(v.tensor_tensor(m[:, :], m[:, :], opens[:, :], ALU.subtract), "below")
            link(v.tensor_tensor(closing[:, :], closing[:, :], opens[:, :], ALU.mult), "closing")
            dve.wait_ge(s_weight, 1)
            for u in range(ETILES):
                dve.wait_ge(s_turned, u + 1)
                out = rows[:, u * QC:(u + 1) * QC]
                t = pt[u % 2]
                link(v.tensor_copy(part[:, u % 2, :], t[:, D:D + 3 * H]))
                weight = bc(part[:, u % 2, 2 * H:3 * H].unsqueeze(2), [P, H, DH])
                v.tensor_tensor(out[:, 0:D].rearrange("p (h d) -> p h d", h=H),
                                t[:, 0:D].rearrange("p (h d) -> p h d", h=H), weight, ALU.mult).then_inc(s_v, 1)
                v.tensor_tensor(out[:, D:D + H], part[:, u % 2, 0:H], part[:, u % 2, 2 * H:3 * H], ALU.mult)\
                    .then_inc(s_v, 1)
                count["n"] += 2
                link(v.tensor_copy(out[:, D + H:QC], part[:, u % 2, H:2 * H]), f"row{u}")

            def body(turns):
                for turn in turns:
                    pe_p.wait_turn(dve, turn)
                    dve_p.tick(v.tensor_scalar(one_hot[:, turn[0], :], keep["cols"][:, 0:P],
                                               keep["ecol"][:, bass.ds(number(turn), 1)], None, ALU.is_equal),
                               turn, "one_hot")
                places = [dve.value_load(eregs[0:1, bass.ds(number(turn), 1), 1:2], min_val=0,
                                         max_val=(BLOCKS - 1) * QC) for turn in turns]
                for turn, at in zip(turns, places):
                    lane = turn[0]
                    pe_p.wait(dve, turn, "summed")
                    place = qc[:, bass.ds(at, QC)]
                    if lane or turn[2]:
                        dve_p.wait(dve, (lane - 1, *turn[1:]) if lane else (LANES - 1, turn[1], turn[2] - 1), "added")
                    dve_p.tick(v.tensor_tensor(place, place, pm[lane][:, 0:QC], ALU.add), turn, "added")

            dve.wait_ge(s_regs, 16)
            pairs_of(dve, body)

        at = count["at"]

        @block.scalar
        def _(act):
            act.wait_ge(s_v, at["below"])
            nc.scalar.activation(up[:, :], m[:, :], ACT.Exp, scale=SCALE).then_inc(s_weight, 1)

        @block.tensor
        def _(pe):
            t = nc.tensor
            pe.wait_ge(s_weight, 1)
            pe.wait_ge(s_v, at["closing"])
            for u in range(ETILES):
                if u >= 2:
                    pe.wait_ge(s_v, at[f"row{u - 2}"])
                cut = slice(u * P, (u + 1) * P)
                t.transpose(pt[u % 2][:, 0:P], ends[:, 0, cut], ident[:, :])
                t.transpose(pt[u % 2][:, P:D], ends[:, 1, cut], ident[:, :])
                for i, row in enumerate((ends[0:H, 2, cut], closing[:, cut], up[:, cut])):
                    mm = t.transpose(pt[u % 2][:, D + i * H:D + (i + 1) * H], row, ident[0:H, 0:H])
                mm.then_inc(s_turned, 1)
            pe.wait_ge(s_v, at[f"row{ETILES - 1}"])
            pe.wait_ge(s_regs, 16)

            def body(turns):
                tiles = [pe.value_load(eregs[0:1, bass.ds(number(turn), 1), 0:1], min_val=0, max_val=(ETILES - 1) * QC)
                         for turn in turns]
                for turn, at_ in zip(turns, tiles):
                    lane = turn[0]
                    dve_p.wait(pe, turn, "one_hot")
                    pe_p.tick(t.matmul(pm[lane][:, 0:QC], one_hot[:, lane, :], rows[:, bass.ds(at_, QC)],
                                       start=True, stop=True), turn, "summed")

            pairs_of(pe, body)


RSQRT_GUESS = 0x5F3759DF
NEWTON = 3
ZPAD = 64
ZBANK = 8
BANK = 4
ROLES = {"next": 1, "new": 0, "old": -1, "older": -2}
WEAVES = {
    "first": (("older", "qkv"), ("new", "norm_in"), ("new", "project"), ("old", "project_in"),
              ("old", "norm_q"), ("older", "qkv_out")),
    "middle": (("new", "merge"), ("new", "turn_agg"), ("new", "h_b"), ("old", "h_b2"), ("older", "qkv"),
               ("older", "qkv_out"), ("new", "attend"),
               ("old", "ffn_2"), ("new", "attended"), ("next", "sums_t"), ("new", "norm_ff"), ("new", "ffn_1"),
               ("old", "ffn_out"), ("old", "norm_q"), ("new", "ffn_1b")),
    "last": (("new", "merge"), ("new", "turn_agg"), ("new", "h_b"), ("old", "h_b2"), ("older", "out_1"), ("older", "gate"), ("older", "out_1b"),
             ("new", "attend"), ("older", "out_2"), ("old", "ffn_2"), ("new", "attended"), ("next", "sums_t"),
             ("new", "norm_ff"), ("older", "y_out"), ("new", "ffn_1"), ("old", "ffn_out"), ("old", "norm_out"),
             ("new", "ffn_1b")),
}


class RoleProgress:

    def __init__(self, nc, ctx, name, weave, steps):
        self.of = {}
        for role in ROLES:
            mine = [s for which, stage in weave if which == role for s in steps.get(stage, ())]
            if mine:
                progress = Progress(nc, ctx, f"{name}_{role}", 2)
                progress.begin(mine)
                self.of.update({s: progress for s in mine})

    def wait(self, eng, turn, step, beside=None):
        self.of[step].wait(eng, turn, step, beside)

    def tick(self, ins, turn, step):
        return self.of[step].tick(ins, turn, step)


def node_pass(nc, kind, a, dram, keep):
    weave = WEAVES[kind]
    layer = 0 if kind != "last" else 1
    nxt = 0 if kind == "first" else 1
    with Phase(nc) as ctx:
        def sb(name, shape, dt=F32):
            return ctx.enter_context(nc.sbuf_tensor(f"{kind}_{name}", shape, dt))

        def ps(name, shape, dt=F32):
            return ctx.enter_context(nc.psum_tensor(f"{kind}_{name}", shape, dt))

        def sem(name):
            return ctx.semaphore(f"{kind}_{name}")

        acc, qc, ident, self_ = keep["acc"], keep["qc"], keep["ident"], keep["self"]
        x = sb("x", [P, 2, D])
        h = sb("h", [P, 2, D])
        xn = sb("xn", [P, 2, D])
        xt = sb("xt", [P, 2, D])
        st = sb("st", [P, 2, 6])
        mv = sb("mv", [P, 2, 2])
        var = sb("var", [P, 2, 1])
        minus_half = sb("minus_half", [P, 2, 1])
        half_bits = sb("half_bits", [P, 2, 1], I32)
        yy = sb("yy", [P, 2, 1])
        rs = sb("rs", [P, 2, 1])
        tmp = sb("tmp", [P, 2, D])
        pt = [ps(f"pt{i}", [P, 512]) for i in range(2)]
        sums = [ps(f"sums{i}", [P, 512]) for i in range(2)]
        ph = [ps(f"ph{i}", [P, 1024]) for i in range(2)]
        loads = []

        def col_of(name, vec):
            n = vec.shape[0] // P
            t = sb(name, [P, n])
            loads.append((t[:, :], vec.rearrange("(c p) -> p c", p=P)))
            return t

        def row_of(name, vec, into=None):
            n = vec.shape[0]
            t = sb(name, [P, n]) if into is None else into
            loads.append((t[:, 0:n] if into is None else into, vec.partition_broadcast(P)))
            return t

        def mat_of(name, mat, into=None):
            c = mat.shape[0] // P
            t = sb(name, [P, c, mat.shape[1]])[:, :, :] if into is None else into
            loads.append((t, mat.rearrange("(c p) n -> p c n", p=P)))
            return t

        if kind == "first":
            w_in = mat_of("w_in", a["L0_gnn_w_in"])
            b_in = row_of("b_in", a["L0_gnn_b_in"])
        if kind != "last":
            w_qkv = sb("w_qkv", [P, 2, 3 * D])
            b_qkv = sb("b_qkv", [P, 3 * D])
            for i, n in enumerate("qkv"):
                mat_of("", a[f"L0_gnn_w{n}"][nxt], w_qkv[:, :, i * D:(i + 1) * D])
                row_of("", a[f"L0_gnn_b{n}"][nxt], b_qkv[:, i * D:(i + 1) * D])
            g1 = col_of("g1", a["L0_gnn_ln1_g"][nxt])
            b1n = col_of("b1n", a["L0_gnn_ln1_b"][nxt])
            kv_out = sb("kv_out", [P, 2, KV])
        if kind != "first":
            w_o = mat_of("w_o", a["L0_gnn_wo"][layer])
            b_o = row_of("b_o", a["L0_gnn_bo"][layer])
            w_1 = mat_of("w_1", a["L0_gnn_w1"][layer])
            b_1 = col_of("b_1", a["L0_gnn_b1"][layer])
            w_2 = mat_of("w_2", a["L0_gnn_w2"][layer])
            b_2 = row_of("b_2", a["L0_gnn_b2"][layer])
            g2 = col_of("g2", a["L0_gnn_ln2_g"][layer])
            b2n = col_of("b2n", a["L0_gnn_ln2_b"][layer])
            h_in = sb("h_in", [P, 2, D])
            v_in = sb("v_in", [P, 2, D])
            agg_x = sb("agg_x", [P, D])
            ab = sb("ab", [P, 2, 2, P])
            agg = sb("agg", [P, 2, D])
            zm = sb("zm", [P, BLOCKS, 2, H])
            mx = sb("mx", [P, BLOCKS, H])
            has = sb("has", [P, BLOCKS, H])
            ee = sb("ee", [P, BLOCKS, 2, H])
            hid = sb("hid", [P, 2, FF])
        if kind == "last":
            f_1 = mat_of("f_1", a["L0_ffn_w1"])
            f_b1 = col_of("f_b1", a["L0_ffn_b1"])
            f_2 = mat_of("f_2", a["L0_ffn_w2"])
            f_b2 = row_of("f_b2", a["L0_ffn_b2"])
            w_r = row_of("w_r", a["L0_ffn_wr"].rearrange("d o -> (d o)"))
            b_r = row_of("b_r", a["L0_ffn_br"])
            gate = sb("gate", [P, 2, 1])
            scratch = sb("scratch", [P, D])

        s_weights = sem("weights")
        s_turned = sem("turned")
        s_factors = sem("factors")
        s_exp = sem("exp")
        s_zero = sem("zero")
        s_x = [sem(f"x{i}") for i in range(2)]
        s_h = [sem(f"h{i}") for i in range(2)]
        s_v = [sem(f"v{i}") for i in range(2)]
        s_hout = [sem(f"h_out{i}") for i in range(2)]
        s_kvout = [sem(f"kv_out{i}") for i in range(2)]

        def norm_steps(tag):
            return [f"{tag}_{s}" for s in
                    ["stats", "moments", "var", "minus_half", "bits", "guess"] +
                    [f"{x}{n}" for n in range(NEWTON) for x in ("square", "newton")] + ["normed"]]

        dve_steps = {
            "norm_in": norm_steps("in"), "project_in": ["h"], "norm_q": norm_steps("q"),
            "qkv_out": ["kv", "q", "qk", "self"],
            "h_b": ["h_b"], "h_b2": ["h_b2"] + (["h_x"] if kind == "last" else []),
            "merge": ["agg", "agg_scaled", "v_scaled", "merged"],
            "attended": ["attended"],
            "norm_ff": norm_steps("ff"),
            "ffn_out": ["ffn"], "norm_out": norm_steps("out"),
            "gate": ["weighed", "base", "gate0", "gate", "gate_kept"], "y_out": ["y_b", "y"],
        }
        pe_steps = {
            "norm_in": ["in_t"], "project": ["in_p"], "norm_q": ["q_t"], "qkv": ["qkv"],
            "sums_t": ["acc_t"], "turn_agg": ["agg_t"], "attend": ["attend"], "norm_ff": ["ff_t"],
            "ffn_1": ["ffn_1_0"], "ffn_1b": ["ffn_1_1"], "ffn_2": ["ffn_2"],
            "norm_out": ["out_t"], "out_1": ["out_1_0"], "out_1b": ["out_1_1"], "out_2": ["out_2"],
        }
        act_steps = {
            "norm_in": ["in_x"], "norm_q": ["q_x0", "q_x"],
            "sums_t": ["acc"], "turn_agg": ["agg_x"], "norm_ff": ["ff_x0", "ff_x"],
            "ffn_1": [f"gelu{i}" for i in range(BANK)], "ffn_1b": [f"gelu{i}" for i in range(BANK, FF // P)],
            "norm_out": ["out_x"],
            "out_1": [f"gelu_out{i}" for i in range(BANK)], "out_1b": [f"gelu_out{i}" for i in range(BANK, FF // P)],
        }
        dve_p = RoleProgress(nc, ctx, f"{kind}_dve", weave, dve_steps)
        pe_p = RoleProgress(nc, ctx, f"{kind}_pe", weave, pe_steps)
        act_p = RoleProgress(nc, ctx, f"{kind}_act", weave, act_steps)

        def later(turn, n):
            lane, k, c = turn
            b = 2 * c + lane + n
            return (b % 2, k, b // 2)

        def exists(turn):
            return turn[1] is not None or 0 <= 2 * turn[2] + turn[0] < BLOCKS

        def woven(do, turn):
            for role, stage in weave:
                if exists(later(turn, ROLES[role])):
                    do(later(turn, ROLES[role]), stage)

        def blocks_of(eng, do):
            for b in range(-1, 4):
                woven(do, later((0, None, 0), b))
            with eng.Fori(2, BLOCKS // 2) as k:
                for lane in range(2):
                    woven(do, (lane, k, 0))
            for b in range(BLOCKS - 1, BLOCKS + 2):
                woven(do, later((0, None, 0), b))

        assert BLOCKS % 2 == 1

        def number(turn, scale=1):
            lane, k, c = turn
            b = (2 * c + lane) * scale
            return b if k is None else k * (2 * scale) + b

        def landed(eng, sems, turn, beside=None):
            lane, k, c = turn
            value = 16 * (c + 1) if k is None else k * 16 + 16 * (c + 1)
            if beside is None:
                eng.wait_ge(sems[lane], value)
            else:
                wait_beside(eng, beside, sems[lane], value)

        def stored_before(eng, sems, turn):
            lane, k, c = turn
            if k is not None or c > 0:
                eng.wait_ge(sems[lane], 16 * c if k is None else k * 16 + 16 * c)

        def z_bank(b0):
            bank = b0 // ZBANK
            if bank < 4:
                return ph[bank // 2][:, (bank % 2) * 512:(bank % 2) * 512 + 512]
            return (pt[0], pt[1], sums[0])[bank - 4][:, :]

        assert ZBANK * ZPAD <= 512 and BLOCKS <= 7 * ZBANK
        before_exp = -(-BLOCKS // ZBANK) + 4

        block = ctx.enter_context(nc.Block())

        @block.sync
        def _(sp):
            def load(turn, first=False, rows=P):
                lane = turn[0]
                before = later(turn, -2)
                at = bass.ds(number(turn, P), rows)
                full = bass.ds(number(turn, P), P)
                if kind != "middle":
                    if not first:
                        dve_p.wait(sp, before, "in_normed" if kind == "first" else "h_x", beside=s_zero)
                    sp.dma_start(x[0:rows, lane, :], a["x"][at, :]).then_inc(s_x[lane], 16)
                if kind != "first":
                    if not first:
                        dve_p.wait(sp, before, "merged", beside=s_zero)
                        dve_p.wait(sp, before, "h_b", beside=s_zero)
                    sp.dma_start(h_in[:, lane, :], dram["h"][full, :]).then_inc(s_h[lane], 16)
                    sp.dma_start(v_in[:, lane, :], dram["kv"][full, D:KV]).then_inc(s_v[lane], 16)

            def store_h(turn):
                lane = turn[0]
                dve_p.wait(sp, turn, "h" if kind == "first" else "ffn", beside=s_zero)
                sp.dma_start(dram["h"][bass.ds(number(turn, P), P), :], h[:, lane, :]).then_inc(s_hout[lane], 16)

            def store_kv(turn):
                lane = turn[0]
                dve_p.wait(sp, turn, "kv", beside=s_zero)
                sp.dma_start(dram["kv"][bass.ds(number(turn, P), P), :], kv_out[:, lane, :])\
                    .then_inc(s_kvout[lane], 16)

            def one(turn, b=None):
                if exists(later(turn, 1)):
                    load(later(turn, 1), first=b is not None and b < 1, rows=LAST if b == BLOCKS - 2 else P)
                if kind != "last":
                    if exists(later(turn, -1)):
                        store_h(later(turn, -1))
                    if exists(later(turn, -2)):
                        store_kv(later(turn, -2))

            sp.wait_ge(s_zero, 1)
            for b in range(-1, 4):
                one(later((0, None, 0), b), b)
            with sp.Fori(2, BLOCKS // 2 - 1) as k:
                for lane in range(2):
                    one((lane, k, 0))
            for b in range(BLOCKS - 3, BLOCKS + 2):
                one(later((0, None, 0), b), b)
            if kind != "last":
                for s in (s_hout, s_kvout):
                    landed(sp, s, (0, None, BLOCKS // 2))
                    landed(sp, s, (1, None, BLOCKS // 2 - 1))

        @block.gpsimd
        def _(pool):
            with nc.allow_non_contiguous_dma(reason="biases and gains as columns"):
                for tile_, source in loads:
                    pool.dma_start(tile_, source).then_inc(s_weights, 16)

        @block.vector
        def _(dve):
            v = nc.vector

            def step(ins, turn, name):
                dve_p.tick(ins, turn, name)
                dve_p.wait(dve, turn, name)

            def norm(turn, rows, tag):
                i = turn[0]
                dve_p.tick(v.bn_stats(out=st[:, i, :], in_=rows), turn, f"{tag}_stats")
                dve_p.wait(dve, turn, f"{tag}_stats", beside=s_weights)
                step(v.bn_aggr(out=mv[:, i, :], in_=st[:, i, :]), turn, f"{tag}_moments")
                dve_p.tick(v.tensor_scalar(var[:, i, :], mv[:, i, 1:2], EPS, None, ALU.add), turn, f"{tag}_var")
                step(v.tensor_scalar(minus_half[:, i, :], mv[:, i, 1:2], EPS, -0.5, ALU.add, ALU.mult),
                     turn, f"{tag}_minus_half")
                step(v.tensor_single_scalar(half_bits[:, i, :], var[:, i, :].bitcast(I32), 1,
                                            op=ALU.logical_shift_right), turn, f"{tag}_bits")
                step(v.tensor_scalar(rs[:, i, :].bitcast(I32), half_bits[:, i, :], -1.0, float(RSQRT_GUESS),
                                     ALU.mult, ALU.add), turn, f"{tag}_guess")
                for n in range(NEWTON):
                    step(v.scalar_tensor_tensor(out=yy[:, i, :], in0=rs[:, i, :], scalar=minus_half[:, i, 0:1],
                                                in1=rs[:, i, :], op0=ALU.mult, op1=ALU.mult),
                         turn, f"{tag}_square{n}")
                    step(v.scalar_tensor_tensor(out=rs[:, i, :], in0=yy[:, i, :], scalar=1.5, in1=rs[:, i, :],
                                                op0=ALU.add, op1=ALU.mult), turn, f"{tag}_newton{n}")
                step(v.tensor_scalar(xn[:, i, :], rows, mv[:, i, 0:1], rs[:, i, 0:1], ALU.subtract, ALU.mult),
                     turn, f"{tag}_normed")

            def heads(ap):
                return ap.rearrange("p (h d) -> p h d", h=H)

            def per_head(ap):
                return bc(ap.unsqueeze(2), [P, H, DH])

            def do(turn, stage):
                i = turn[0]
                xi, hi, prod = x[:, i, :], h[:, i, :], pt[i][:, D:2 * D]
                if stage == "norm_in":
                    landed(dve, s_x, turn)
                    if exists(later(turn, -2)):
                        pe_p.wait(dve, later(turn, -2), "q_t")
                    norm(turn, xi, "in")
                elif stage == "project_in":
                    stored_before(dve, s_hout, turn)
                    pe_p.wait(dve, turn, "in_p")
                    step(v.tensor_tensor(hi, prod, b_in[:, :], ALU.add), turn, "h")
                elif stage == "norm_q":
                    norm(turn, hi, "q")
                elif stage == "qkv_out":
                    pe_p.wait(dve, turn, "qkv")
                    stored_before(dve, s_kvout, turn)
                    q = qc[:, bass.ds(number(turn, QC), D)]
                    dve_p.tick(v.tensor_tensor(kv_out[:, i, :], ph[i][:, D:3 * D], b_qkv[:, D:3 * D], ALU.add),
                               turn, "kv")
                    step(v.tensor_tensor(q, ph[i][:, 0:D], b_qkv[:, 0:D], ALU.add), turn, "q")
                    dve_p.tick(v.tensor_tensor(tmp[:, i, :], q, kv_out[:, i, 0:D], ALU.mult), turn, "qk")
                    dve_p.wait(dve, turn, "qk", beside=s_weights)
                    step(v.tensor_reduce(self_[:, bass.ds(number(turn, H), H)], heads(tmp[:, i, :]), AX.X, ALU.add),
                         turn, "self")
                elif stage == "merge":
                    pe_p.wait(dve, turn, "acc_t")
                    step(v.tensor_tensor(agg[:, i, :], sums[i][:, 0:D], qc[:, bass.ds(number(turn, QC), D)], ALU.add),
                         turn, "agg")
                    landed(dve, s_v, turn)
                    by = zm[:, :, :, :].rearrange("p b c h -> p (b c h)")
                    by_sum = by[:, bass.ds(number(turn, 2 * H), H)]
                    by_own = by[:, bass.ds(number(turn, 2 * H) + H, H)]
                    dve_p.tick(v.tensor_tensor(heads(agg[:, i, :]), heads(agg[:, i, :]), per_head(by_sum), ALU.mult),
                               turn, "agg_scaled")
                    step(v.tensor_tensor(heads(v_in[:, i, :]), heads(v_in[:, i, :]), per_head(by_own), ALU.mult),
                         turn, "v_scaled")
                    step(v.tensor_tensor(agg[:, i, :], agg[:, i, :], v_in[:, i, :], ALU.add), turn, "merged")
                elif stage == "h_b":
                    landed(dve, s_h, turn)
                    if kind == "middle":
                        stored_before(dve, s_hout, turn)
                    dve_p.tick(v.tensor_tensor(hi, h_in[:, i, :], b_o[:, :], ALU.add), turn, "h_b")
                elif stage == "h_b2":
                    step(v.tensor_tensor(hi, hi, b_2[:, :], ALU.add), turn, "h_b2")
                    if kind == "last":
                        landed(dve, s_x, turn)
                        dve_p.tick(v.tensor_tensor(hi, hi, xi, ALU.add), turn, "h_x")
                elif stage == "attended":
                    dve_p.wait(dve, turn, "h_b")
                    pe_p.wait(dve, turn, "attend")
                    step(v.tensor_tensor(hi, hi, prod, ALU.add), turn, "attended")
                elif stage == "norm_ff":
                    norm(turn, hi, "ff")
                elif stage == "ffn_out":
                    pe_p.wait(dve, turn, "ffn_2")
                    if kind == "last":
                        dve_p.wait(dve, turn, "h_x")
                        step(v.tensor_tensor(tmp[:, i, :], hi, prod, ALU.add), turn, "ffn")
                    else:
                        step(v.tensor_tensor(hi, hi, prod, ALU.add), turn, "ffn")
                elif stage == "norm_out":
                    norm(turn, tmp[:, i, :], "out")
                elif stage == "gate":
                    dve_p.tick(v.tensor_tensor(scratch[:, :], xn[:, i, :], w_r[:, :], ALU.mult), turn, "weighed")
                    dve_p.tick(v.tensor_tensor(qc[:, bass.ds(number(turn, QC), D)], tmp[:, i, :], xn[:, i, :],
                                               ALU.add), turn, "base")
                    dve_p.wait(dve, turn, "weighed")
                    step(v.tensor_reduce(gate[:, i, :], scratch[:, :], AX.X, ALU.add), turn, "gate0")
                    step(v.tensor_tensor(gate[:, i, :], gate[:, i, :], b_r[:, :], ALU.add), turn, "gate")
                    dve_p.tick(v.tensor_copy(keep["gates"][:, bass.ds(number(turn), 1)], gate[:, i, :]),
                               turn, "gate_kept")
                elif stage == "y_out":
                    pe_p.wait(dve, turn, "out_2")
                    step(v.tensor_tensor(scratch[:, :], sums[i][:, 0:D], f_b2[:, :], ALU.add), turn, "y_b")
                    step(v.tensor_scalar(acc[:, 0:2, bass.ds(number(turn, P), P)],
                                         scratch[:, :].rearrange("p (c n) -> p c n", c=2), gate[:, i, 0:1], None,
                                         ALU.mult), turn, "y")

            done = [0]

            def factor(ins, wait=True):
                ins.then_inc(s_factors, 1)
                done[0] += 1
                if wait:
                    dve.wait_ge(s_factors, done[0])

            def factors():
                ends = qc[:, :].rearrange("p (b n) -> p b n", n=QC)[:, :, D:D + 2 * H]
                own = self_[:, :].rearrange("p (b h) -> p b h", h=H)
                dve.wait_ge(s_turned, 1)
                for b0 in range(0, BLOCKS, ZBANK):
                    n = min(ZBANK, BLOCKS - b0)
                    turned = z_bank(b0)[:, 0:n * ZPAD].rearrange("p (b c n) -> p b c n", c=2, n=ZPAD // 2)
                    factor(v.tensor_tensor(zm[:, b0:b0 + n, :, :], turned[:, :, :, 0:H],
                                           ends[:, b0:b0 + n, :].rearrange("p b (c h) -> p b c h", c=2), ALU.add),
                           b0 + n == BLOCKS)
                z, m = zm[:, :, 0, :], zm[:, :, 1, :]
                factor(v.tensor_tensor(mx[:, :, :], own, m, ALU.max), wait=False)
                factor(v.tensor_scalar(has[:, :, :], z, 0.5, None, ALU.is_ge))
                factor(v.tensor_tensor(ee[:, :, 0, :], m, mx[:, :, :], ALU.subtract), wait=False)
                factor(v.tensor_tensor(ee[:, :, 1, :], own, mx[:, :, :], ALU.subtract))
                dve.wait_ge(s_exp, 1)
                factor(v.tensor_tensor(mx[:, :, :], z, ee[:, :, 0, :], ALU.mult))
                factor(v.tensor_tensor(mx[:, :, :], mx[:, :, :], ee[:, :, 1, :], ALU.add))
                factor(v.reciprocal(mx[:, :, :], mx[:, :, :]))
                factor(v.tensor_tensor(mx[:, :, :], mx[:, :, :], has[:, :, :], ALU.mult))
                factor(v.tensor_tensor(zm[:, :, 0, :], ee[:, :, 0, :], mx[:, :, :], ALU.mult), wait=False)
                factor(v.tensor_tensor(zm[:, :, 1, :], ee[:, :, 1, :], mx[:, :, :], ALU.mult))

            v.memset(x[:, :, :], 0.0).then_inc(s_zero, 1)
            if kind != "first":
                factors()
            dve.wait_ge(s_weights, 16 * len(loads))
            blocks_of(dve, do)

        @block.tensor
        def _(pe):
            t = nc.tensor

            def turn_rows(turn, rows, name):
                for half in range(2):
                    mm = t.transpose(pt[turn[0]][:, half * P:(half + 1) * P], rows[:, half * P:(half + 1) * P],
                                     ident[:, :])
                pe_p.tick(mm, turn, name)

            def project(turn, rows_t, w, name):
                for half in range(2):
                    mm = t.matmul(pt[turn[0]][:, D:2 * D], rows_t[:, half * P:(half + 1) * P], w[:, half, :],
                                  start=(half == 0), stop=(half == 1))
                pe_p.tick(mm, turn, name)

            def hidden(turn, w, name, bank):
                i = turn[0]
                for c in range(bank * BANK, (bank + 1) * BANK):
                    for half in range(2):
                        mm = t.matmul(ph[i][:, c * P:(c + 1) * P], w[:, half, c * P:(c + 1) * P],
                                      xt[:, i, half * P:(half + 1) * P], start=(half == 0), stop=(half == 1))
                pe_p.tick(mm, turn, f"{name}_{bank}")

            def output(turn, w, name, gelu, out):
                for c in range(FF // P):
                    act_p.wait(pe, turn, f"{gelu}{c}")
                    mm = t.matmul(out, hid[:, turn[0], c * P:(c + 1) * P], w[:, c, :],
                                  start=(c == 0), stop=(c == FF // P - 1))
                pe_p.tick(mm, turn, name)

            def do(turn, stage):
                i = turn[0]
                if stage in ("norm_in", "norm_q", "norm_ff", "norm_out"):
                    tag = stage[5:]
                    dve_p.wait(pe, turn, f"{tag}_normed")
                    turn_rows(turn, xn[:, i, :], f"{tag}_t")
                elif stage == "project":
                    act_p.wait(pe, turn, "in_x")
                    project(turn, xt[:, i, :], w_in, "in_p")
                elif stage == "qkv":
                    act_p.wait(pe, turn, "q_x")
                    for at, n in ((0, 512), (512, D)):
                        for half in range(2):
                            mm = t.matmul(ph[i][:, at:at + n], xt[:, i, half * P:(half + 1) * P],
                                          w_qkv[:, half, at:at + n], start=(half == 0), stop=(half == 1))
                    pe_p.tick(mm, turn, "qkv")
                elif stage == "sums_t":
                    act_p.wait(pe, turn, "acc", beside=s_weights)
                    if exists(later(turn, -2)):
                        dve_p.wait(pe, later(turn, -2), "agg", beside=s_weights)
                    if kind == "last" and exists(later(turn, -4)):
                        dve_p.wait(pe, later(turn, -4), "y_b", beside=s_weights)
                    for half in range(2):
                        mm = t.transpose(sums[i][:, half * P:(half + 1) * P], ab[:, i, half, :], ident[:, :])
                    pe_p.tick(mm, turn, "acc_t")
                elif stage == "turn_agg":
                    if exists(later(turn, -2)):
                        act_p.wait(pe, later(turn, -2), "q_x" if kind == "middle" else "out_x")
                    dve_p.wait(pe, turn, "merged")
                    turn_rows(turn, agg[:, i, :], "agg_t")
                elif stage == "attend":
                    act_p.wait(pe, turn, "agg_x")
                    project(turn, agg_x, w_o, "attend")
                elif stage == "ffn_1":
                    act_p.wait(pe, turn, "ff_x")
                    hidden(turn, w_1, "ffn_1", 0)
                elif stage == "ffn_1b":
                    hidden(turn, w_1, "ffn_1", 1)
                elif stage == "ffn_2":
                    output(turn, w_2, "ffn_2", "gelu", pt[i][:, D:2 * D])
                elif stage == "out_1":
                    act_p.wait(pe, turn, "out_x")
                    hidden(turn, f_1, "out_1", 0)
                elif stage == "out_1b":
                    hidden(turn, f_1, "out_1", 1)
                elif stage == "out_2":
                    if exists(later(turn, 2)):
                        dve_p.wait(pe, later(turn, 2), "agg")
                    output(turn, f_2, "out_2", "gelu_out", sums[i][:, 0:D])

            if kind != "first":
                for b in range(BLOCKS):
                    at = (b % ZBANK) * ZPAD
                    mm = t.transpose(z_bank(b)[:, at:at + ZM], acc[0:ZM, 2, b * P:(b + 1) * P], ident[0:ZM, 0:ZM])
                mm.then_inc(s_turned, 1)
            pe.wait_ge(s_weights, 16 * len(loads))
            if kind != "first":
                pe.wait_ge(s_factors, -(-BLOCKS // ZBANK))
            blocks_of(pe, do)

        @block.scalar
        def _(act):
            s = nc.scalar

            def do(turn, stage):
                i = turn[0]
                if stage in ("norm_in", "norm_out", "turn_agg"):
                    tag = {"norm_in": "in", "norm_out": "out", "turn_agg": "agg"}[stage]
                    pe_p.wait(act, turn, f"{tag}_t")
                    act_p.tick(s.copy(agg_x[:, :] if tag == "agg" else xt[:, i, :], pt[i][:, 0:D]), turn, f"{tag}_x")
                elif stage in ("norm_q", "norm_ff"):
                    tag, g, b = ("q", g1, b1n) if stage == "norm_q" else ("ff", g2, b2n)
                    pe_p.wait(act, turn, f"{tag}_t")
                    for half in range(2):
                        cut = slice(half * P, (half + 1) * P)
                        act_p.tick(s.activation(xt[:, i, cut], pt[i][:, cut], ACT.Identity,
                                                bias=b[:, half:half + 1], scale=g[:, half:half + 1]),
                                   turn, f"{tag}_x" if half else f"{tag}_x0")
                elif stage == "sums_t":
                    if exists(later(turn, -2)):
                        pe_p.wait(act, later(turn, -2), "acc_t")
                    act_p.tick(s.copy(ab[:, i, :, :], acc[:, 0:2, bass.ds(number(turn, P), P)]), turn, "acc")
                elif stage in ("ffn_1", "ffn_1b", "out_1", "out_1b"):
                    pe_name, name, func, bias = (("ffn_1", "gelu", ACT.Gelu, b_1) if stage in ("ffn_1", "ffn_1b") else
                                                 ("out_1", "gelu_out", ACT.Gelu_apprx_tanh, f_b1))
                    bank = 1 if stage in ("ffn_1b", "out_1b") else 0
                    pe_p.wait(act, turn, f"{pe_name}_{bank}")
                    for c in range(bank * BANK, (bank + 1) * BANK):
                        cut = slice(c * P, (c + 1) * P)
                        act_p.tick(s.activation(hid[:, i, cut], ph[i][:, cut], func, bias=bias[:, c:c + 1]),
                                   turn, f"{name}{c}")

            if kind != "first":
                act.wait_ge(s_factors, before_exp)
                s.activation(ee[:, :, :, :], ee[:, :, :, :], ACT.Exp, scale=SCALE).then_inc(s_exp, 1)
            act.wait_ge(s_weights, 16 * len(loads))
            blocks_of(act, do)


def select_and_store(nc, dram, keep, out):
    with Phase(nc) as ctx:
        def sb(name, shape, dt=F32):
            return ctx.enter_context(nc.sbuf_tensor(f"final_{name}", shape, dt))

        def sem(name):
            return ctx.semaphore(f"final_{name}")

        acc, qc, gates = keep["acc"], keep["qc"], keep["gates"]
        node_i = sb("node_i", [P, BLOCKS], I32)
        valid = sb("valid", [P, BLOCKS])
        hide = sb("hide", [P, BLOCKS])
        u = sb("u", [P, BLOCKS])
        w = sb("w", [P, BLOCKS])
        cmp_ = sb("cmp", [P, BLOCKS])
        part = sb("part", [P, 1])
        ones = sb("ones", [P, P])
        before = sb("before", [P, P])
        sign = sb("sign", [P, 1])
        rank = sb("rank", [P, 1])
        cand = sb("cand", [P, 1], I32)
        theta = sb("theta", [P, 1], I32)
        bit = sb("bit", [P, 1], I32)
        take_f = sb("take_f", [P, 1])
        take_i = sb("take_i", [P, 1], I32)
        bound = sb("bound", [P, 1])
        above = sb("above", [P, BLOCKS])
        equal = sb("equal", [P, BLOCKS])
        zero = sb("zero", [P, BLOCKS])
        run = sb("run", [P, BLOCKS])
        sel = sb("sel", [P, BLOCKS])
        rows = sb("rows", [P, 7, D])
        rows2 = sb("rows2", [P, 7, D])
        total = ctx.enter_context(nc.psum_tensor("final_total", [P, 1], F32))
        cols = ctx.enter_context(nc.psum_tensor("final_cols", [P, BLOCKS], F32))
        prior = ctx.enter_context(nc.psum_tensor("final_prior", [P, BLOCKS], F32))

        s_iota = sem("iota")
        s_tri = sem("triangle")
        s_v = sem("dve")
        s_total = sem("total")
        s_prior = sem("prior")
        s_out = [sem(f"out{i}") for i in range(2)]
        count = {"n": 0, "at": {}}
        need = []
        SPAN = 7
        assert BLOCKS % SPAN == 0

        block = ctx.enter_context(nc.Block())

        @block.gpsimd
        def _(pool):
            g = nc.gpsimd
            g.iota(node_i[:, :], pattern=[[P, BLOCKS]], base=0, channel_multiplier=1).then_inc(s_iota, 1)
            g.memset(before[:, :], 1.0).then_inc(s_tri, 1)
            pool.wait_ge(s_tri, 1)
            g.affine_select(out=before[:, :], in_=before[:, :], compare_op=ALU.is_gt, fill=0.0,
                            base=0, pattern=[[1, P]], channel_multiplier=-1).then_inc(s_tri, 1)

        @block.vector
        def _(dve):
            v = nc.vector

            def link(ins, name=None):
                ins.then_inc(s_v, 1)
                count["n"] += 1
                if name:
                    count["at"][name] = count["n"]
                dve.wait_ge(s_v, count["n"])

            def count_of(in0, scalar, op):
                link(v.tensor_scalar(cmp_[:, :], in0, scalar, 0.0, op, ALU.add, accum_out=part[:, :]))
                need.append(count["n"])
                dve.wait_ge(s_total, len(need))

            link(v.memset(ones[:, :], 1.0))
            link(v.memset(zero[:, :], 1.0))
            link(v.memset(theta[:, :], 0))
            link(v.memset(bit[:, :], 1 << 30))
            dve.wait_ge(s_iota, 1)
            link(v.tensor_scalar(valid[:, :], node_i[:, :], float(N), None, ALU.is_lt))
            link(v.tensor_scalar(hide[:, :], valid[:, :], -1.0, 3e38, ALU.add, ALU.mult))
            link(v.tensor_tensor(u[:, :], gates[:, :], valid[:, :], ALU.mult))
            link(v.tensor_tensor(w[:, :], u[:, :], hide[:, :], ALU.add))
            count_of(w[:, :], 0.0, ALU.is_ge)
            link(v.tensor_scalar(take_f[:, :], total[:, :], float(TOPK), None, ALU.is_ge))
            link(v.tensor_scalar(sign[:, :], take_f[:, :], 2.0, -1.0, ALU.mult, ALU.add))
            link(v.tensor_scalar(rank[:, :], take_f[:, :], float(2 * TOPK - N - 1), float(N - TOPK + 1),
                                 ALU.mult, ALU.add))
            link(v.tensor_scalar(u[:, :], u[:, :], sign[:, 0:1], None, ALU.mult))
            link(v.tensor_tensor(u[:, :], u[:, :], hide[:, :], ALU.add))
            for _ in range(31):
                link(v.tensor_tensor(cand[:, :], theta[:, :], bit[:, :], ALU.bitwise_or))
                count_of(u[:, :], cand[:, :].bitcast(F32), ALU.is_ge)
                link(v.tensor_tensor(take_f[:, :], total[:, :], rank[:, :], ALU.is_ge))
                link(v.tensor_copy(take_i[:, :], take_f[:, :]))
                link(v.tensor_tensor(take_i[:, :], take_i[:, :], bit[:, :], ALU.mult))
                link(v.tensor_tensor(theta[:, :], theta[:, :], take_i[:, :], ALU.bitwise_or))
                link(v.tensor_single_scalar(bit[:, :], bit[:, :], 1, op=ALU.logical_shift_right))
            link(v.tensor_tensor(bound[:, :], theta[:, :].bitcast(F32), sign[:, :], ALU.mult))
            link(v.tensor_scalar(above[:, :], w[:, :], bound[:, 0:1], None, ALU.is_gt))
            link(v.tensor_scalar(equal[:, :], w[:, :], bound[:, 0:1], None, ALU.is_equal), "equal")
            count_of(w[:, :], bound[:, 0:1], ALU.is_gt)
            link(v.tensor_scalar(rank[:, :], total[:, :], -1.0, float(TOPK), ALU.mult, ALU.add))
            dve.wait_ge(s_prior, 1)
            link(v.tensor_tensor_scan(run[:, :], zero[:, :], cols[:, :], 0.0, ALU.mult, ALU.add))
            link(v.tensor_tensor(run[:, :], run[:, :], cols[:, :], ALU.subtract))
            link(v.tensor_tensor(run[:, :], run[:, :], prior[:, :], ALU.add))
            link(v.tensor_scalar(run[:, :], run[:, :], rank[:, 0:1], None, ALU.is_lt))
            link(v.tensor_tensor(equal[:, :], equal[:, :], run[:, :], ALU.mult))
            link(v.tensor_tensor(sel[:, :], above[:, :], equal[:, :], ALU.add))
            for b in range(BLOCKS):
                n = b // SPAN
                if b % SPAN == 0 and n >= 2:
                    dve.wait_ge(s_out[n % 2], 16 * (n // 2))
                o = (rows if n % 2 == 0 else rows2)[:, b % SPAN, :]
                v.scalar_tensor_tensor(out=o.rearrange("p (c n) -> p c n", c=2), in0=acc[:, 0:2, b * P:(b + 1) * P],
                                       scalar=sel[:, b:b + 1],
                                       in1=qc[:, b * QC:b * QC + D].rearrange("p (c n) -> p c n", c=2),
                                       op0=ALU.mult, op1=ALU.add).then_inc(s_v, 1)
                count["n"] += 1
                if b % SPAN == SPAN - 1:
                    count["at"][f"rows{n}"] = count["n"]

        at = count["at"]

        @block.tensor
        def _(pe):
            t = nc.tensor
            for i, n in enumerate(need):
                if i == len(need) - 1:
                    pe.wait_ge(s_tri, 2)
                    pe.wait_ge(s_v, at["equal"])
                    t.matmul(cols[:, :], ones[:, :], equal[:, :], start=True, stop=True)
                    t.matmul(prior[:, :], before[:, :], equal[:, :], start=True, stop=True).then_inc(s_prior, 1)
                pe.wait_ge(s_v, n)
                t.matmul(total[:, :], ones[:, :], part[:, :], start=True, stop=True).then_inc(s_total, 1)

        @block.sync
        def _(sp):
            for n in range(BLOCKS // SPAN):
                sp.wait_ge(s_v, at[f"rows{n}"])
                r = rows if n % 2 == 0 else rows2
                first = n * SPAN * P
                if n < BLOCKS // SPAN - 1:
                    sp.dma_start(out[first:first + SPAN * P, :].rearrange("(b p) d -> p b d", p=P), r[:, :, :])\
                        .then_inc(s_out[n % 2], 16)
                else:
                    whole = (SPAN - 1) * P
                    sp.dma_start(out[first:first + whole, :].rearrange("(b p) d -> p b d", p=P),
                                 r[:, 0:SPAN - 1, :]).then_inc(s_out[n % 2], 16)
                    sp.dma_start(out[first + whole:N, :], r[0:LAST, SPAN - 1, :]).then_inc(s_out[n % 2], 16)
            sp.wait_ge(s_out[0], 16 * 5)
            sp.wait_ge(s_out[1], 16 * 3)


def build(nc, a, out):
    with ExitStack() as ctx:
        def sb(name, shape, dt=F32):
            return ctx.enter_context(nc.sbuf_tensor(name, shape, dt))

        def dr(name, shape, dt=F32):
            return nc.dram_tensor(name, shape, dt).ap()

        keep = {"ident": sb("ident", [P, P]), "cols": sb("cols", [P, SELW]), "part": sb("part", [P, 1]),
                "ecol": sb("ecol", [P, P]), "self": sb("self", [P, BLOCKS * H]), "gates": sb("gates", [P, BLOCKS])}
        dram = {"src": dr("src_padded", (TILES * P,), I32), "dst": dr("dst_padded", (TILES * P,), I32),
                "ends": dr("step_ends", (SC * P * 2,)), "regs": dr("step_regs", (SC * P, 2), I32),
                "rel": dr("step_rel", (SC * P, P), BF16), "flags": dr("step_flags", (2, SC * P, P)),
                "idx": dr("step_src", (P, SC * P), I32), "col": dr("step_col", (P, SC * P)),
                "last": dr("step_last", (P, SC * P)), "eregs": dr("end_regs", (P, 2), I32),
                "h": dr("h", (BLOCKS * P, D)), "kv": dr("kv", (BLOCKS * P, KV))}
        constants(nc, keep)
        plan_steps(nc, a["src"], a["dst"], dram, keep)
        keep["qc"] = sb("qc", [P, BLOCKS * QC])
        keep["acc"] = sb("acc", [P, 3, (BLOCKS + 1) * P])
        clear_sums(nc, keep)
        node_pass(nc, "first", a, dram, keep)
        for layer in range(LAYERS):
            with nc.sbuf_tensor(f"ends{layer}", [P, 3, ENDS], F32) as ends:
                keep["ends"] = ends
                edge_pass(nc, layer, dram, keep)
                merge_ends(nc, layer, dram, keep)
            node_pass(nc, "middle" if layer < LAYERS - 1 else "last", a, dram, keep)
        select_and_store(nc, dram, keep, out)


def clear_sums(nc, keep):
    with nc.Block() as block:
        @block.vector
        def _(dve):
            nc.vector.memset(keep["acc"][:, :, :], 0.0)


_OUT = ((N, D), "float32")


def kernel(**inputs):
    import numpy as _np
    import concourse.bacc as _bacc
    from concourse.bass_utils import run_bass_kernel_spmd as _run

    nc = _bacc.Bacc("TRN2", target_bir_lowering=False, num_devices=1)
    arrays, args = {}, {}
    for name, value in inputs.items():
        a = _np.ascontiguousarray(value)
        arrays[f"in_{name}"] = a
        args[name] = nc.dram_tensor(f"in_{name}", a.shape, mybir.dt.from_np(a.dtype), kind="ExternalInput").ap()
    out = nc.dram_tensor("out_0", _OUT[0], F32, kind="ExternalOutput").ap()
    build(nc, args, out)
    r = _run(nc, [arrays], core_ids=[0])
    return r.results[0]["out_0"]
```
